# Optimizing a Trainium2 kernel written in Bass

```python
import numpy as np
import jax
import jax.numpy as jnp

def _softmax(x, axis=-1):
    return jax.nn.softmax(x, axis=axis)

def _gelu(x):
    return jax.nn.gelu(x, approximate=True)

def _silu(x):
    return jax.nn.silu(x)

def _sigmoid(x):
    return jax.nn.sigmoid(x)

def _layernorm(x, axis=-1, eps=1e-05):
    m = jnp.mean(x, axis=axis, keepdims=True)
    v = jnp.var(x, axis=axis, keepdims=True)
    return (x - m) / jnp.sqrt(v + eps)

def _scatter_add(tgt, idx, src, axis=0):
    return tgt.at[idx].add(src)

def _segment_sum(src, seg, n):
    return jax.ops.segment_sum(src, seg, n)
kernel_name = 'mk_decoder_preln_d1_seqx_r4_0f9d7a'

def setup_inputs(seed: int=0):
    np.random.seed(seed)
    _w = jnp.asarray

    def _rec_inputs():
        import jax
        import jax.numpy as jnp
        _rk = jax.random.key(seed)
        x = -0.0003929 + 0.9999 * jax.random.normal(jax.random.fold_in(_rk, 1), (8, 512, 256), jnp.float32)
        _lenS = 512 - jax.random.randint(jax.random.fold_in(_rk, 7), (8,), 0, max(1, 512 // 4) + 1, jnp.int32)
        _lenS2 = 64 - jax.random.randint(jax.random.fold_in(_rk, 8), (8,), 0, max(1, 64 // 4) + 1, jnp.int32)
        _ctx_512P = jax.random.normal(jax.random.fold_in(_rk, 11), (8, 16, 128), jnp.float32)
        _ctx_512c = jax.random.dirichlet(jax.random.fold_in(_rk, 511), 0.3 * jnp.ones((16,), jnp.float32), (8, 64))
        _ctx_512t = jnp.einsum('bsk,bkd->bsd', _ctx_512c, _ctx_512P)
        _ctx_512t = _ctx_512t * jax.lax.rsqrt(jnp.mean(jnp.square(_ctx_512t)) + 1e-12) * 0.953939
        ctx_512 = -1.39393e-06 + 0.999914 * (_ctx_512t + 0.3 * jax.random.normal(jax.random.fold_in(_rk, 611), (8, 64, 128), jnp.float32))
        return (x, ctx_512)
    x, ctx_512 = _rec_inputs()

    def _L0_attn_setup():
        import jax, jax.numpy as jnp
        import numpy as np
        import math
        NEG_INF = -1e+38

        def wkv_scan(w, u, k, v):
            B, T, C = k.shape

            def step(carry, kv_t):
                a, b, pp = carry
                kt, vt = kv_t
                ww = u + kt
                q = jnp.maximum(pp, ww)
                e1 = jnp.exp(pp - q)
                e2 = jnp.exp(ww - q)
                y = (e1 * a + e2 * vt) / (e1 * b + e2)
                ww2 = pp + w
                q2 = jnp.maximum(ww2, kt)
                e1b = jnp.exp(ww2 - q2)
                e2b = jnp.exp(kt - q2)
                return ((e1b * a + e2b * vt, e1b * b + e2b, q2), y)
            init = (jnp.zeros((B, C), k.dtype), jnp.zeros((B, C), k.dtype), jnp.full((B, C), NEG_INF, k.dtype))
            kT = jnp.swapaxes(k, 0, 1)
            vT = jnp.swapaxes(v, 0, 1)
            _, ys = jax.lax.scan(step, init, (kT, vT))
            return jnp.swapaxes(ys, 0, 1)
        key = jax.random.key(seed)
        B, T, C = (16, 256, 256)
        k1, k2, k3, k4 = jax.random.split(key, 4)
        x = jax.random.normal(k1, (B, T, C), dtype=jnp.float32)
        scale = 0.02
        Wk = jax.random.normal(k2, (C, C), dtype=jnp.float32) * scale
        Wr = jax.random.normal(k3, (C, C), dtype=jnp.float32) * scale
        Wo = jax.random.normal(k4, (C, C), dtype=jnp.float32) * scale
        h = np.arange(C, dtype=np.float64)
        decay_speed = -5.0 + 8.0 * (h / (C - 1)) ** (0.7 + 1.3 * 1)
        zigzag = ((np.arange(C) + 1) % 3 - 1) * 0.5
        time_first = np.ones(C) * math.log(0.3) + zigzag
        return {'x': x, 'Wk': Wk, 'Wr': Wr, 'Wo': Wo, 'time_decay': jnp.asarray(decay_speed, dtype=jnp.float32), 'time_first': jnp.asarray(time_first, dtype=jnp.float32)}
    _L0_attn_all = _L0_attn_setup()
    _L0_attn_in = {k: v for k, v in _L0_attn_all.items() if k in ('Wk', 'Wr', 'Wo', 'time_decay', 'time_first')}
    del _L0_attn_all

    def _L0_xattn_setup():
        import jax, jax.numpy as jnp
        import numpy as np
        HEADS = 16
        D_MODEL = 256
        IMG_MODEL = 128
        D_K = D_MODEL // HEADS
        key = jax.random.key(seed)
        ks = jax.random.split(key, 12)
        B, LQ, LKV = (8, 512, 256)
        s_dm = 1.0 / np.sqrt(D_MODEL)
        s_im = 1.0 / np.sqrt(IMG_MODEL)
        return {'q': jax.random.normal(ks[0], (B, LQ, D_MODEL), jnp.float32), 'k': jax.random.normal(ks[1], (B, LKV, IMG_MODEL), jnp.float32), 'v': jax.random.normal(ks[2], (B, LKV, IMG_MODEL), jnp.float32), 'Wq': jax.random.normal(ks[3], (D_MODEL, D_MODEL), jnp.float32) * s_dm, 'bq': jnp.zeros((D_MODEL,), jnp.float32), 'Wk': jax.random.normal(ks[4], (IMG_MODEL, D_MODEL), jnp.float32) * s_im, 'bk': jnp.zeros((D_MODEL,), jnp.float32), 'Wv': jax.random.normal(ks[5], (IMG_MODEL, D_MODEL), jnp.float32) * s_im, 'bv': jnp.zeros((D_MODEL,), jnp.float32), 'Wo': jax.random.normal(ks[6], (D_MODEL, D_MODEL), jnp.float32) * s_dm, 'bo': jnp.zeros((D_MODEL,), jnp.float32)}
    _L0_xattn_all = _L0_xattn_setup()
    _L0_xattn_in = {k: v for k, v in _L0_xattn_all.items() if k in ('Wq', 'bq', 'Wk', 'bk', 'Wv', 'bv', 'Wo', 'bo')}
    del _L0_xattn_all

    def _L0_ffn_setup():
        import jax, jax.numpy as jnp
        import numpy as np
        T, Z, D_DIM = (8, 512, 256)
        N_EXP, P_SLOT, H = (64, 32, 256)
        LN_EPS = 1e-05
        key = jax.random.key(seed)
        k = jax.random.split(key, 5)
        s = 0.02
        return {'x': jax.random.normal(k[0], (T, Z, D_DIM), dtype=jnp.float32), 'phi_w': jax.random.normal(k[1], (N_EXP * P_SLOT, D_DIM), dtype=jnp.float32) * s, 'phi_b': jax.random.normal(k[2], (N_EXP * P_SLOT,), dtype=jnp.float32) * s, 'expert_w': jax.random.normal(k[3], (N_EXP, D_DIM, H), dtype=jnp.float32) * s, 'expert_b': jax.random.normal(k[4], (N_EXP, H), dtype=jnp.float32) * s}
    _L0_ffn_all = _L0_ffn_setup()
    _L0_ffn_in = {k: v for k, v in _L0_ffn_all.items() if k in ('phi_w', 'phi_b', 'expert_w', 'expert_b')}
    del _L0_ffn_all
    return {'x': x, 'ctx_512': ctx_512, 'L0_attn_Wk': _L0_attn_in['Wk'], 'L0_attn_Wr': _L0_attn_in['Wr'], 'L0_attn_Wo': _L0_attn_in['Wo'], 'L0_attn_time_decay': _L0_attn_in['time_decay'], 'L0_attn_time_first': _L0_attn_in['time_first'], 'L0_xattn_Wq': _L0_xattn_in['Wq'], 'L0_xattn_bq': _L0_xattn_in['bq'], 'L0_xattn_Wk': _L0_xattn_in['Wk'], 'L0_xattn_bk': _L0_xattn_in['bk'], 'L0_xattn_Wv': _L0_xattn_in['Wv'], 'L0_xattn_bv': _L0_xattn_in['bv'], 'L0_xattn_Wo': _L0_xattn_in['Wo'], 'L0_xattn_bo': _L0_xattn_in['bo'], 'L0_ffn_phi_w': _L0_ffn_in['phi_w'], 'L0_ffn_phi_b': _L0_ffn_in['phi_b'], 'L0_ffn_expert_w': _L0_ffn_in['expert_w'], 'L0_ffn_expert_b': _L0_ffn_in['expert_b']}

def reference(x, ctx_512, L0_attn_Wk, L0_attn_Wr, L0_attn_Wo, L0_attn_time_decay, L0_attn_time_first, L0_xattn_Wq, L0_xattn_bq, L0_xattn_Wk, L0_xattn_bk, L0_xattn_Wv, L0_xattn_bv, L0_xattn_Wo, L0_xattn_bo, L0_ffn_phi_w, L0_ffn_phi_b, L0_ffn_expert_w, L0_ffn_expert_b):
    import jax
    import jax.numpy as jnp

    def _L0_attn_ref(x, Wk, Wr, Wo, time_decay, time_first):
        import jax, jax.numpy as jnp
        import numpy as np
        import math
        NEG_INF = -1e+38

        def wkv_scan(w, u, k, v):
            B, T, C = k.shape

            def step(carry, kv_t):
                a, b, pp = carry
                kt, vt = kv_t
                ww = u + kt
                q = jnp.maximum(pp, ww)
                e1 = jnp.exp(pp - q)
                e2 = jnp.exp(ww - q)
                y = (e1 * a + e2 * vt) / (e1 * b + e2)
                ww2 = pp + w
                q2 = jnp.maximum(ww2, kt)
                e1b = jnp.exp(ww2 - q2)
                e2b = jnp.exp(kt - q2)
                return ((e1b * a + e2b * vt, e1b * b + e2b, q2), y)
            init = (jnp.zeros((B, C), k.dtype), jnp.zeros((B, C), k.dtype), jnp.full((B, C), NEG_INF, k.dtype))
            kT = jnp.swapaxes(k, 0, 1)
            vT = jnp.swapaxes(v, 0, 1)
            _, ys = jax.lax.scan(step, init, (kT, vT))
            return jnp.swapaxes(ys, 0, 1)
        k = jnp.einsum('btc,hc->bth', x, Wk)
        r = jnp.einsum('btc,hc->bth', x, Wr)
        v = r
        w = -jnp.exp(time_decay)
        y = wkv_scan(w, time_first, k, v)
        out = jax.nn.sigmoid(r) * y
        return jnp.einsum('bth,ch->btc', out, Wo)

    def _L0_xattn_ref(q, k, v, Wq, bq, Wk, bk, Wv, bv, Wo, bo):
        import jax, jax.numpy as jnp
        import numpy as np
        HEADS = 16
        D_MODEL = 256
        IMG_MODEL = 128
        D_K = D_MODEL // HEADS
        B, LQ, _ = q.shape
        LKV = k.shape[1]
        qh = (q @ Wq + bq).reshape(B, LQ, HEADS, D_K).transpose(0, 2, 1, 3)
        kh = (k @ Wk + bk).reshape(B, LKV, HEADS, D_K).transpose(0, 2, 1, 3)
        vh = (v @ Wv + bv).reshape(B, LKV, HEADS, D_K).transpose(0, 2, 1, 3)
        scale = 1.0 / np.sqrt(D_K)
        scores = jnp.einsum('bhqd,bhkd->bhqk', qh, kh) * scale
        attn = jax.nn.softmax(scores, axis=-1)
        out = jnp.einsum('bhqk,bhkd->bhqd', attn, vh)
        concat = out.transpose(0, 2, 1, 3).reshape(B, LQ, D_MODEL)
        return concat @ Wo + bo

    def _L0_ffn_ref(x, phi_w, phi_b, expert_w, expert_b):
        import jax, jax.numpy as jnp
        import numpy as np
        T, Z, D_DIM = (8, 512, 256)
        N_EXP, P_SLOT, H = (64, 32, 256)
        LN_EPS = 1e-05
        t, z, d = x.shape
        n = expert_w.shape[0]
        p = phi_w.shape[0] // n
        logits = (jnp.einsum('tzd,ed->tze', x, phi_w) + phi_b).reshape(t, z, n, p)
        D = jax.nn.softmax(logits, axis=3)
        C = jax.nn.softmax(logits, axis=2)
        X_tilde = jnp.einsum('tznp,tzd->npd', D, x)
        X_tilde = jnp.clip(X_tilde, -33000.0, 65000.0)
        mu = jnp.mean(X_tilde, axis=-1, keepdims=True)
        var = jnp.mean(jnp.square(X_tilde - mu), axis=-1, keepdims=True)
        X_tilde = (X_tilde - mu) * jax.lax.rsqrt(var + LN_EPS)
        X_tilde = jnp.tanh(X_tilde)
        Y_tilde = jnp.einsum('npd,ndH->npH', X_tilde, expert_w) + expert_b[:, None, :]
        Y = jnp.einsum('tznp,npH->tzH', C, Y_tilde)
        return Y
    x = x + _L0_attn_ref(_layernorm(x, axis=-1), L0_attn_Wk, L0_attn_Wr, L0_attn_Wo, L0_attn_time_decay, L0_attn_time_first)
    x = x + _L0_xattn_ref(_layernorm(x, axis=-1), ctx_512, ctx_512, L0_xattn_Wq, L0_xattn_bq, L0_xattn_Wk, L0_xattn_bk, L0_xattn_Wv, L0_xattn_bv, L0_xattn_Wo, L0_xattn_bo)
    x = x + _L0_ffn_ref(_layernorm(x, axis=-1), L0_ffn_phi_w, L0_ffn_phi_b, L0_ffn_expert_w, L0_ffn_expert_b)
    return x

_drawn_inputs = setup_inputs


def setup_inputs(seed=0):
    import zlib

    import numpy as np

    out = dict(_drawn_inputs(seed))
    spreads = {'L0_xattn_bq': (0.0, 0.1),
     'L0_xattn_bk': (0.0, 2.0),
     'L0_xattn_bv': (0.0, 0.1),
     'L0_xattn_bo': (0.0, 0.1)}
    factors = {'L0_attn_Wk': 8.0,
     'L0_attn_Wr': 3.139,
     'L0_attn_Wo': 3.102,
     'L0_attn_time_decay': 3.641,
     'L0_attn_time_first': 8.0,
     'L0_ffn_phi_b': 26.864}
    for name, (base, spread) in spreads.items():
        noise = np.random.default_rng([zlib.crc32(name.encode()), seed]).standard_normal(out[name].shape)
        drawn = base * np.exp(spread * noise) if base else spread * noise
        out[name] = jnp.asarray(drawn.astype(out[name].dtype))
    for name, factor in factors.items():
        out[name] = (out[name] * factor).astype(out[name].dtype)
    return out
```

```python
from contextlib import ExitStack

import concourse.bass as bass
from concourse import mybir

F32 = mybir.dt.float32
BF16 = mybir.dt.bfloat16
ALU = mybir.AluOpType
ACT = mybir.ActivationFunctionType
AX = mybir.AxisListType

P = 128
B, T, C = 8, 512, 256
CC = C // P
BT = T // P
NT = B * BT
KV, CD = 64, 128
HEADS = 16
DK = C // HEADS
EPS = 1e-5
NEG_INF = -1e38
LIMIT = 40.0

GH = 6
GROUPS = [6, 6, 4]
GR = GH * DK
GK = GR + HEADS
GN = GH * KV
PAIRS = HEADS // 2
VW = 2 * (DK + 1)

EXPERTS, SLOTS = 64, 32
ES = EXPERTS * SLOTS
ST = ES // P
EPT = P // SLOTS
BLK = 512
EB = ES // BLK


def after(eng, sem, count):
    if isinstance(count, int) and count <= 0:
        return
    eng.wait_ge(sem, count)


def setup(nc, d, s):
    with ExitStack() as ctx:
        def sem(name):
            return ctx.enter_context(nc.semaphore(name))

        raw = ctx.enter_context(nc.sbuf_tensor("raw_weights", [P, 3, CC, C], F32))
        decay = ctx.enter_context(nc.sbuf_tensor("decay", [P, CC], F32))
        decay_e = ctx.enter_context(nc.sbuf_tensor("decay_e", [P, CC], F32))
        weights_in = sem("weights_in")
        vectors_in = sem("vectors_in")
        ident_zero = sem("ident_zero")
        ident_done = sem("ident_done")
        turned = sem("weights_turned")
        copied = sem("weights_copied")
        decay_exp = sem("decay_exp")
        consts = sem("consts")
        bank_sem = [sem(f"bank_turned{i}") for i in range(2)]
        block = ctx.enter_context(nc.Block())

        @block.sync
        def _(sp):
            for n, w in enumerate((d["attn_Wk"], d["attn_Wr"], d["attn_Wo"])):
                sp.dma_start(raw[:, n], w.rearrange("(a p) c -> p a c", p=P)).then_inc(weights_in, 16)
            sp.wait_ge(weights_in, 48)
            sp.wait_ge(vectors_in, 16 * 2)

        @block.gpsimd
        def _(pool):
            pool.memset(s["ident"][:], 0.0).then_inc(ident_zero, 1)
            pool.wait_ge(ident_zero, 1)
            pool.affine_select(out=s["ident"][:], in_=s["ident"][:], compare_op=ALU.not_equal, fill=1.0,
                               base=0, pattern=[[-1, P]], channel_multiplier=1).then_inc(ident_done, 1)

        @block.scalar
        def _(act):
            with nc.allow_non_contiguous_dma(reason="one value per channel, once"):
                act.dma_start(decay[:], d["attn_decay"].rearrange("(a p) -> p a", p=P)).then_inc(vectors_in, 16)
                act.dma_start(s["u"][:], d["attn_first"].rearrange("(a p) -> p a", p=P)).then_inc(vectors_in, 16)
            act.wait_ge(vectors_in, 32)
            act.activation(decay_e[:], decay[:], ACT.Exp).then_inc(decay_exp, 1)

        @block.tensor
        def _(pe):
            pe.wait_ge(ident_done, 1)
            pe.wait_ge(weights_in, 48)
            for n in range(3):
                for cc in range(CC):
                    if n * CC + cc >= 2:
                        pe.wait_ge(copied, n * CC + cc - 1)
                    for hc in range(CC):
                        m = pe.transpose(s["ps"][:, (n * CC + cc) % 2, hc * P:(hc + 1) * P],
                                         raw[:, n, hc, cc * P:(cc + 1) * P], s["ident"][:])
                    m.then_inc(turned, 1)

        @block.vector
        def _(dve):
            dve.memset(s["eps"][:], EPS).then_inc(consts, 1)
            for n in range(3 * CC):
                dve.wait_ge(turned, n + 1)
                dve.tensor_copy(s["attn_wT"][:, n // CC, n % CC, :], s["ps"][:, n % 2, 0:C]).then_inc(copied, 1)
            dve.wait_ge(decay_exp, 1)
            dve.tensor_scalar(s["w"][:], decay_e[:], -1.0, None, ALU.mult).then_inc(consts, 1)
            dve.tensor_scalar(s["cap"][:], s["u"][:], -1.0, LIMIT, ALU.mult, ALU.add).then_inc(consts, 1)
            dve.wait_ge(consts, 3)


def mixing(nc, d, s):
    ps, x_res, ident = s["ps"], s["x_res"], s["ident"]
    wkT, wrT, woT = (s["attn_wT"][:, n] for n in range(3))
    with ExitStack() as ctx:
        def sb(name, shape):
            return ctx.enter_context(nc.sbuf_tensor(name, shape, F32))

        def sem(name):
            return ctx.enter_context(nc.semaphore(name))

        stats = sb("m_stats", [P, 2, BT, 6])
        mv = sb("m_mv", [P, 2, BT, 2])
        lnv = sb("m_lnv", [P, 2, BT])
        rstd = sb("m_rstd", [P, 2, BT])
        xn = sb("m_xn", [P, 2, BT, C])
        xnT = sb("m_xnT", [P, CC, T])
        kr = sb("m_kr", [P, 2, 2, CC, T])
        top = sb("m_top", [P, CC, T + 1])
        num = sb("m_num", [P, CC, T + 1])
        den = sb("m_den", [P, CC, T + 1])
        gap = sb("m_gap", [P, CC, T])
        up = sb("m_up", [P, CC, T])
        down = sb("m_down", [P, CC, T])
        ev = sb("m_ev", [P, CC, T])
        now = sb("m_now", [P, CC, T])
        er = sb("m_er", [P, CC, T])
        bot = sb("m_bot", [P, CC, T])
        val = sb("m_val", [P, CC, T])
        lsig = sb("m_lsig", [P, CC, T])
        oT = sb("m_oT", [P, 2, CC, T])

        x_in = [sem(f"m_x_in{i}") for i in range(2)]
        stats_ready = sem("m_stats_ready")
        mv_ready = sem("m_mv_ready")
        waited = sem("m_waited")
        lnv_ready = sem("m_lnv_ready")
        rstd_ready = sem("m_rstd_ready")
        xn_ready = sem("m_xn_ready")
        xn_turned = sem("m_xn_turned")
        xnT_ready = sem("m_xnT_ready")
        kr_done = sem("m_kr_done")
        kr_ready = sem("m_kr_ready")
        first = sem("m_first_columns")
        top_ready = sem("m_top_ready")
        gap_ready = sem("m_gap_ready")
        up_ready = sem("m_up_ready")
        down_ready = sem("m_down_ready")
        now_capped = sem("m_now_capped")
        now_ready = sem("m_now_ready")
        up_exp = sem("m_up_exp")
        down_exp = sem("m_down_exp")
        er_ready = sem("m_er_ready")
        er_capped = sem("m_er_capped")
        ev_ready = sem("m_ev_ready")
        num_ready = sem("m_num_ready")
        den_ready = sem("m_den_ready")
        bot_ready = sem("m_bot_ready")
        val_ready = sem("m_val_ready")
        vsum_ready = sem("m_vsum_ready")
        lbot_ready = sem("m_lbot_ready")
        lsig_ready = sem("m_lsig_ready")
        lsum_ready = sem("m_lsum_ready")
        rec_ready = sem("m_rec_ready")
        oT_ready = sem("m_oT_ready")
        out_done = sem("m_out_done")
        res_done = sem("m_res_done")
        block = ctx.enter_context(nc.Block())

        def loaded(b, par):
            return 8 * b + 16 - 8 * par

        def pipeline(eng, front, back):
            front(0, 0)
            front(1, 1)
            back(0, 0)
            front(2, 0)
            back(1, 1)
            with eng.Fori(2, B - 3, 2) as i:
                front(i + 1, 1)
                back(i, 0)
                front(i + 2, 0)
                back(i + 1, 1)
            front(B - 1, 1)
            back(B - 2, 0)
            back(B - 1, 1)

        @block.sync
        def _(sp):
            def load(b, par):
                after(sp, stats_ready, b - 1)
                sp.dma_start(x_res[:, bass.ds(b * BT, BT), :],
                             s["x_dram"][:, bass.ds(b * BT, BT), :]).then_inc(x_in[par], 16)
            load(0, 0)
            load(1, 1)
            with sp.Fori(2, B - 1, 2) as i:
                load(i, 0)
                load(i + 1, 1)

        @block.vector
        def _(dve):
            for buf, v in ((top, NEG_INF), (num, 0.0), (den, 0.0)):
                ins = dve.memset(buf[:, :, 0:1], v)
            ins.then_inc(first, 1)

            def front(b, par):
                dve.wait_ge(x_in[par], loaded(b, par))
                after(dve, xn_ready, b)
                for i in range(BT):
                    ins = dve.bn_stats(stats[:, par, i], x_res[:, b * BT + i, :])
                ins.then_inc(stats_ready, 1)
                dve.wait_ge(stats_ready, b + 1)
                after(dve, rstd_ready, b - 1)
                dve.sem_inc(waited, 1)
                for i in range(BT):
                    ins = dve.bn_aggr(mv[:, par, i], stats[:, par, i])
                ins.then_inc(mv_ready, 1)
                dve.wait_ge(rstd_ready, b + 1)
                after(dve, xn_turned, b - 1)
                for i in range(BT):
                    ins = dve.tensor_scalar(xn[:, par, i], x_res[:, b * BT + i, :], mv[:, par, i, 0:1],
                                            rstd[:, par, i:i + 1], ALU.subtract, ALU.mult)
                ins.then_inc(xn_ready, 1)

            def back(b, par):
                n = 2 * b
                dve.wait_ge(kr_ready, b + 1)
                for h in range(CC):
                    after(dve, lsig_ready, n + h - 1)
                    dve.tensor_scalar(er[:, h], kr[:, par, 1, h], -LIMIT, None, ALU.max).then_inc(er_capped, 1)
                for h in range(CC):
                    after(dve, gap_ready, n - 1 + h)
                    dve.tensor_tensor_scan(top[:, h, 1:T + 1], s["w"][:, h:h + 1].to_broadcast([P, T]),
                                           kr[:, par, 0, h], NEG_INF, ALU.add, ALU.max).then_inc(top_ready, 1)
                for h in range(CC):
                    dve.wait_ge(gap_ready, n + h + 1)
                    after(dve, up_exp, n - 1 + h)
                    dve.tensor_scalar(up[:, h], gap[:, h], s["w"][:, h:h + 1], 0.0,
                                      ALU.subtract, ALU.max).then_inc(up_ready, 1)
                    after(dve, val_ready, n - 1 + h)
                    dve.tensor_scalar(now[:, h], gap[:, h], s["cap"][:, h:h + 1], None,
                                      ALU.min).then_inc(now_capped, 1)
                    dve.tensor_scalar(down[:, h], gap[:, h], s["w"][:, h:h + 1], 0.0,
                                      ALU.subtract, ALU.min).then_inc(down_ready, 1)
                for h in range(CC):
                    dve.wait_ge(up_exp, n + h + 1)
                    dve.wait_ge(first, 1)
                    after(dve, bot_ready, n + h - 1)
                    dve.tensor_tensor_scan(den[:, h, 1:T + 1], up[:, h], down[:, h], 0.0,
                                           ALU.mult, ALU.add).then_inc(den_ready, 1)
                    dve.wait_ge(ev_ready, n + h + 1)
                    after(dve, vsum_ready, n + h - 1)
                    dve.tensor_tensor_scan(num[:, h, 1:T + 1], up[:, h], ev[:, h], 0.0,
                                           ALU.mult, ALU.add).then_inc(num_ready, 1)
                    dve.wait_ge(den_ready, n + h + 1)
                    after(dve, rec_ready, n + h - 1)
                    dve.wait_ge(now_ready, n + h + 1)
                    dve.tensor_tensor(bot[:, h], now[:, h], den[:, h, 0:T], ALU.add).then_inc(bot_ready, 1)
                    after(dve, oT_ready, n + h - 1)
                    dve.tensor_tensor(val[:, h], now[:, h], kr[:, par, 1, h], ALU.mult).then_inc(val_ready, 1)
                    dve.wait_ge(val_ready, n + h + 1)
                    dve.wait_ge(num_ready, n + h + 1)
                    dve.tensor_tensor(val[:, h], val[:, h], num[:, h, 0:T], ALU.add).then_inc(vsum_ready, 1)
                for j in range(2):
                    dve.wait_ge(out_done, 2 * b + j + 1)
                    rows = x_res[:, bass.ds(b * BT + 2 * j, 2), :]
                    dve.tensor_tensor(rows, ps[:, 6 + j, :].rearrange("p (a c) -> p a c", a=2), rows,
                                      ALU.add).then_inc(res_done, 1)
            pipeline(dve, front, back)

        @block.gpsimd
        def _(pool):
            def back(b, par):
                n = 2 * b
                for h in range(CC):
                    pool.wait_ge(top_ready, n + h + 1)
                    after(pool, down_ready, n + h - 1)
                    after(pool, now_capped, n + h - 1)
                    pool.tensor_tensor(gap[:, h], kr[:, par, 0, h], top[:, h, 0:T],
                                       ALU.subtract).then_inc(gap_ready, 1)
                for h in range(CC):
                    pool.wait_ge(down_exp, n + h + 1)
                    after(pool, num_ready, n + h - 1)
                    pool.tensor_tensor(ev[:, h], down[:, h], kr[:, par, 1, h], ALU.mult).then_inc(ev_ready, 1)
                for h in range(CC):
                    pool.wait_ge(lbot_ready, n + h + 1)
                    pool.wait_ge(lsig_ready, n + h + 1)
                    pool.tensor_tensor(bot[:, h], bot[:, h], lsig[:, h], ALU.add).then_inc(lsum_ready, 1)
                for h in range(CC):
                    pool.wait_ge(rec_ready, n + h + 1)
                    pool.wait_ge(vsum_ready, n + h + 1)
                    after(pool, out_done, 2 * b - 2)
                    pool.tensor_tensor(oT[:, par, h], val[:, h], bot[:, h], ALU.mult).then_inc(oT_ready, 1)
            back(0, 0)
            back(1, 1)
            with pool.Fori(2, B - 1, 2) as i:
                back(i, 0)
                back(i + 1, 1)

        @block.scalar
        def _(act):
            def front(b, par):
                act.wait_ge(mv_ready, b + 1)
                after(act, xn_ready, b - 1)
                act.activation(lnv[:, par], mv[:, par, :, 1], ACT.Ln, bias=s["eps"][:, 0:1]).then_inc(lnv_ready, 1)
                act.wait_ge(lnv_ready, b + 1)
                act.activation(rstd[:, par], lnv[:, par], ACT.Exp, scale=-0.5).then_inc(rstd_ready, 1)
                act.wait_ge(xn_turned, b + 1)
                after(act, kr_done, b)
                act.copy(xnT[:], ps[:, 0:CC, :]).then_inc(xnT_ready, 1)
                act.wait_ge(kr_done, b + 1)
                after(act, oT_ready, 2 * b - 2)
                act.copy(kr[:, par].rearrange("p a h t -> p (a h) t"), ps[:, 2:6, :]).then_inc(kr_ready, 1)

            def back(b, par):
                n = 2 * b
                for h in range(CC):
                    act.wait_ge(er_capped, n + h + 1)
                    act.activation(er[:, h], er[:, h], ACT.Exp, scale=-1.0).then_inc(er_ready, 1)
                for h in range(CC):
                    act.wait_ge(now_capped, n + h + 1)
                    act.activation(now[:, h], now[:, h], ACT.Exp, bias=s["u"][:, h:h + 1]).then_inc(now_ready, 1)
                for h in range(CC):
                    act.wait_ge(down_ready, n + h + 1)
                    act.activation(down[:, h], down[:, h], ACT.Exp).then_inc(down_exp, 1)
                    act.activation(up[:, h], up[:, h], ACT.Exp, scale=-1.0).then_inc(up_exp, 1)
                for h in range(CC):
                    act.wait_ge(er_ready, n + h + 1)
                    after(act, lsum_ready, n + h - 1)
                    act.activation(lsig[:, h], er[:, h], ACT.Ln, bias=1.0).then_inc(lsig_ready, 1)
                for h in range(CC):
                    act.wait_ge(bot_ready, n + h + 1)
                    act.activation(bot[:, h], bot[:, h], ACT.Ln).then_inc(lbot_ready, 1)
                for h in range(CC):
                    act.wait_ge(lsum_ready, n + h + 1)
                    act.activation(bot[:, h], bot[:, h], ACT.Exp, scale=-1.0).then_inc(rec_ready, 1)
            act.preload_act_table_set("natural_log_exp_and_others")
            pipeline(act, front, back)

        @block.tensor
        def _(pe):
            def front(b, par):
                pe.wait_ge(xn_ready, b + 1)
                after(pe, xnT_ready, b)
                for cc in range(CC):
                    for i in range(BT):
                        m = pe.transpose(ps[:, cc, i * P:(i + 1) * P], xn[:, par, i, cc * P:(cc + 1) * P],
                                         ident[:])
                m.then_inc(xn_turned, 1)
                pe.wait_ge(xnT_ready, b + 1)
                after(pe, kr_ready, b)
                for a, w in ((0, wkT), (1, wrT)):
                    for h in range(CC):
                        for cc in range(CC):
                            m = pe.matmul(ps[:, 2 + 2 * a + h, :], w[:, cc, h * P:(h + 1) * P], xnT[:, cc],
                                          start=(cc == 0), stop=(cc == CC - 1))
                m.then_inc(kr_done, 1)

            def back(b, par):
                pe.wait_ge(oT_ready, 2 * b + 2)
                for i in range(BT):
                    if i % 2 == 0:
                        after(pe, res_done, 2 * b - 1 + i // 2)
                    for h in range(CC):
                        m = pe.matmul(ps[:, 6 + i // 2, (i % 2) * C:(i % 2 + 1) * C],
                                      oT[:, par, h, i * P:(i + 1) * P], woT[:, h, :],
                                      start=(h == 0), stop=(h == CC - 1))
                    if i % 2:
                        m.then_inc(out_done, 1)
            pipeline(pe, front, back)


def attend_setup(nc, d, s):
    ps, ident = s["ps"], s["ident"]
    with ExitStack() as ctx:
        def sem(name):
            return ctx.enter_context(nc.semaphore(name))

        ctx_in = ctx.enter_context(nc.sbuf_tensor("ctx_in", [P, B * KV // P, CD], F32))
        ctxT = ctx.enter_context(nc.sbuf_tensor("ctxT", [P, B, 2, KV], F32))
        wk = ctx.enter_context(nc.sbuf_tensor("x_wk", [P, C], F32))
        wv = ctx.enter_context(nc.sbuf_tensor("x_wv", [P, C], F32))
        bk = ctx.enter_context(nc.sbuf_tensor("x_bk", [GR, 3], F32))
        bv = ctx.enter_context(nc.sbuf_tensor("x_bv", [P, C], F32))
        loads = sem("x_loads")
        zeroed = sem("x_zeroed")
        shaped = sem("x_shaped")
        ctx_turned = sem("x_ctx_turned")
        ctxT_ready = sem("x_ctxT_ready")
        k_done = sem("x_k_done")
        v_done = sem("x_v_done")
        kT_ready = sem("x_kT_ready")
        v_ready = sem("x_v_ready")
        n_loads = 11
        block = ctx.enter_context(nc.Block())

        @block.sync
        def _(sp):
            sp.dma_start(ctx_in[:], d["ctx"].rearrange("(a e) k c -> (e k) a c", e=2)).then_inc(loads, 16)
            sp.dma_start(wk[:], d["Wk"]).then_inc(loads, 16)
            sp.dma_start(wv[:], d["Wv"]).then_inc(loads, 16)
            sp.dma_start(s["wq"][:], d["Wq"].rearrange("(a p) n -> p a n", p=P)).then_inc(loads, 16)
            sp.dma_start(s["wo"][:], d["Wo"].rearrange("(a p) n -> p a n", p=P)).then_inc(loads, 16)
            for row, dst in (("bv", bv), ("bo", s["bo"])):
                sp.dma_start(dst[:], d[row].partition_broadcast(P)).then_inc(loads, 16)
            with nc.allow_non_contiguous_dma(reason="one value per channel, once"):
                for row, dst in (("bq", s["bq"]), ("bk", bk)):
                    sp.dma_start(dst[:, 0:2], d[row][0:2 * GR].rearrange("(g p) -> p g", p=GR)).then_inc(loads, 16)
                    sp.dma_start(dst[0:C - 2 * GR, 2:3],
                                 d[row][2 * GR:C].rearrange("(g p) -> p g", g=1)).then_inc(loads, 16)

            sp.wait_ge(loads, 16 * n_loads)

        @block.gpsimd
        def _(pool):
            pool.memset(s["headmask"][:], 1.0)
            pool.memset(s["kblk"][:], 0.0)
            pool.memset(s["nm"][:], 0.0).then_inc(zeroed, 1)
            pool.wait_ge(zeroed, 1)
            pool.affine_select(out=s["headmask"][:], in_=s["headmask"][:], compare_op=ALU.is_ge, fill=0.0,
                               base=0, pattern=[[-DK, GH]], channel_multiplier=1).then_inc(shaped, 1)
            pool.wait_ge(shaped, 1)
            pool.affine_select(out=s["headmask"][:], in_=s["headmask"][:], compare_op=ALU.is_ge, fill=0.0,
                               base=DK - 1, pattern=[[DK, GH]], channel_multiplier=-1).then_inc(shaped, 1)
            for par in range(2):
                pool.affine_select(out=s["kblk"][:, par], in_=s["kblk"][:, par], compare_op=ALU.not_equal,
                                   fill=1.0, base=GR, pattern=[[GH, 3], [1, GH], [0, KV]],
                                   channel_multiplier=-1).then_inc(shaped, 1)
            pool.wait_ge(shaped, 4)

        @block.tensor
        def _(pe):
            pe.wait_ge(loads, 16 * n_loads)
            for a in range(B * KV // P):
                m = pe.transpose(ps[:, 0, a * P:(a + 1) * P], ctx_in[:, a, :], ident[:])
            m.then_inc(ctx_turned, 1)
            pe.wait_ge(ctxT_ready, 2)
            for g in range(3):
                rows = GROUPS[g] * DK
                m = pe.matmul(ps[0:rows, 1 + g, :], wk[:, g * GR:g * GR + rows], ctxT[:, :, 0, :],
                              start=True, stop=True)
            m.then_inc(k_done, 1)
            for b in range(B):
                m = pe.matmul(ps[:, 4 + b // 2, (b % 2) * C:(b % 2 + 1) * C],
                              ctxT[:, b].rearrange("p a k -> p (a k)"), wv[:], start=True, stop=True)
            m.then_inc(v_done, 1)

        @block.vector
        def _(dve):
            dve.memset(s["vblk"][:], 0.0)
            dve.memset(s["kT"][:], 0.0)
            dve.memset(s["qT"][:], 0.0).then_inc(v_ready, 1)
            dve.wait_ge(v_ready, 1)
            dve.memset(s["vblk"][0:KV, :, :, DK:DK + 1], 1.0)
            dve.memset(s["vblk"][KV:P, :, :, VW - 1:VW], 1.0)
            dve.wait_ge(ctx_turned, 1)
            for a in range(2):
                dve.tensor_copy(ctxT[:, :, a, :], ps[:, 0, :].rearrange("p (b k) -> p b k", b=B)).then_inc(ctxT_ready, 1)
            dve.wait_ge(loads, 16 * n_loads)
            dve.wait_ge(k_done, 1)
            for g in range(3):
                rows = GROUPS[g] * DK
                dve.tensor_scalar(s["kT"][0:rows, g], ps[0:rows, 1 + g, :], bk[0:rows, g:g + 1], DK ** -0.5,
                                  ALU.add, ALU.mult).then_inc(kT_ready, 1)
            dve.wait_ge(v_done, 1)
            for b in range(B):
                for e in range(2):
                    rows = slice(e * KV, (e + 1) * KV)
                    made = ps[rows, 4 + b // 2, (b % 2) * C:(b % 2 + 1) * C]
                    dve.tensor_tensor(s["vblk"][rows, b, :, e * (DK + 1):e * (DK + 1) + DK],
                                      made.rearrange("p (j e d) -> p j e d", e=2, d=DK)[:, :, e, :],
                                      bv[rows].rearrange("p (j e d) -> p j e d", e=2, d=DK)[:, :, e, :],
                                      ALU.add).then_inc(v_ready, 1)
            dve.wait_ge(v_ready, 1 + 2 * B)
            dve.wait_ge(kT_ready, 3)


BACK = ["S0", "S1", "S2", "S3", "S4", "S5", "S6", "S7", "O0", "O1", "A0", "O2", "A1", "R0",
        "O3", "A2", "R1", "A3", "R2", "R3"]
FRONT_AT = {1: "turn", 3: "query", 5: "max0", 7: "max1", 9: "max2", 11: "max3", 14: "turn_max"}


def attend(nc, d, s):
    ps, x_res, ident = s["ps"], s["x_res"], s["ident"]
    qT, kblk, vblk, nm = s["qT"], s["kblk"], s["vblk"], s["nm"]
    RING = 5
    with ExitStack() as ctx:
        def sb(name, shape):
            return ctx.enter_context(nc.sbuf_tensor(name, shape, F32))

        def sem(name):
            return ctx.enter_context(nc.semaphore(name))

        stats = sb("a_stats", [P, BT, 6])
        mv = sb("a_mv", [P, BT, 2])
        lnv = sb("a_lnv", [P, BT])
        rstd = sb("a_rstd", [P, BT])
        xn = sb("a_xn", [P, BT, C])
        xnT = sb("a_xnT", [P, CC, T])
        ex = sb("a_ex", [P, 2, PAIRS, T])
        rsum = sb("a_rsum", [P, 2, HEADS])
        at = sb("a_at", [P, 2, C])
        aT = sb("a_aT", [P, 2, CC, P])

        stats_ready = sem("a_stats_ready")
        mv_ready = sem("a_mv_ready")
        waited = sem("a_waited")
        lnv_ready = sem("a_lnv_ready")
        rstd_ready = sem("a_rstd_ready")
        xn_ready = sem("a_xn_ready")
        xn_turned = sem("a_xn_turned")
        xnT_ready = sem("a_xnT_ready")
        bias_added = sem("a_bias_added")
        q_done = sem("a_q_done")
        q_ready = sem("a_q_ready")
        kblk_ready = sem("a_kblk_ready")
        s1_done = sem("a_s1_done")
        max_ready = sem("a_max_ready")
        max_turned = sem("a_max_turned")
        maxT_ready = sem("a_maxT_ready")
        s2_done = sem("a_s2_done")
        exp_ready = sem("a_exp_ready")
        o_done = sem("a_o_done")
        rsum_ready = sem("a_rsum_ready")
        at_ready = sem("a_at_ready")
        at_turned = sem("a_at_turned")
        aT_ready = sem("a_aT_ready")
        proj_done = sem("a_proj_done")
        res_done = sem("a_res_done")
        block = ctx.enter_context(nc.Block())

        def pipeline(eng, step):
            step(-1, 1, True, False)
            step(0, 0, True, True)
            step(1, 1, True, True)
            with eng.Fori(2, B - 3, 2) as i:
                step(i, 0, True, True)
                step(i + 1, 1, True, True)
            step(B - 2, 0, True, True)
            step(B - 1, 1, False, True)

        @block.vector
        def _(dve):
            def norm(b):
                after(dve, xn_ready, b)
                for i in range(BT):
                    ins = dve.bn_stats(stats[:, i], x_res[:, b * BT + i, :])
                ins.then_inc(stats_ready, 1)
                dve.wait_ge(stats_ready, b + 1)
                dve.sem_inc(waited, 1)
                for i in range(BT):
                    ins = dve.bn_aggr(mv[:, i], stats[:, i])
                ins.then_inc(mv_ready, 1)

            def normed(b):
                dve.wait_ge(rstd_ready, b + 1)
                after(dve, xn_turned, b)
                for i in range(BT):
                    ins = dve.tensor_scalar(xn[:, i], x_res[:, b * BT + i, :], mv[:, i, 0:1],
                                            rstd[:, i:i + 1], ALU.subtract, ALU.mult)
                ins.then_inc(xn_ready, 1)

            def maxima(b, i):
                dve.wait_ge(s1_done, BT * b + i + 1)
                if i == 0:
                    after(dve, max_turned, b)
                dve.tensor_reduce(nm[:, i, GR:GR + 2 * GH],
                                  ps[:, 2:4, 0:GN].rearrange("p a (h k) -> p a h k", k=KV), AX.X, ALU.max,
                                  negate=True)
                dve.tensor_reduce(nm[:, i, GR + 2 * GH:GK],
                                  ps[:, 4, 0:GROUPS[2] * KV].rearrange("p (h k) -> p h k", k=KV), AX.X, ALU.max,
                                  negate=True).then_inc(max_ready, 1)

            def weigh(b, i, k):
                n = BT * b + i
                O = ps[:, RING + k % 3, 0:PAIRS * VW].rearrange("p (h w) -> p h w", w=DK + 1)
                dve.wait_ge(o_done, n + 1)
                dve.reciprocal(rsum[:, i % 2, :], O[:, :, DK]).then_inc(rsum_ready, 1)
                dve.wait_ge(rsum_ready, n + 1)
                after(dve, at_turned, n - 1)
                dve.tensor_tensor(at[:, i % 2].rearrange("p (h w) -> p h w", w=DK), O[:, :, 0:DK],
                                  rsum[:, i % 2, :].unsqueeze(2).to_broadcast([P, HEADS, DK]),
                                  ALU.mult).then_inc(at_ready, 1)

            def add(b, i, k):
                dve.wait_ge(proj_done, BT * b + i + 1)
                if i == 0:
                    dve.wait_ge(bias_added, b + 1)
                row = x_res[:, b * BT + i, :]
                dve.tensor_tensor(row, ps[:, RING + k % 3, 0:C], row, ALU.add).then_inc(res_done, 1)

            def step(b, par, front, back):
                for k, name in enumerate(BACK):
                    if back and name[0] == "O":
                        weigh(b, int(name[1]), k)
                    if back and name[0] == "R":
                        add(b, int(name[1]), k)
                    if front and k == 0:
                        norm(b + 1)
                        normed(b + 1)
                    if front and FRONT_AT.get(k, "").startswith("max"):
                        maxima(b + 1, int(FRONT_AT[k][3]))
            pipeline(dve, step)

        @block.gpsimd
        def _(pool):
            def front(b, par):
                after(pool, s2_done, PAIRS * (b - 1))
                for g in range(3):
                    ins = pool.tensor_tensor(
                        kblk[0:GR, par, g].rearrange("p (h k) -> p h k", k=KV),
                        s["kT"][:, g, bass.ds(b * KV, KV)].unsqueeze(1).to_broadcast([GR, GH, KV]),
                        s["headmask"][:].unsqueeze(2).to_broadcast([GR, GH, KV]), ALU.mult)
                ins.then_inc(kblk_ready, 1)
                pool.wait_ge(xn_ready, b + 1)
                for i in range(BT):
                    row = x_res[:, b * BT + i, :]
                    ins = pool.tensor_tensor(row, row, s["bo"][:], ALU.add)
                ins.then_inc(bias_added, 1)

            front(0, 0)
            front(1, 1)
            with pool.Fori(2, B - 1, 2) as i:
                front(i, 0)
                front(i + 1, 1)

        @block.scalar
        def _(act):
            def root(b):
                act.wait_ge(mv_ready, b + 1)
                act.activation(lnv[:], mv[:, :, 1], ACT.Ln, bias=s["eps"][:, 0:1]).then_inc(lnv_ready, 1)
                act.wait_ge(lnv_ready, b + 1)
                act.activation(rstd[:], lnv[:], ACT.Exp, scale=-0.5).then_inc(rstd_ready, 1)

            def turned(b):
                act.wait_ge(xn_turned, b + 1)
                after(act, q_done, b)
                act.copy(xnT[:], ps[:, 0:CC, :]).then_inc(xnT_ready, 1)

            def query(b, par):
                act.wait_ge(q_done, b + 1)
                after(act, s2_done, PAIRS * (b - 1))
                for g in range(3):
                    rows = GROUPS[g] * DK
                    ins = act.activation(qT[0:rows, par, g], ps[0:rows, 2 + g, :], ACT.Identity,
                                         bias=s["bq"][0:rows, g:g + 1])
                ins.then_inc(q_ready, 1)

            def max_rows(b, par):
                act.wait_ge(max_turned, b + 1)
                act.copy(qT[GR:GK, par], ps[GR:GK, 0:1, :].to_broadcast([HEADS, 3, T])).then_inc(maxT_ready, 1)

            def exps(b, par, j, k):
                act.wait_ge(s2_done, PAIRS * b + j + 1)
                if j == 0:
                    after(act, o_done, BT * (b - 1))
                act.activation(ex[:, par, j], ps[:, RING + k % 3, :], ACT.Exp).then_inc(exp_ready, 1)

            def turn_out(b, i, k):
                n = BT * b + i
                act.wait_ge(at_turned, n + 1)
                after(act, proj_done, n - 1)
                act.copy(aT[:, i % 2].rearrange("p a t -> p (a t)"),
                         ps[:, RING + k % 3, 0:C]).then_inc(aT_ready, 1)

            def step(b, par, front, back):
                for k, name in enumerate(BACK):
                    if front and k == 0:
                        root(b + 1)
                    if back and name[0] == "S":
                        exps(b, par, int(name[1]), k)
                    if back and name[0] == "A":
                        turn_out(b, int(name[1]), k)
                    if front and k in FRONT_AT:
                        if FRONT_AT[k] == "turn":
                            turned(b + 1)
                        if FRONT_AT[k] == "query":
                            query(b + 1, 1 - par)
                        if FRONT_AT[k] == "turn_max":
                            max_rows(b + 1, 1 - par)
            pipeline(act, step)

        @block.tensor
        def _(pe):
            def turn(b, par):
                pe.wait_ge(xn_ready, b + 1)
                after(pe, maxT_ready, b)
                for cc in range(CC):
                    for i in range(BT):
                        m = pe.transpose(ps[:, cc, i * P:(i + 1) * P], xn[:, i, cc * P:(cc + 1) * P], ident[:])
                m.then_inc(xn_turned, 1)

            def query(b, par):
                pe.wait_ge(xnT_ready, b + 1)
                after(pe, max_ready, BT * b)
                for g in range(3):
                    rows = GROUPS[g] * DK
                    for cc in range(CC):
                        m = pe.matmul(ps[0:rows, 2 + g, :], s["wq"][:, cc, g * GR:g * GR + rows], xnT[:, cc],
                                      start=(cc == 0), stop=(cc == CC - 1))
                m.then_inc(q_done, 1)

            def score(b, par, i):
                if i == 0:
                    pe.wait_ge(q_ready, b + 1)
                    pe.wait_ge(kblk_ready, b + 1)
                else:
                    pe.wait_ge(max_ready, BT * b + i)
                for g in range(3):
                    cols = GROUPS[g] * KV
                    m = pe.matmul(ps[:, 2 + g, 0:cols], qT[0:GR, par, g, i * P:(i + 1) * P],
                                  kblk[0:GR, par, g, 0:cols], start=True, stop=True)
                m.then_inc(s1_done, 1)

            def turn_max(b, par):
                pe.wait_ge(max_ready, BT * (b + 1))
                for i in range(BT):
                    m = pe.transpose(ps[0:GK, 0, i * P:(i + 1) * P], nm[:, i, :], ident[:])
                m.then_inc(max_turned, 1)

            def free(b, k):
                prev, at = (k - 3, b) if k >= 3 else ((18 if k == 0 else 19 if k == 1 else 17), b - 1)
                kind, i = BACK[prev][0], int(BACK[prev][1])
                read, per = {"S": (exp_ready, PAIRS), "O": (at_ready, BT), "A": (aT_ready, BT),
                             "R": (res_done, BT)}[kind]
                after(pe, read, per * at + i + 1)

            def back(b, par, k):
                kind, i = BACK[k][0], int(BACK[k][1])
                bank = RING + k % 3
                free(b, k)
                if kind == "S":
                    if i == 0:
                        pe.wait_ge(maxT_ready, b + 1)
                    g, o = divmod(i, GH // 2)
                    pe.matmul(ps[:, bank, :], kblk[:, par, g, o * P:(o + 1) * P], qT[:, par, g, :],
                              start=True, stop=True).then_inc(s2_done, 1)
                if kind == "O":
                    if i == 0:
                        pe.wait_ge(exp_ready, PAIRS * (b + 1))
                    for j in range(PAIRS):
                        m = pe.matmul(ps[:, bank, j * VW:(j + 1) * VW], ex[:, par, j, i * P:(i + 1) * P],
                                      vblk[:, b, j, :], start=True, stop=True)
                    m.then_inc(o_done, 1)
                if kind == "A":
                    pe.wait_ge(at_ready, BT * b + i + 1)
                    for cc in range(CC):
                        m = pe.transpose(ps[:, bank, cc * P:(cc + 1) * P], at[:, i % 2, cc * P:(cc + 1) * P],
                                         ident[:])
                    m.then_inc(at_turned, 1)
                if kind == "R":
                    pe.wait_ge(aT_ready, BT * b + i + 1)
                    for cc in range(CC):
                        m = pe.matmul(ps[:, bank, 0:C], aT[:, i % 2, cc, :], s["wo"][:, cc, :],
                                      start=(cc == 0), stop=(cc == CC - 1))
                    m.then_inc(proj_done, 1)

            def step(b, par, front, do_back):
                for k in range(len(BACK)):
                    if do_back:
                        back(b, par, k)
                    if front and k in FRONT_AT:
                        name = FRONT_AT[k]
                        if name == "turn":
                            turn(b + 1, 1 - par)
                        elif name == "query":
                            query(b + 1, 1 - par)
                        elif name == "turn_max":
                            turn_max(b + 1, 1 - par)
                        else:
                            score(b + 1, 1 - par, int(name[3]))
            pipeline(pe, step)


def route_setup(nc, d, s):
    ps, ident = s["ps"], s["ident"]
    with ExitStack() as ctx:
        def sb(name, shape, dt=F32):
            return ctx.enter_context(nc.sbuf_tensor(name, shape, dt))

        def sem(name):
            return ctx.enter_context(nc.semaphore(name))

        phi = sb("phi", [P, ST, C])
        bias = sb("phi_bias", [P, ES // P])
        rest = sb("phi_rest", [P, 2, ES // P])
        parts = sb("phi_parts", [P, 3, ES // P], BF16)
        split = nc.dram_tensor("phi_b_split", [3, ES], BF16).ap()
        phi_in = sem("phi_in")
        bias_in = sem("phi_bias_in")
        parts_ready = sem("phi_parts_ready")
        rest_ready = sem("phi_rest_ready")
        parts_out = sem("phi_parts_out")
        rows_in = sem("phi_rows_in")
        filled = sem("r_filled")
        zeroed = sem("r_zeroed")
        shaped = sem("r_shaped")
        turned = sem("phi_turned")
        copied = sem("phi_copied")
        block = ctx.enter_context(nc.Block())

        @block.sync
        def _(sp):
            sp.dma_start(phi[:], d["phi_w"].rearrange("(a p) c -> p a c", p=P)).then_inc(phi_in, 16)
            sp.dma_start(bias[:], d["phi_b"].rearrange("(p a) -> p a", p=P)).then_inc(bias_in, 16)
            sp.wait_ge(parts_ready, 3)
            with nc.allow_non_contiguous_dma(reason="12 KB, once"):
                sp.dma_start(split.rearrange("j (p a) -> p j a", p=P), parts[:]).then_inc(parts_out, 16)
            sp.wait_ge(parts_out, 16)
            sp.wait_ge(filled, 1)
            for j in range(3):
                sp.dma_start(s["bias_rows"][32 * j:32 * j + 1, :], split[j:j + 1, :]).then_inc(rows_in, 16)
            sp.wait_ge(rows_in, 48)

        @block.vector
        def _(dve):
            dve.memset(s["bias_rows"][:], 0.0)
            dve.memset(s["ones"][:], 1.0)
            dve.memset(s["xacc"][:], 0.0).then_inc(filled, 1)
            dve.tensor_copy(s["identb"][:], ident[:]).then_inc(filled, 1)
            dve.wait_ge(bias_in, 16)
            dve.tensor_copy(parts[:, 0], bias[:]).then_inc(parts_ready, 1)
            dve.wait_ge(parts_ready, 1)
            dve.tensor_tensor(rest[:, 0], bias[:], parts[:, 0], ALU.subtract).then_inc(rest_ready, 1)
            dve.wait_ge(rest_ready, 1)
            dve.tensor_copy(parts[:, 1], rest[:, 0]).then_inc(parts_ready, 1)
            dve.wait_ge(parts_ready, 2)
            dve.tensor_tensor(rest[:, 1], rest[:, 0], parts[:, 1], ALU.subtract).then_inc(rest_ready, 1)
            dve.wait_ge(rest_ready, 2)
            dve.tensor_copy(parts[:, 2], rest[:, 1]).then_inc(parts_ready, 1)
            for n in range(CC * EB):
                dve.wait_ge(turned, n + 1)
                dve.tensor_copy(s["phiT"][:, n // EB, (n % EB) * BLK:(n % EB + 1) * BLK],
                                ps[:, n % 2, :]).then_inc(copied, 1)

        @block.gpsimd
        def _(pool):
            pool.memset(s["sel_add"][:], 0.0)
            pool.memset(s["sel_swap"][:], 0.0).then_inc(zeroed, 1)
            pool.wait_ge(zeroed, 1)
            by_expert = dict(compare_op=ALU.not_equal, base=0, pattern=[[1, EXPERTS], [0, SLOTS]],
                             channel_multiplier=-1)
            pool.affine_select(out=s["sel_add"][:], in_=s["sel_add"][:], fill=1.0, **by_expert).then_inc(shaped, 1)
            pool.affine_select(out=s["sel_swap"][:], in_=s["sel_swap"][:], fill=-1.0, **by_expert).then_inc(shaped, 1)
            pool.wait_ge(shaped, 2)
            pool.affine_select(out=s["sel_swap"][:], in_=s["sel_swap"][:], fill=1.0, compare_op=ALU.not_equal,
                               base=EXPERTS, pattern=[[0, EXPERTS], [1, SLOTS]],
                               channel_multiplier=-1).then_inc(shaped, 1)
            pool.wait_ge(shaped, 3)

        @block.tensor
        def _(pe):
            pe.wait_ge(phi_in, 16)
            for n in range(CC * EB):
                if n >= 2:
                    pe.wait_ge(copied, n - 1)
                for i in range(BLK // P):
                    m = pe.transpose(ps[:, n % 2, i * P:(i + 1) * P],
                                     phi[:, (n % EB) * (BLK // P) + i, (n // EB) * P:(n // EB + 1) * P], ident[:])
                m.then_inc(turned, 1)


def route(nc, d, s):
    ps, x_res, ident = s["ps"], s["x_res"], s["ident"]
    phiT, xacc = s["phiT"], s["xacc"]
    SMALL, TURN, DISP = 4, 5, 6
    NM = EXPERTS + SLOTS
    UNITS = CC * EB
    with ExitStack() as ctx:
        def sb(name, shape, dt=F32):
            return ctx.enter_context(nc.sbuf_tensor(name, shape, dt))

        def sem(name):
            return ctx.enter_context(nc.semaphore(name))

        stats = sb("r_stats", [P, 6])
        mv = sb("r_mv", [P, 2])
        lnv = sb("r_lnv", [P, 1])
        rstd = sb("r_rstd", [P, 1])
        xn = sb("r_xn", [P, 2, C])
        xh = sb("r_xh", [P, 4, C])
        xhT = sb("r_xhT", [P, 2, CC, P])
        nab = sb("r_nab", [P, 2, NM], BF16)
        nabT = sb("r_nabT", [NM, P], BF16)
        disp = sb("r_disp", [P, 4, ES])
        comb = sb("r_comb", [P, 2, ES])
        combT = sb("r_combT", [P, 2, ST, P])
        sum_d = sb("r_sum_d", [P, EXPERTS])
        sum_c = sb("r_sum_c", [P, SLOTS])
        rec_d = sb("r_rec_d", [P, 2, EXPERTS])
        rec_c = sb("r_rec_c", [P, 2, SLOTS])
        turned_max = ps[0:NM, SMALL, 0:P // 2].bitcast(BF16)

        stats_ready = sem("r_stats_ready")
        waited = sem("r_waited")
        copy_waited = sem("r_copy_waited")
        mv_ready = sem("r_mv_ready")
        lnv_ready = sem("r_lnv_ready")
        rstd_ready = sem("r_rstd_ready")
        xn_ready = sem("r_xn_ready")
        xh_ready = sem("r_xh_ready")
        xn_turned = sem("r_xn_turned")
        xhT_ready = sem("r_xhT_ready")
        logits_done = sem("r_logits_done")
        max_ready = sem("r_max_ready")
        max_turned = sem("r_max_turned")
        maxT_ready = sem("r_maxT_ready")
        less_a = sem("r_less_expert_max")
        less_b = sem("r_less_slot_max")
        exp_d = sem("r_exp_d")
        exp_c = sem("r_exp_c")
        sum_d_ready = sem("r_sum_d_ready")
        sum_c_ready = sem("r_sum_c_ready")
        rec_d_ready = sem("r_rec_d_ready")
        rec_c_ready = sem("r_rec_c_ready")
        disp_ready = sem("r_disp_ready")
        comb_ready = sem("r_comb_ready")
        comb_turned = sem("r_comb_turned")
        combT_ready = sem("r_combT_ready")
        combT_out = [sem(f"r_combT_out{i}") for i in range(2)]
        unit_done = sem("r_unit_done")
        unit_added = sem("r_unit_added")
        block = ctx.enter_context(nc.Block())

        def pipeline(eng, step):
            for t in range(4):
                step(t, t)
            with eng.Fori(4, NT - 7, 4) as i:
                for r in range(4):
                    step(i + r, r)
            for t in range(NT - 4, NT + 2):
                step(t, t % 4)

        def known(t):
            return isinstance(t, int)

        def has_tile(t):
            return not known(t) or 0 <= t < NT

        def pair_units(t, r):
            return 4 * (t - r) + UNITS

        @block.sync
        def _(sp):
            def step(t, r):
                if has_tile(t - 1):
                    par = (r + 1) % 2
                    sp.wait_ge(combT_ready, EB * t)
                    sp.dma_start(s["combT_dram"][bass.ds(t - 1, 1)].rearrange("t p n -> p (t n)"),
                                 combT[:, par].rearrange("p a t -> p (a t)")).then_inc(combT_out[par], 16)
            pipeline(sp, step)
            for par in range(2):
                sp.wait_ge(combT_out[par], 16 * NT // 2)

        @block.vector
        def _(dve):
            def norm(t, r):
                dve.bn_stats(stats[:], x_res[:, bass.ds(t, 1), :].rearrange("p a c -> p (a c)")
                             if not known(t) else x_res[:, t, :]).then_inc(stats_ready, 1)
                dve.wait_ge(stats_ready, t + 1)
                dve.sem_inc(waited, 1)
                dve.bn_aggr(mv[:], stats[:]).then_inc(mv_ready, 1)

            def normed(t, r):
                dve.wait_ge(rstd_ready, t + 1)
                after(dve, xn_turned, t - 1)
                after(dve, xh_ready, t - 1)
                dve.tensor_scalar(xn[:, r % 2], x_res[:, t, :], mv[:, 0:1], rstd[:, 0:1],
                                  ALU.subtract, ALU.mult).then_inc(xn_ready, 1)

            def maxima(t, r):
                L = ps[:, 0:EB, :]
                dve.wait_ge(logits_done, t + 1)
                after(dve, max_turned, t - 1)
                dve.tensor_reduce(nab[:, r % 2, 0:EXPERTS], L.rearrange("p b (n q) -> p (b n) q", q=SLOTS),
                                  AX.X, ALU.max, negate=True)
                dve.tensor_reduce(nab[:, r % 2, EXPERTS:NM], L.rearrange("p b (n q) -> p q (b n)", q=SLOTS),
                                  AX.X, ALU.max, negate=True).then_inc(max_ready, 1)

            def sums(t, r):
                dve.wait_ge(exp_d, t + 1)
                dve.tensor_reduce(sum_d[:], disp[:, r].rearrange("p (n q) -> p n q", q=SLOTS), AX.X,
                                  ALU.add).then_inc(sum_d_ready, 1)
                dve.wait_ge(sum_d_ready, t + 1)
                after(dve, disp_ready, t - 1)
                dve.reciprocal(rec_d[:, r % 2], sum_d[:]).then_inc(rec_d_ready, 1)
                dve.wait_ge(exp_c, 2 * t + 2)
                dve.tensor_reduce(sum_c[:], comb[:, r % 2].rearrange("p (n q) -> p q n", q=SLOTS), AX.X,
                                  ALU.add).then_inc(sum_c_ready, 1)
                dve.wait_ge(sum_c_ready, t + 1)
                after(dve, comb_ready, t - 1)
                dve.reciprocal(rec_c[:, r % 2], sum_c[:]).then_inc(rec_c_ready, 1)

            def unit(t, r, n):
                u = (r % 2) * 4 + n
                done = pair_units(t - 2, r % 2) - UNITS + u + 1
                dve.wait_ge(unit_done, done)
                part = xacc[:, u // EB, (u % EB) * BLK:(u % EB + 1) * BLK]
                dve.tensor_tensor(part, ps[:, DISP + u % 2, :], part, ALU.add).then_inc(unit_added, 1)

            def step(t, r):
                if known(t) and t == 0:
                    norm(0, 0)
                    normed(0, 0)
                if has_tile(t):
                    maxima(t, r)
                if has_tile(t - 2) or known(t) and t >= 2:
                    unit(t, r, 0)
                    unit(t, r, 1)
                if has_tile(t + 1):
                    norm(t + 1, (r + 1) % 4)
                if has_tile(t - 2) or known(t) and t >= 2:
                    unit(t, r, 2)
                    unit(t, r, 3)
                if has_tile(t + 1):
                    normed(t + 1, (r + 1) % 4)
                if has_tile(t):
                    sums(t, r)
            pipeline(dve, step)

        @block.gpsimd
        def _(pool):
            def step(t, r):
                if known(t) and t == 0:
                    pool.wait_ge(xn_ready, 1)
                    pool.tensor_copy(xh[:, 0], xn[:, 0]).then_inc(xh_ready, 1)
                if has_tile(t + 1):
                    q = (r + 1) % 4
                    pool.wait_ge(xn_ready, t + 2)
                    after(pool, unit_done, pair_units(t - 3, (r + 1) % 2))
                    pool.sem_inc(copy_waited, 1)
                    pool.tensor_copy(xh[:, q], xn[:, q % 2]).then_inc(xh_ready, 1)
                if has_tile(t):
                    pool.wait_ge(rec_d_ready, t + 1)
                    pool.tensor_tensor(disp[:, r].rearrange("p (n q) -> p n q", q=SLOTS),
                                       disp[:, r].rearrange("p (n q) -> p n q", q=SLOTS),
                                       rec_d[:, r % 2].unsqueeze(2).to_broadcast([P, EXPERTS, SLOTS]),
                                       ALU.mult).then_inc(disp_ready, 1)
                    pool.wait_ge(rec_c_ready, t + 1)
                    pool.tensor_tensor(comb[:, r % 2].rearrange("p (n q) -> p n q", q=SLOTS),
                                       comb[:, r % 2].rearrange("p (n q) -> p n q", q=SLOTS),
                                       rec_c[:, r % 2].unsqueeze(1).to_broadcast([P, EXPERTS, SLOTS]),
                                       ALU.mult).then_inc(comb_ready, 1)
            pipeline(pool, step)

        @block.scalar
        def _(act):
            def root(t):
                act.wait_ge(mv_ready, t + 1)
                act.activation(lnv[:], mv[:, 1:2], ACT.Ln, bias=s["eps"][:, 0:1]).then_inc(lnv_ready, 1)
                act.wait_ge(lnv_ready, t + 1)
                act.activation(rstd[:], lnv[:], ACT.Exp, scale=-0.5).then_inc(rstd_ready, 1)

            def xhT_copy(t, r):
                act.wait_ge(xn_turned, t + 1)
                after(act, logits_done, t - 1)
                act.copy(xhT[:, r % 2].rearrange("p a t -> p (a t)"), ps[:, SMALL, 0:C]).then_inc(xhT_ready, 1)

            def combT_copy(t, r, n):
                act.wait_ge(comb_turned, EB * t + n + 1)
                if n == 0:
                    after(act, combT_out[r % 2], 8 * (t - r % 2))
                act.copy(combT[:, r % 2, 4 * n:4 * n + 4].rearrange("p a t -> p (a t)"),
                         ps[:, TURN, :]).then_inc(combT_ready, 1)

            def step(t, r):
                q = (r - 1) % 4
                if known(t) and t == 0:
                    root(0)
                    xhT_copy(0, 0)
                if has_tile(t - 1):
                    combT_copy(t - 1, q, 0)
                    combT_copy(t - 1, q, 1)
                if has_tile(t):
                    act.wait_ge(max_turned, t + 1)
                    after(act, less_b, t)
                    act.copy(nabT[:], turned_max).then_inc(maxT_ready, 1)
                if has_tile(t - 1):
                    combT_copy(t - 1, q, 2)
                if has_tile(t + 1):
                    root(t + 1)
                if has_tile(t):
                    act.wait_ge(less_a, t + 1)
                    after(act, unit_done, pair_units(t - 4, r % 2))
                    act.activation(disp[:, r], ps[:, 0:EB, :].rearrange("p b n -> p (b n)"),
                                   ACT.Exp).then_inc(exp_d, 1)
                if has_tile(t - 1):
                    combT_copy(t - 1, q, 3)
                if has_tile(t):
                    act.wait_ge(less_b, t + 1)
                    after(act, comb_turned, EB * (t - 1))
                    for h in range(2):
                        act.activation(comb[:, r % 2, h * 2 * BLK:(h + 1) * 2 * BLK],
                                       ps[:, 2 * h:2 * h + 2, :].rearrange("p b n -> p (b n)"),
                                       ACT.Exp).then_inc(exp_c, 1)
                if has_tile(t + 1):
                    xhT_copy(t + 1, (r + 1) % 4)
            act.preload_act_table_set("natural_log_exp_and_others")
            pipeline(act, step)

        @block.tensor
        def _(pe):
            def turn_xn(t, r):
                pe.wait_ge(xn_ready, t + 1)
                after(pe, maxT_ready, t)
                for cc in range(CC):
                    m = pe.transpose(ps[:, SMALL, cc * P:(cc + 1) * P], xn[:, r % 2, cc * P:(cc + 1) * P],
                                     ident[:])
                m.then_inc(xn_turned, 1)

            def logits(t, r):
                pe.wait_ge(xhT_ready, t + 1)
                for b in range(EB):
                    if b % 2 == 0:
                        after(pe, exp_c, 2 * t - 1 + b // 2)
                    cols = slice(b * BLK, (b + 1) * BLK)
                    pe.matmul(ps[:, b, :], s["ones"][:], s["bias_rows"][:, cols], start=True, stop=False)
                    for cc in range(CC):
                        m = pe.matmul(ps[:, b, :], xhT[:, r % 2, cc], phiT[:, cc, cols],
                                      start=False, stop=(cc == CC - 1))
                m.then_inc(logits_done, 1)

            def turn_max(t, r):
                pe.wait_ge(max_ready, t + 1)
                pe.wait_ge(xhT_ready, t + 1)
                pe.transpose(turned_max, nab[:, r % 2, :], s["identb"][:]).then_inc(max_turned, 1)

            def shift(t, r, rows, selector, done):
                for b in range(EB):
                    m = pe.matmul(ps[:, b, :], nabT[0:rows], selector[0:rows, b * BLK:(b + 1) * BLK],
                                  start=False, stop=True, skip_group_check=True)
                m.then_inc(done, 1)

            def unit(t, r, n):
                u = (r % 2) * 4 + n
                q = (r - 2 - r % 2) % 4
                if n == 0 and r % 2 == 0:
                    pe.wait_ge(disp_ready, t)
                    pe.wait_ge(xh_ready, t)
                after(pe, unit_added, pair_units(t - 2, r % 2) - UNITS + u - 1)
                for k in range(2):
                    m = pe.matmul(ps[:, DISP + u % 2, :], xh[:, q + k, (u // EB) * P:(u // EB + 1) * P],
                                  disp[:, q + k, (u % EB) * BLK:(u % EB + 1) * BLK],
                                  start=(k == 0), stop=(k == 1))
                m.then_inc(unit_done, 1)

            def turn_comb(t, r, n):
                if n == 0:
                    pe.wait_ge(comb_ready, t + 1)
                after(pe, combT_ready, EB * t + n)
                for i in range(BLK // P):
                    m = pe.transpose(ps[:, TURN, i * P:(i + 1) * P],
                                     comb[:, r % 2, n * BLK + i * P:n * BLK + (i + 1) * P], ident[:])
                m.then_inc(comb_turned, 1)

            def step(t, r):
                def pair(n):
                    if known(t) and t < 2:
                        pass
                    else:
                        unit(t, r, n)
                    if has_tile(t - 1):
                        turn_comb(t - 1, (r - 1) % 4, n)
                if known(t) and t == 0:
                    turn_xn(0, 0)
                if has_tile(t):
                    logits(t, r)
                pair(0)
                pair(1)
                if has_tile(t):
                    turn_max(t, r)
                pair(2)
                if has_tile(t):
                    pe.wait_ge(maxT_ready, t + 1)
                    shift(t, r, EXPERTS, s["sel_add"], less_a)
                pair(3)
                if has_tile(t):
                    pe.wait_ge(exp_d, t + 1)
                    shift(t, r, NM, s["sel_swap"], less_b)
                if has_tile(t + 1):
                    turn_xn(t + 1, (r + 1) % 4)
            pipeline(pe, step)


def experts(nc, d, s):
    ps, ident, xacc, xt, yt = s["ps"], s["ident"], s["xacc"], s["xt"], s["yt"]
    RING = 3
    with ExitStack() as ctx:
        def sb(name, shape):
            return ctx.enter_context(nc.sbuf_tensor(name, shape, F32))

        def sem(name):
            return ctx.enter_context(nc.semaphore(name))

        stats = sb("e_stats", [P, ST, 6])
        mv = sb("e_mv", [P, ST, 2])
        lnv = sb("e_lnv", [P, ST])
        rstd = sb("e_rstd", [P, ST])
        shift = sb("e_shift", [P, ST])
        ew = sb("e_weights", [P, RING, EPT, CC, C])
        eb = sb("e_bias", [P, ST, C])
        w_in = [sem(f"e_w_in{i}") for i in range(RING)]
        b_in = sem("e_b_in")
        x_turned = sem("e_x_turned")
        xt_ready = sem("e_xt_ready")
        stats_ready = sem("e_stats_ready")
        mv_ready = sem("e_mv_ready")
        lnv_ready = sem("e_lnv_ready")
        rstd_ready = sem("e_rstd_ready")
        shift_ready = sem("e_shift_ready")
        tanh_ready = sem("e_tanh_ready")
        t_turned = sem("e_t_turned")
        thT_ready = sem("e_thT_ready")
        y_done = sem("e_y_done")
        y_ready = sem("e_y_ready")
        block = ctx.enter_context(nc.Block())

        @block.sync
        def _(sp):
            w = d["expert_w"].rearrange("(s e) (a p) h -> s p e a h", e=EPT, p=P)
            for n in range(ST):
                if n >= RING:
                    sp.wait_ge(y_done, n - RING + 1)
                sp.dma_start(ew[:, n % RING].rearrange("p e a h -> p (e a) h"),
                             w[n].rearrange("p e a h -> p (e a) h")).then_inc(w_in[n % RING], 16)
                if n == 0:
                    for e in range(EPT):
                        sp.dma_start(eb[e * SLOTS:(e + 1) * SLOTS],
                                     d["expert_b"].rearrange("(s e) h -> e s h", e=EPT)[e]
                                     .partition_broadcast(SLOTS)).then_inc(b_in, 16)

        @block.tensor
        def _(pe):
            for n in range(ST):
                if n >= 2:
                    pe.wait_ge(xt_ready, n - 1)
                for cc in range(CC):
                    m = pe.transpose(ps[:, n % 2, cc * P:(cc + 1) * P], xacc[:, cc, n * P:(n + 1) * P], ident[:])
                m.then_inc(x_turned, 1)
            for n in range(ST):
                pe.wait_ge(tanh_ready, n + 1)
                if n >= 2:
                    pe.wait_ge(thT_ready, n - 1)
                for cc in range(CC):
                    m = pe.transpose(ps[:, 2 + n % 2, cc * P:(cc + 1) * P], xt[:, n, cc * P:(cc + 1) * P], ident[:])
                m.then_inc(t_turned, 1)
            for n in range(ST):
                pe.wait_ge(w_in[n % RING], 16 * (n // RING + 1))
                pe.wait_ge(thT_ready, n + 1)
                if n >= 2:
                    pe.wait_ge(y_ready, n - 1)
                for e in range(EPT):
                    rows = slice(e * SLOTS, (e + 1) * SLOTS)
                    for cc in range(CC):
                        m = pe.matmul(ps[rows, 4 + n % 2, 0:C], xacc[:, cc, n * P + e * SLOTS:n * P + (e + 1) * SLOTS],
                                      ew[:, n % RING, e, cc, :], start=(cc == 0), stop=(cc == CC - 1),
                                      tile_position=(0, e * SLOTS))
                m.then_inc(y_done, 1)

        @block.vector
        def _(dve):
            for n in range(ST):
                dve.wait_ge(x_turned, n + 1)
                dve.tensor_scalar(xt[:, n], ps[:, n % 2, 0:C], -33000.0, 65000.0, ALU.max, ALU.min).then_inc(xt_ready, 1)
            for n in range(ST):
                dve.wait_ge(xt_ready, n + 1)
                dve.bn_stats(stats[:, n], xt[:, n]).then_inc(stats_ready, 1)
            for n in range(ST):
                dve.wait_ge(stats_ready, n + 1)
                dve.bn_aggr(mv[:, n], stats[:, n]).then_inc(mv_ready, 1)
            dve.wait_ge(rstd_ready, 1)
            dve.wait_ge(mv_ready, ST)
            dve.scalar_tensor_tensor(out=shift[:], in0=mv[:, :, 0], scalar=-1.0, in1=rstd[:], op0=ALU.mult,
                                     op1=ALU.mult).then_inc(shift_ready, 1)
            for n in range(ST):
                dve.wait_ge(t_turned, n + 1)
                if n == 0:
                    dve.wait_ge(x_turned, ST)
                dve.tensor_copy(xacc[:, :, n * P:(n + 1) * P],
                                ps[:, 2 + n % 2, 0:C].rearrange("p (a t) -> p a t", a=CC)).then_inc(thT_ready, 1)
            dve.wait_ge(b_in, 16 * EPT)
            for n in range(ST):
                dve.wait_ge(y_done, n + 1)
                dve.tensor_tensor(yt[:, n], ps[:, 4 + n % 2, 0:C], eb[:, n], ALU.add).then_inc(y_ready, 1)

        @block.scalar
        def _(act):
            act.wait_ge(mv_ready, ST)
            act.activation(lnv[:], mv[:, :, 1], ACT.Ln, bias=s["eps"][:, 0:1]).then_inc(lnv_ready, 1)
            act.wait_ge(lnv_ready, 1)
            act.activation(rstd[:], lnv[:], ACT.Exp, scale=-0.5).then_inc(rstd_ready, 1)
            act.wait_ge(shift_ready, 1)
            act.wait_ge(rstd_ready, 1)
            for n in range(ST):
                act.activation(xt[:, n], xt[:, n], ACT.Tanh, bias=shift[:, n:n + 1],
                               scale=rstd[:, n:n + 1]).then_inc(tanh_ready, 1)


def combine(nc, d, s):
    ps, x_res, yt = s["ps"], s["x_res"], s["yt"]
    RING = 4
    with ExitStack() as ctx:
        def sem(name):
            return ctx.enter_context(nc.semaphore(name))

        ct = ctx.enter_context(nc.sbuf_tensor("c_combT", [P, RING, ST * P], F32))
        ct_in = [sem(f"c_in{i}") for i in range(RING)]
        y_done = sem("c_y_done")
        sum_ready = sem("c_sum_ready")
        stored = [sem(f"c_stored{i}") for i in range(RING)]
        block = ctx.enter_context(nc.Block())

        def pipeline(eng, step):
            for r in range(RING):
                step(r, r)
            with eng.Fori(RING, NT - RING + 1, RING) as i:
                for r in range(RING):
                    step(i + r, r)

        @block.sync
        def _(sp):
            def step(t, r):
                after(sp, y_done, t - RING + 1)
                sp.dma_start(ct[:, r], s["combT_dram"][bass.ds(t, 1)].rearrange("t p n -> p (t n)")
                             ).then_inc(ct_in[r], 16)
            pipeline(sp, step)

        @block.scalar
        def _(act):
            def step(t, r):
                act.wait_ge(sum_ready, t + 1)
                act.dma_start(s["out_dram"][:, bass.ds(t, 1), :], x_res[:, bass.ds(t, 1), :]).then_inc(stored[r], 16)
            pipeline(act, step)
            for r in range(RING):
                act.wait_ge(stored[r], 16 * NT // RING)

        @block.tensor
        def _(pe):
            def step(t, r):
                pe.wait_ge(ct_in[r], 4 * (t - r) + 16)
                after(pe, sum_ready, t - 1)
                for n in range(ST):
                    m = pe.matmul(ps[:, r % 2, 0:C], ct[:, r, n * P:(n + 1) * P], yt[:, n],
                                  start=(n == 0), stop=(n == ST - 1))
                m.then_inc(y_done, 1)
            pipeline(pe, step)

        @block.vector
        def _(dve):
            def step(t, r):
                dve.wait_ge(y_done, t + 1)
                dve.tensor_tensor(x_res[:, t, :], ps[:, r % 2, 0:C], x_res[:, t, :], ALU.add).then_inc(sum_ready, 1)
            pipeline(dve, step)


def route_and_experts(nc, d, s):
    with ExitStack() as ctx:
        s["combT_dram"] = nc.dram_tensor("combine_turned", [NT, P, ST * P], F32).ap()
        s["xacc"] = ctx.enter_context(nc.sbuf_tensor("xacc", [P, CC, ES], F32))
        with ExitStack() as route_ctx:
            for name, shape, dt in (("phiT", [P, CC, ES], F32), ("sel_add", [EXPERTS, ES], BF16),
                                    ("sel_swap", [EXPERTS + SLOTS, ES], BF16), ("bias_rows", [96, ES], BF16),
                                    ("ones", [96, P], BF16), ("identb", [P, P], BF16)):
                s[name] = route_ctx.enter_context(nc.sbuf_tensor(f"r_{name}", shape, dt))
            route_setup(nc, d, s)
            route(nc, d, s)
        s["xt"] = ctx.enter_context(nc.sbuf_tensor("e_xt", [P, ST, C], F32))
        s["yt"] = ctx.enter_context(nc.sbuf_tensor("e_yt", [P, ST, C], F32))
        experts(nc, d, s)
        combine(nc, d, s)



def decoder(nc, d, out):
    with ExitStack() as ctx:
        def sb(name, shape, dt=F32):
            return ctx.enter_context(nc.sbuf_tensor(name, shape, dt))

        s = {
            "ident": sb("ident", [P, P]),
            "eps": sb("eps", [P, 1]),
            "w": sb("w", [P, CC]),
            "u": sb("u", [P, CC]),
            "cap": sb("cap", [P, CC]),
            "attn_wT": sb("attn_wT", [P, 3, CC, C]),
            "x_res": sb("x_res", [P, NT, C]),
            "ps": ctx.enter_context(nc.psum_tensor("ps", [P, 8, BLK], F32)),
            "x_dram": d["x"].rearrange("b (i p) c -> p (b i) c", p=P),
            "out_dram": out.rearrange("b (i p) c -> p (b i) c", p=P),
        }
        setup(nc, d, s)
        mixing(nc, d, s)
        with ExitStack() as attend_ctx:
            for name, shape in (("wq", [P, CC, C]), ("wo", [P, CC, C]), ("bq", [GR, 3]), ("bo", [P, C]),
                                ("kT", [GR, 3, B * KV]), ("headmask", [GR, GH]), ("kblk", [GK, 2, 3, GN]),
                                ("vblk", [P, B, PAIRS, VW]), ("qT", [GK, 2, 3, T]), ("nm", [P, BT, GK])):
                s[name] = attend_ctx.enter_context(nc.sbuf_tensor(f"x_{name}", shape, F32))
            attend_setup(nc, d, s)
            attend(nc, d, s)
        route_and_experts(nc, d, s)


_INS = {"x": "x", "ctx": "ctx_512", "attn_Wk": "L0_attn_Wk", "attn_Wr": "L0_attn_Wr", "attn_Wo": "L0_attn_Wo",
        "attn_decay": "L0_attn_time_decay", "attn_first": "L0_attn_time_first",
        "Wq": "L0_xattn_Wq", "bq": "L0_xattn_bq", "Wk": "L0_xattn_Wk", "bk": "L0_xattn_bk",
        "Wv": "L0_xattn_Wv", "bv": "L0_xattn_bv", "Wo": "L0_xattn_Wo", "bo": "L0_xattn_bo",
        "phi_w": "L0_ffn_phi_w", "phi_b": "L0_ffn_phi_b", "expert_w": "L0_ffn_expert_w",
        "expert_b": "L0_ffn_expert_b"}


def kernel(**inputs):
    import numpy as np
    import concourse.bacc as bacc
    from concourse.bass_utils import run_bass_kernel_spmd

    nc = bacc.Bacc("TRN2", target_bir_lowering=False, num_devices=1)
    arrays, dram = {}, {}
    for short, name in _INS.items():
        a = np.ascontiguousarray(inputs[name])
        arrays[f"in_{short}"] = a
        dram[short] = nc.dram_tensor(f"in_{short}", a.shape, F32, kind="ExternalInput").ap()
    out = nc.dram_tensor("out_x", (B, T, C), F32, kind="ExternalOutput").ap()
    decoder(nc, dram, out)
    return run_bass_kernel_spmd(nc, [arrays], core_ids=[0]).results[0]["out_x"]
```

```python
from contextlib import ExitStack

import concourse.bass as bass
from concourse import mybir

F32 = mybir.dt.float32
F32R = mybir.dt.float32r
BF16 = mybir.dt.bfloat16
ALU = mybir.AluOpType
ACT = mybir.ActivationFunctionType
AX = mybir.AxisListType

P = 128
B, T, C = 8, 512, 256
CC = C // P
BT = T // P
NT = B * BT
KV, CD = 64, 128
HEADS = 16
DK = C // HEADS
EPS = 1e-5
NEG_INF = -1e38
LIMIT = 40.0

GH = 6
GROUPS = [6, 6, 4]
GR = GH * DK
GK = GR + HEADS
GN = GH * KV
PAIRS = HEADS // 2
VW = 2 * (DK + 1)

EXPERTS, SLOTS = 64, 32
ES = EXPERTS * SLOTS
ST = ES // P
EPT = P // SLOTS
BLK = 512
EB = ES // BLK


def after(eng, sem, count):
    if isinstance(count, int) and count <= 0:
        return
    eng.wait_ge(sem, count)


def setup(nc, d, s):
    with ExitStack() as ctx:
        def sem(name):
            return ctx.enter_context(nc.semaphore(name))

        raw = ctx.enter_context(nc.sbuf_tensor("raw_weights", [P, 3, CC, C], F32))
        decay = ctx.enter_context(nc.sbuf_tensor("decay", [P, CC], F32))
        decay_e = ctx.enter_context(nc.sbuf_tensor("decay_e", [P, CC], F32))
        weights_in = sem("weights_in")
        vectors_in = sem("vectors_in")
        ident_zero = sem("ident_zero")
        ident_done = sem("ident_done")
        turned = sem("weights_turned")
        copied = sem("weights_copied")
        decay_exp = sem("decay_exp")
        consts = sem("consts")
        bank_sem = [sem(f"bank_turned{i}") for i in range(2)]
        block = ctx.enter_context(nc.Block())

        @block.sync
        def _(sp):
            for n, w in enumerate((d["attn_Wk"], d["attn_Wr"], d["attn_Wo"])):
                sp.dma_start(raw[:, n], w.rearrange("(a p) c -> p a c", p=P)).then_inc(weights_in, 16)
            sp.wait_ge(weights_in, 48)
            sp.wait_ge(vectors_in, 16 * 2)

        @block.gpsimd
        def _(pool):
            pool.memset(s["ident"][:], 0.0).then_inc(ident_zero, 1)
            pool.wait_ge(ident_zero, 1)
            pool.affine_select(out=s["ident"][:], in_=s["ident"][:], compare_op=ALU.not_equal, fill=1.0,
                               base=0, pattern=[[-1, P]], channel_multiplier=1).then_inc(ident_done, 1)

        @block.scalar
        def _(act):
            with nc.allow_non_contiguous_dma(reason="one value per channel, once"):
                act.dma_start(decay[:], d["attn_decay"].rearrange("(a p) -> p a", p=P)).then_inc(vectors_in, 16)
                act.dma_start(s["u"][:], d["attn_first"].rearrange("(a p) -> p a", p=P)).then_inc(vectors_in, 16)
            act.wait_ge(vectors_in, 32)
            act.activation(decay_e[:], decay[:], ACT.Exp).then_inc(decay_exp, 1)

        @block.tensor
        def _(pe):
            pe.wait_ge(ident_done, 1)
            pe.wait_ge(weights_in, 48)
            for n in range(3):
                for cc in range(CC):
                    if n * CC + cc >= 2:
                        pe.wait_ge(copied, n * CC + cc - 1)
                    for hc in range(CC):
                        m = pe.transpose(s["ps"][:, (n * CC + cc) % 2, hc * P:(hc + 1) * P],
                                         raw[:, n, hc, cc * P:(cc + 1) * P], s["ident"][:])
                    m.then_inc(turned, 1)

        @block.vector
        def _(dve):
            dve.memset(s["eps"][:], EPS).then_inc(consts, 1)
            for n in range(3 * CC):
                dve.wait_ge(turned, n + 1)
                dve.tensor_copy(s["attn_wT"][:, n // CC, n % CC, :], s["ps"][:, n % 2, 0:C]).then_inc(copied, 1)
            dve.wait_ge(decay_exp, 1)
            dve.tensor_scalar(s["w"][:], decay_e[:], -1.0, None, ALU.mult).then_inc(consts, 1)
            dve.tensor_scalar(s["cap"][:], s["u"][:], -1.0, LIMIT, ALU.mult, ALU.add).then_inc(consts, 1)
            dve.wait_ge(consts, 3)


def mixing(nc, d, s):
    ps, x_res, ident = s["ps"], s["x_res"], s["ident"]
    wkT, wrT, woT = (s["attn_wT"][:, n] for n in range(3))
    with ExitStack() as ctx:
        def sb(name, shape):
            return ctx.enter_context(nc.sbuf_tensor(name, shape, F32))

        def sem(name):
            return ctx.enter_context(nc.semaphore(name))

        stats = sb("m_stats", [P, 2, BT, 6])
        mv = sb("m_mv", [P, 2, BT, 2])
        lnv = sb("m_lnv", [P, 2, BT])
        rstd = sb("m_rstd", [P, 2, BT])
        xn = sb("m_xn", [P, 2, BT, C])
        xnT = sb("m_xnT", [P, CC, T])
        kr = sb("m_kr", [P, 2, 2, CC, T])
        top = sb("m_top", [P, CC, T + 1])
        num = sb("m_num", [P, CC, T + 1])
        den = sb("m_den", [P, CC, T + 1])
        gap = sb("m_gap", [P, CC, T])
        up = sb("m_up", [P, 2, CC, T])
        down = sb("m_down", [P, 2, CC, T])
        ev = sb("m_ev", [P, 2, CC, T])
        now = sb("m_now", [P, 2, CC, T])
        er = sb("m_er", [P, CC, T])
        bot = sb("m_bot", [P, CC, T])
        val = sb("m_val", [P, CC, T])
        lsig = sb("m_lsig", [P, 2, CC, T])
        oT = sb("m_oT", [P, 2, CC, T])

        x_in = [sem(f"m_x_in{i}") for i in range(2)]
        stats_ready = sem("m_stats_ready")
        mv_ready = sem("m_mv_ready")
        waited = sem("m_waited")
        lnv_ready = sem("m_lnv_ready")
        rstd_ready = sem("m_rstd_ready")
        xn_ready = sem("m_xn_ready")
        xn_turned = sem("m_xn_turned")
        xnT_ready = sem("m_xnT_ready")
        kr_done = sem("m_kr_done")
        kr_ready = sem("m_kr_ready")
        first = sem("m_first_columns")
        top_ready = sem("m_top_ready")
        gap_ready = sem("m_gap_ready")
        up_ready = sem("m_up_ready")
        down_ready = sem("m_down_ready")
        now_capped = sem("m_now_capped")
        now_ready = sem("m_now_ready")
        up_exp = sem("m_up_exp")
        down_exp = sem("m_down_exp")
        er_ready = sem("m_er_ready")
        er_capped = sem("m_er_capped")
        ev_ready = sem("m_ev_ready")
        num_ready = sem("m_num_ready")
        den_ready = sem("m_den_ready")
        bot_ready = sem("m_bot_ready")
        val_ready = sem("m_val_ready")
        vsum_ready = sem("m_vsum_ready")
        lbot_ready = sem("m_lbot_ready")
        lsig_ready = sem("m_lsig_ready")
        lsum_ready = sem("m_lsum_ready")
        rec_ready = sem("m_rec_ready")
        oT_ready = sem("m_oT_ready")
        out_done = sem("m_out_done")
        res_done = sem("m_res_done")
        block = ctx.enter_context(nc.Block())

        def loaded(b, par):
            return 8 * b + 16 - 8 * par

        def pipeline(eng, step):
            for b in range(-2, 2):
                step(b, b % 2)
            with eng.Fori(2, B - 3, 2) as i:
                step(i, 0)
                step(i + 1, 1)
            for b in range(B - 2, B + 1):
                step(b, b % 2)

        def has(b):
            return not isinstance(b, int) or 0 <= b < B

        @block.sync
        def _(sp):
            def load(b, par):
                after(sp, stats_ready, b - 1)
                sp.dma_start(x_res[:, bass.ds(b * BT, BT), :],
                             s["x_dram"][:, bass.ds(b * BT, BT), :]).then_inc(x_in[par], 16)
            load(0, 0)
            load(1, 1)
            with sp.Fori(2, B - 1, 2) as i:
                load(i, 0)
                load(i + 1, 1)

        @block.vector
        def _(dve):
            for buf, v in ((top, NEG_INF), (num, 0.0), (den, 0.0)):
                ins = dve.memset(buf[:, :, 0:1], v)
            ins.then_inc(first, 1)

            def norm(b, par):
                dve.wait_ge(x_in[par], loaded(b, par))
                for i in range(BT):
                    ins = dve.bn_stats(stats[:, par, i], x_res[:, b * BT + i, :])
                ins.then_inc(stats_ready, 1)
                dve.wait_ge(stats_ready, b + 1)
                after(dve, rstd_ready, b - 1)
                dve.sem_inc(waited, 1)
                for i in range(BT):
                    ins = dve.bn_aggr(mv[:, par, i], stats[:, par, i])
                ins.then_inc(mv_ready, 1)

            def normed(b, par):
                dve.wait_ge(rstd_ready, b + 1)
                after(dve, xn_turned, b - 1)
                for i in range(BT):
                    ins = dve.tensor_scalar(xn[:, par, i], x_res[:, b * BT + i, :], mv[:, par, i, 0:1],
                                            rstd[:, par, i:i + 1], ALU.subtract, ALU.mult)
                ins.then_inc(xn_ready, 1)

            def running_max(b, par):
                n = 2 * b
                dve.wait_ge(kr_ready, b + 1)
                for h in range(CC):
                    after(dve, gap_ready, n - 1 + h)
                    dve.tensor_tensor_scan(top[:, h, 1:T + 1], s["w"][:, h:h + 1].to_broadcast([P, T]),
                                           kr[:, par, 0, h], NEG_INF, ALU.add, ALU.max).then_inc(top_ready, 1)
                for h in range(CC):
                    after(dve, lsig_ready, n + h - 1)
                    dve.tensor_scalar(er[:, h], kr[:, par, 1, h], -LIMIT, None, ALU.max).then_inc(er_capped, 1)

            def exponents(b, par):
                n = 2 * b
                for h in range(CC):
                    dve.wait_ge(gap_ready, n + h + 1)
                    after(dve, num_ready, n + h - 3)
                    after(dve, val_ready, n + h - 3)
                    dve.tensor_scalar(down[:, par, h], gap[:, h], s["w"][:, h:h + 1], 0.0,
                                      ALU.subtract, ALU.min).then_inc(down_ready, 1)
                    dve.tensor_scalar(up[:, par, h], gap[:, h], s["w"][:, h:h + 1], 0.0,
                                      ALU.subtract, ALU.max).then_inc(up_ready, 1)
                    dve.tensor_scalar(now[:, par, h], gap[:, h], s["cap"][:, h:h + 1], None,
                                      ALU.min).then_inc(now_capped, 1)

            def sums(b, par):
                n = 2 * b
                for h in range(CC):
                    dve.wait_ge(up_exp, n + h + 1)
                    dve.wait_ge(first, 1)
                    after(dve, bot_ready, n + h - 1)
                    dve.tensor_tensor_scan(den[:, h, 1:T + 1], up[:, par, h], down[:, par, h], 0.0,
                                           ALU.mult, ALU.add).then_inc(den_ready, 1)
                    dve.wait_ge(ev_ready, n + h + 1)
                    after(dve, vsum_ready, n + h - 1)
                    dve.tensor_tensor_scan(num[:, h, 1:T + 1], up[:, par, h], ev[:, par, h], 0.0,
                                           ALU.mult, ALU.add).then_inc(num_ready, 1)
                    dve.wait_ge(den_ready, n + h + 1)
                    dve.wait_ge(now_ready, n + h + 1)
                    after(dve, oT_ready, n + h - 1)
                    dve.tensor_tensor(bot[:, h], now[:, par, h], den[:, h, 0:T], ALU.add).then_inc(bot_ready, 1)
                for h in range(CC):
                    dve.wait_ge(val_ready, n + h + 1)
                    dve.wait_ge(num_ready, n + h + 1)
                    dve.tensor_tensor(val[:, h], val[:, h], num[:, h, 0:T], ALU.add).then_inc(vsum_ready, 1)

            def residual(b):
                for j in range(2):
                    dve.wait_ge(out_done, 2 * b + j + 1)
                    rows = x_res[:, bass.ds(b * BT + 2 * j, 2), :]
                    dve.tensor_tensor(rows, ps[:, 6 + j, :].rearrange("p (a c) -> p a c", a=2), rows,
                                      ALU.add).then_inc(res_done, 1)

            def step(b, par):
                if has(b + 2):
                    norm(b + 2, par)
                if has(b - 1):
                    residual(b - 1)
                if has(b + 2):
                    normed(b + 2, par)
                if has(b + 1):
                    running_max(b + 1, 1 - par)
                if has(b):
                    sums(b, par)
                if has(b + 1):
                    exponents(b + 1, 1 - par)
            pipeline(dve, step)

        @block.gpsimd
        def _(pool):
            def gaps(b, par):
                n = 2 * b
                for h in range(CC):
                    pool.wait_ge(top_ready, n + h + 1)
                    after(pool, now_capped, n + h - 1)
                    pool.tensor_tensor(gap[:, h], kr[:, par, 0, h], top[:, h, 0:T],
                                       ALU.subtract).then_inc(gap_ready, 1)

            def values(b, par):
                n = 2 * b
                for h in range(CC):
                    pool.wait_ge(down_exp, n + h + 1)
                    after(pool, num_ready, n + h - 3)
                    pool.tensor_tensor(ev[:, par, h], down[:, par, h], kr[:, par, 1, h],
                                       ALU.mult).then_inc(ev_ready, 1)

            def value_now(b, par):
                n = 2 * b
                for h in range(CC):
                    pool.wait_ge(now_ready, n + h + 1)
                    after(pool, oT_ready, n + h - 1)
                    pool.tensor_tensor(val[:, h], now[:, par, h], kr[:, par, 1, h], ALU.mult).then_inc(val_ready, 1)

            def quotient(b, par):
                n = 2 * b
                for h in range(CC):
                    pool.wait_ge(lbot_ready, n + h + 1)
                    pool.wait_ge(lsig_ready, n + h + 1)
                    pool.tensor_tensor(bot[:, h], bot[:, h], lsig[:, par, h], ALU.add).then_inc(lsum_ready, 1)
                for h in range(CC):
                    pool.wait_ge(rec_ready, n + h + 1)
                    pool.wait_ge(vsum_ready, n + h + 1)
                    after(pool, out_done, 2 * b - 2)
                    pool.tensor_tensor(oT[:, par, h], val[:, h], bot[:, h], ALU.mult).then_inc(oT_ready, 1)

            def step(b, par):
                if has(b):
                    value_now(b, par)
                if has(b + 1):
                    gaps(b + 1, 1 - par)
                if has(b):
                    quotient(b, par)
                if has(b + 1):
                    values(b + 1, 1 - par)
            pipeline(pool, step)

        @block.scalar
        def _(act):
            def root(b, par):
                act.wait_ge(mv_ready, b + 1)
                after(act, xn_ready, b - 1)
                act.activation(lnv[:, par], mv[:, par, :, 1], ACT.Ln, bias=s["eps"][:, 0:1]).then_inc(lnv_ready, 1)
                act.wait_ge(lnv_ready, b + 1)
                act.activation(rstd[:, par], lnv[:, par], ACT.Exp, scale=-0.5).then_inc(rstd_ready, 1)

            def evacuate_xnT(b):
                act.wait_ge(xn_turned, b + 1)
                after(act, kr_done, b)
                act.copy(xnT[:], ps[:, 0:CC, :]).then_inc(xnT_ready, 1)

            def evacuate_kr(b, par):
                act.wait_ge(kr_done, b + 1)
                after(act, val_ready, 2 * b - 2)
                act.copy(kr[:, par].rearrange("p a h t -> p (a h) t"), ps[:, 2:6, :]).then_inc(kr_ready, 1)

            def sigmoid_log(b, par):
                n = 2 * b
                for h in range(CC):
                    act.wait_ge(er_capped, n + h + 1)
                    act.activation(er[:, h], er[:, h], ACT.Exp, scale=-1.0).then_inc(er_ready, 1)
                for h in range(CC):
                    act.wait_ge(er_ready, n + h + 1)
                    after(act, lsum_ready, n + h - 3)
                    act.activation(lsig[:, par, h], er[:, h], ACT.Ln, bias=1.0).then_inc(lsig_ready, 1)

            def exponentials(b, par):
                n = 2 * b
                for h in range(CC):
                    act.wait_ge(down_ready, n + h + 1)
                    act.activation(down[:, par, h], down[:, par, h], ACT.Exp).then_inc(down_exp, 1)
                    act.wait_ge(up_ready, n + h + 1)
                    act.activation(up[:, par, h], up[:, par, h], ACT.Exp, scale=-1.0).then_inc(up_exp, 1)
                    act.wait_ge(now_capped, n + h + 1)
                    act.activation(now[:, par, h], now[:, par, h], ACT.Exp,
                                   bias=s["u"][:, h:h + 1]).then_inc(now_ready, 1)

            def bottom_log(b):
                for h in range(CC):
                    act.wait_ge(bot_ready, 2 * b + h + 1)
                    act.activation(bot[:, h], bot[:, h], ACT.Ln).then_inc(lbot_ready, 1)

            def reciprocal(b):
                for h in range(CC):
                    act.wait_ge(lsum_ready, 2 * b + h + 1)
                    act.activation(bot[:, h], bot[:, h], ACT.Exp, scale=-1.0).then_inc(rec_ready, 1)

            def step(b, par):
                if has(b + 2):
                    root(b + 2, par)
                    evacuate_xnT(b + 2)
                if has(b + 1):
                    sigmoid_log(b + 1, 1 - par)
                if has(b):
                    bottom_log(b)
                if has(b):
                    reciprocal(b)
                if has(b + 1):
                    exponentials(b + 1, 1 - par)
                if has(b + 2):
                    evacuate_kr(b + 2, par)
            act.preload_act_table_set("natural_log_exp_and_others")
            pipeline(act, step)

        @block.tensor
        def _(pe):
            def turn(b, par):
                pe.wait_ge(xn_ready, b + 1)
                after(pe, xnT_ready, b)
                for cc in range(CC):
                    for i in range(BT):
                        m = pe.transpose(ps[:, cc, i * P:(i + 1) * P], xn[:, par, i, cc * P:(cc + 1) * P],
                                         ident[:])
                m.then_inc(xn_turned, 1)

            def project(b):
                pe.wait_ge(xnT_ready, b + 1)
                after(pe, kr_ready, b)
                for a, w in ((0, wkT), (1, wrT)):
                    for h in range(CC):
                        for cc in range(CC):
                            m = pe.matmul(ps[:, 2 + 2 * a + h, :], w[:, cc, h * P:(h + 1) * P], xnT[:, cc],
                                          start=(cc == 0), stop=(cc == CC - 1))
                m.then_inc(kr_done, 1)

            def out(b, par):
                pe.wait_ge(oT_ready, 2 * b + 2)
                for i in range(BT):
                    if i % 2 == 0:
                        after(pe, res_done, 2 * b - 1 + i // 2)
                    for h in range(CC):
                        m = pe.matmul(ps[:, 6 + i // 2, (i % 2) * C:(i % 2 + 1) * C],
                                      oT[:, par, h, i * P:(i + 1) * P], woT[:, h, :],
                                      start=(h == 0), stop=(h == CC - 1))
                    if i % 2:
                        m.then_inc(out_done, 1)

            def step(b, par):
                if has(b + 2):
                    turn(b + 2, par)
                    project(b + 2)
                if has(b):
                    out(b, par)
            pipeline(pe, step)


def attend_setup(nc, d, s):
    ps, ident = s["ps"], s["ident"]
    with ExitStack() as ctx:
        def sem(name):
            return ctx.enter_context(nc.semaphore(name))

        ctx_in = ctx.enter_context(nc.sbuf_tensor("ctx_in", [P, B * KV // P, CD], F32))
        ctxT = ctx.enter_context(nc.sbuf_tensor("ctxT", [P, B, 2, KV], F32))
        wk = ctx.enter_context(nc.sbuf_tensor("x_wk", [P, C], F32))
        wv = ctx.enter_context(nc.sbuf_tensor("x_wv", [P, C], F32))
        bk = ctx.enter_context(nc.sbuf_tensor("x_bk", [GR, 3], F32))
        bv = ctx.enter_context(nc.sbuf_tensor("x_bv", [P, C], F32))
        wq = ctx.enter_context(nc.sbuf_tensor("x_wq", [P, CC, C], F32))
        kT = ctx.enter_context(nc.sbuf_tensor("x_kT", [GR, 3, B * KV], F32))
        rows_of = ctx.enter_context(nc.sbuf_tensor("x_rows_of_heads", [GK, 3, GH, KV], F32))
        loads = sem("x_loads")
        high_ready = sem("x_high_ready")
        zeroed = sem("x_zeroed")
        shaped = sem("x_shaped")
        ctx_turned = sem("x_ctx_turned")
        ctxT_ready = sem("x_ctxT_ready")
        k_done = sem("x_k_done")
        v_done = sem("x_v_done")
        kT_ready = sem("x_kT_ready")
        v_ready = sem("x_v_ready")
        n_loads = 11
        block = ctx.enter_context(nc.Block())

        @block.sync
        def _(sp):
            sp.dma_start(ctx_in[:], d["ctx"].rearrange("(a e) k c -> (e k) a c", e=2)).then_inc(loads, 16)
            sp.dma_start(wk[:], d["Wk"]).then_inc(loads, 16)
            sp.dma_start(wv[:], d["Wv"]).then_inc(loads, 16)
            sp.dma_start(wq[:], d["Wq"].rearrange("(a p) n -> p a n", p=P)).then_inc(loads, 16)
            sp.dma_start(s["wo"][:], d["Wo"].rearrange("(a p) n -> p a n", p=P)).then_inc(loads, 16)
            for row, dst in (("bv", bv), ("bo", s["bo"])):
                sp.dma_start(dst[:], d[row].partition_broadcast(P)).then_inc(loads, 16)
            with nc.allow_non_contiguous_dma(reason="one value per channel, once"):
                for row, dst in (("bq", s["bq"]), ("bk", bk)):
                    sp.dma_start(dst[:, 0:2], d[row][0:2 * GR].rearrange("(g p) -> p g", p=GR)).then_inc(loads, 16)
                    sp.dma_start(dst[0:C - 2 * GR, 2:3],
                                 d[row][2 * GR:C].rearrange("(g p) -> p g", g=1)).then_inc(loads, 16)

            sp.wait_ge(loads, 16 * n_loads)

        @block.gpsimd
        def _(pool):
            pool.memset(s["headmask"][:], 1.0)
            pool.memset(rows_of[:], 0.0)
            pool.memset(s["nm"][:], 0.0).then_inc(zeroed, 1)
            pool.wait_ge(zeroed, 1)
            pool.affine_select(out=s["headmask"][:], in_=s["headmask"][:], compare_op=ALU.is_ge, fill=0.0,
                               base=0, pattern=[[-DK, GH]], channel_multiplier=1).then_inc(shaped, 1)
            pool.wait_ge(shaped, 1)
            pool.affine_select(out=s["headmask"][:], in_=s["headmask"][:], compare_op=ALU.is_ge, fill=0.0,
                               base=DK - 1, pattern=[[DK, GH]], channel_multiplier=-1).then_inc(shaped, 1)
            pool.affine_select(out=rows_of[:], in_=rows_of[:], compare_op=ALU.not_equal,
                               fill=1.0, base=GR, pattern=[[GH, 3], [1, GH], [0, KV]],
                               channel_multiplier=-1).then_inc(shaped, 1)
            pool.wait_ge(shaped, 3)

        @block.tensor
        def _(pe):
            pe.wait_ge(loads, 16 * n_loads)
            for a in range(B * KV // P):
                m = pe.transpose(ps[:, 0, a * P:(a + 1) * P], ctx_in[:, a, :], ident[:])
            m.then_inc(ctx_turned, 1)
            pe.wait_ge(ctxT_ready, 2)
            for g in range(3):
                rows = GROUPS[g] * DK
                m = pe.matmul(ps[0:rows, 1 + g, :], wk[:, g * GR:g * GR + rows], ctxT[:, :, 0, :],
                              start=True, stop=True)
            m.then_inc(k_done, 1)
            for b in range(B):
                m = pe.matmul(ps[:, 4 + b // 2, (b % 2) * C:(b % 2 + 1) * C],
                              ctxT[:, b].rearrange("p a k -> p (a k)"), wv[:], start=True, stop=True)
            m.then_inc(v_done, 1)

        @block.vector
        def _(dve):
            dve.memset(s["vblk"][:], 0.0)
            dve.memset(kT[:], 0.0)
            for name in ("qT_high", "qT_low", "kblk_high", "kblk_low"):
                ins = dve.memset(s[name][:].bitcast(F32), 0.0)
            ins.then_inc(v_ready, 1)
            dve.wait_ge(v_ready, 1)
            dve.memset(s["vblk"][0:KV, :, :, DK:DK + 1], 1.0)
            dve.memset(s["vblk"][KV:P, :, :, VW - 1:VW], 1.0)
            dve.wait_ge(ctx_turned, 1)
            for a in range(2):
                dve.tensor_copy(ctxT[:, :, a, :], ps[:, 0, :].rearrange("p (b k) -> p b k", b=B)).then_inc(ctxT_ready, 1)
            dve.wait_ge(loads, 16 * n_loads)
            dve.wait_ge(k_done, 1)
            for g in range(3):
                rows = GROUPS[g] * DK
                dve.tensor_scalar(kT[0:rows, g], ps[0:rows, 1 + g, :], bk[0:rows, g:g + 1], DK ** -0.5,
                                  ALU.add, ALU.mult).then_inc(kT_ready, 1)
            dve.wait_ge(v_done, 1)
            for b in range(B):
                for e in range(2):
                    rows = slice(e * KV, (e + 1) * KV)
                    made = ps[rows, 4 + b // 2, (b % 2) * C:(b % 2 + 1) * C]
                    dve.tensor_tensor(s["vblk"][rows, b, :, e * (DK + 1):e * (DK + 1) + DK],
                                      made.rearrange("p (j e d) -> p j e d", e=2, d=DK)[:, :, e, :],
                                      bv[rows].rearrange("p (j e d) -> p j e d", e=2, d=DK)[:, :, e, :],
                                      ALU.add).then_inc(v_ready, 1)
            dve.wait_ge(v_ready, 1 + 2 * B)
            dve.wait_ge(kT_ready, 3)
            for n, (whole, name) in enumerate(((kT, "kT"), (wq, "wq"))):
                dve.tensor_copy(s[name + "_high"][:], whole[:]).then_inc(high_ready, 1)
                dve.wait_ge(high_ready, n + 1)
                dve.tensor_tensor(s[name + "_low"][:], whole[:], s[name + "_high"][:].bitcast(F32), ALU.subtract)
            dve.wait_ge(shaped, 3)
            for par in range(2):
                dve.tensor_copy(s["kblk_high"][GR:GK, par], rows_of[GR:GK].rearrange("p g h k -> p g (h k)")
                                ).then_inc(high_ready, 1)
            dve.wait_ge(high_ready, 4)


BACK = ["S0", "S1", "S2", "S3", "S4", "S5", "S6", "S7", "O0", "O1", "A0", "O2", "A1", "R0",
        "O3", "A2", "R1", "A3", "R2", "R3"]
FRONT_AT = {1: "turn", 3: "query", 5: "max0", 7: "max1", 9: "max2", 11: "max3", 14: "turn_max"}


def attend(nc, d, s):
    ps, x_res, ident = s["ps"], s["x_res"], s["ident"]
    qT_high, qT_low, kblk_high, kblk_low = s["qT_high"], s["qT_low"], s["kblk_high"], s["kblk_low"]
    vblk, nm = s["vblk"], s["nm"]
    RING = 5
    with ExitStack() as ctx:
        def sb(name, shape):
            return ctx.enter_context(nc.sbuf_tensor(name, shape, F32))

        def sem(name):
            return ctx.enter_context(nc.semaphore(name))

        stats = sb("a_stats", [P, BT, 6])
        mv = sb("a_mv", [P, BT, 2])
        lnv = sb("a_lnv", [P, BT])
        rstd = sb("a_rstd", [P, BT])
        xn = sb("a_xn", [P, BT, C])
        xnT_high = ctx.enter_context(nc.sbuf_tensor("a_xnT_high", [P, CC, T], F32R))
        xnT_low = ctx.enter_context(nc.sbuf_tensor("a_xnT_low", [P, CC, T], F32R))
        ex = sb("a_ex", [P, 2, PAIRS, T])
        rsum = sb("a_rsum", [P, 2, HEADS])
        at = sb("a_at", [P, 2, C])
        aT = sb("a_aT", [P, 2, CC, P])

        stats_ready = sem("a_stats_ready")
        mv_ready = sem("a_mv_ready")
        waited = sem("a_waited")
        lnv_ready = sem("a_lnv_ready")
        rstd_ready = sem("a_rstd_ready")
        xn_ready = sem("a_xn_ready")
        xn_turned = sem("a_xn_turned")
        xnT_high_ready = sem("a_xnT_high_ready")
        xnT_ready = sem("a_xnT_ready")
        bias_added = sem("a_bias_added")
        q_done = sem("a_q_done")
        q_high_ready = sem("a_q_high_ready")
        q_ready = sem("a_q_ready")
        kblk_ready = sem("a_kblk_ready")
        s1_done = sem("a_s1_done")
        max_ready = sem("a_max_ready")
        max_turned = sem("a_max_turned")
        maxT_ready = sem("a_maxT_ready")
        s2_done = sem("a_s2_done")
        exp_ready = sem("a_exp_ready")
        o_done = sem("a_o_done")
        rsum_ready = sem("a_rsum_ready")
        at_ready = sem("a_at_ready")
        at_turned = sem("a_at_turned")
        aT_ready = sem("a_aT_ready")
        proj_done = sem("a_proj_done")
        res_done = sem("a_res_done")
        block = ctx.enter_context(nc.Block())

        def pipeline(eng, step):
            step(-1, 1, True, False)
            step(0, 0, True, True)
            step(1, 1, True, True)
            with eng.Fori(2, B - 3, 2) as i:
                step(i, 0, True, True)
                step(i + 1, 1, True, True)
            step(B - 2, 0, True, True)
            step(B - 1, 1, False, True)

        @block.vector
        def _(dve):
            def norm(b):
                after(dve, xn_ready, b)
                for i in range(BT):
                    ins = dve.bn_stats(stats[:, i], x_res[:, b * BT + i, :])
                ins.then_inc(stats_ready, 1)
                dve.wait_ge(stats_ready, b + 1)
                dve.sem_inc(waited, 1)
                for i in range(BT):
                    ins = dve.bn_aggr(mv[:, i], stats[:, i])
                ins.then_inc(mv_ready, 1)

            def normed(b):
                dve.wait_ge(rstd_ready, b + 1)
                after(dve, xn_turned, b)
                for i in range(BT):
                    ins = dve.tensor_scalar(xn[:, i], x_res[:, b * BT + i, :], mv[:, i, 0:1],
                                            rstd[:, i:i + 1], ALU.subtract, ALU.mult)
                ins.then_inc(xn_ready, 1)

            def xnT_rest(b):
                dve.wait_ge(xnT_high_ready, b + 1)
                after(dve, q_done, b)
                dve.tensor_tensor(xnT_low[:], ps[:, 0:CC, :], xnT_high[:].bitcast(F32),
                                  ALU.subtract).then_inc(xnT_ready, 1)

            def query_rest(b, par):
                dve.wait_ge(q_high_ready, b + 1)
                after(dve, s2_done, PAIRS * (b - 1))
                for g in range(3):
                    rows = GROUPS[g] * DK
                    ins = dve.scalar_tensor_tensor(out=qT_low[0:rows, par, g], in0=ps[0:rows, 2 + g, :],
                                                   scalar=s["bq"][0:rows, g:g + 1],
                                                   in1=qT_high[0:rows, par, g].bitcast(F32),
                                                   op0=ALU.add, op1=ALU.subtract)
                ins.then_inc(q_ready, 1)

            def maxima(b, i):
                dve.wait_ge(s1_done, BT * b + i + 1)
                if i == 0:
                    after(dve, max_turned, b)
                dve.tensor_reduce(nm[:, i, GR:GR + 2 * GH],
                                  ps[:, 2:4, 0:GN].rearrange("p a (h k) -> p a h k", k=KV), AX.X, ALU.max,
                                  negate=True)
                dve.tensor_reduce(nm[:, i, GR + 2 * GH:GK],
                                  ps[:, 4, 0:GROUPS[2] * KV].rearrange("p (h k) -> p h k", k=KV), AX.X, ALU.max,
                                  negate=True).then_inc(max_ready, 1)

            def weigh(b, i, k):
                n = BT * b + i
                O = ps[:, RING + k % 3, 0:PAIRS * VW].rearrange("p (h w) -> p h w", w=DK + 1)
                dve.wait_ge(o_done, n + 1)
                dve.reciprocal(rsum[:, i % 2, :], O[:, :, DK]).then_inc(rsum_ready, 1)
                dve.wait_ge(rsum_ready, n + 1)
                after(dve, at_turned, n - 1)
                dve.tensor_tensor(at[:, i % 2].rearrange("p (h w) -> p h w", w=DK), O[:, :, 0:DK],
                                  rsum[:, i % 2, :].unsqueeze(2).to_broadcast([P, HEADS, DK]),
                                  ALU.mult).then_inc(at_ready, 1)

            def add(b, i, k):
                dve.wait_ge(proj_done, BT * b + i + 1)
                if i == 0:
                    dve.wait_ge(bias_added, b + 1)
                row = x_res[:, b * BT + i, :]
                dve.tensor_tensor(row, ps[:, RING + k % 3, 0:C], row, ALU.add).then_inc(res_done, 1)

            def step(b, par, front, back):
                for k, name in enumerate(BACK):
                    if back and name[0] == "O":
                        weigh(b, int(name[1]), k)
                    if back and name[0] == "R":
                        add(b, int(name[1]), k)
                    if front and k == 0:
                        norm(b + 1)
                        normed(b + 1)
                    if front and FRONT_AT.get(k) == "turn":
                        xnT_rest(b + 1)
                    if front and FRONT_AT.get(k) == "query":
                        query_rest(b + 1, 1 - par)
                    if front and FRONT_AT.get(k, "").startswith("max"):
                        maxima(b + 1, int(FRONT_AT[k][3]))
            pipeline(dve, step)

        @block.gpsimd
        def _(pool):
            def front(b, par):
                after(pool, s2_done, PAIRS * (b - 1))
                for into, whole in ((kblk_high, "kT_high"), (kblk_low, "kT_low")):
                    for g in range(3):
                        ins = pool.tensor_tensor(
                            into[0:GR, par, g].rearrange("p (h k) -> p h k", k=KV),
                            s[whole][:, g, bass.ds(b * KV, KV)].bitcast(F32).unsqueeze(1)
                            .to_broadcast([GR, GH, KV]),
                            s["headmask"][:].unsqueeze(2).to_broadcast([GR, GH, KV]), ALU.mult)
                ins.then_inc(kblk_ready, 1)
                pool.wait_ge(xn_ready, b + 1)
                for i in range(BT):
                    row = x_res[:, b * BT + i, :]
                    ins = pool.tensor_tensor(row, row, s["bo"][:], ALU.add)
                ins.then_inc(bias_added, 1)

            front(0, 0)
            front(1, 1)
            with pool.Fori(2, B - 1, 2) as i:
                front(i, 0)
                front(i + 1, 1)

        @block.scalar
        def _(act):
            def root(b):
                act.wait_ge(mv_ready, b + 1)
                act.activation(lnv[:], mv[:, :, 1], ACT.Ln, bias=s["eps"][:, 0:1]).then_inc(lnv_ready, 1)
                act.wait_ge(lnv_ready, b + 1)
                act.activation(rstd[:], lnv[:], ACT.Exp, scale=-0.5).then_inc(rstd_ready, 1)

            def turned(b):
                act.wait_ge(xn_turned, b + 1)
                after(act, q_done, b)
                act.copy(xnT_high[:], ps[:, 0:CC, :]).then_inc(xnT_high_ready, 1)

            def query(b, par):
                act.wait_ge(q_done, b + 1)
                after(act, s2_done, PAIRS * (b - 1))
                for g in range(3):
                    rows = GROUPS[g] * DK
                    ins = act.activation(qT_high[0:rows, par, g], ps[0:rows, 2 + g, :], ACT.Identity,
                                         bias=s["bq"][0:rows, g:g + 1])
                ins.then_inc(q_high_ready, 1)

            def max_rows(b, par):
                act.wait_ge(max_turned, b + 1)
                act.copy(qT_high[GR:GK, par], ps[GR:GK, 0:1, :].to_broadcast([HEADS, 3, T])).then_inc(maxT_ready, 1)

            def exps(b, par, j, k):
                act.wait_ge(s2_done, PAIRS * b + j + 1)
                if j == 0:
                    after(act, o_done, BT * (b - 1))
                act.activation(ex[:, par, j], ps[:, RING + k % 3, :], ACT.Exp).then_inc(exp_ready, 1)

            def turn_out(b, i, k):
                n = BT * b + i
                act.wait_ge(at_turned, n + 1)
                after(act, proj_done, n - 1)
                act.copy(aT[:, i % 2].rearrange("p a t -> p (a t)"),
                         ps[:, RING + k % 3, 0:C]).then_inc(aT_ready, 1)

            def step(b, par, front, back):
                for k, name in enumerate(BACK):
                    if front and k == 0:
                        root(b + 1)
                    if back and name[0] == "S":
                        exps(b, par, int(name[1]), k)
                    if back and name[0] == "A":
                        turn_out(b, int(name[1]), k)
                    if front and k in FRONT_AT:
                        if FRONT_AT[k] == "turn":
                            turned(b + 1)
                        if FRONT_AT[k] == "query":
                            query(b + 1, 1 - par)
                        if FRONT_AT[k] == "turn_max":
                            max_rows(b + 1, 1 - par)
            pipeline(act, step)

        @block.tensor
        def _(pe):
            def turn(b, par):
                pe.wait_ge(xn_ready, b + 1)
                after(pe, maxT_ready, b)
                for cc in range(CC):
                    for i in range(BT):
                        m = pe.transpose(ps[:, cc, i * P:(i + 1) * P], xn[:, i, cc * P:(cc + 1) * P], ident[:])
                m.then_inc(xn_turned, 1)

            def query(b, par):
                pe.wait_ge(xnT_ready, b + 1)
                after(pe, max_ready, BT * b)
                for g in range(3):
                    rows = GROUPS[g] * DK
                    for cc in range(CC):
                        for w, x in (("wq_high", xnT_high), ("wq_high", xnT_low), ("wq_low", xnT_high)):
                            m = pe.matmul(ps[0:rows, 2 + g, :], s[w][:, cc, g * GR:g * GR + rows], x[:, cc],
                                          start=(cc == 0 and x is xnT_high and w == "wq_high"),
                                          stop=(cc == CC - 1 and w == "wq_low"))
                m.then_inc(q_done, 1)

            def score(b, par, i):
                if i == 0:
                    pe.wait_ge(q_ready, b + 1)
                    pe.wait_ge(kblk_ready, b + 1)
                else:
                    pe.wait_ge(max_ready, BT * b + i)
                for g in range(3):
                    cols = GROUPS[g] * KV
                    m = pe.matmul(ps[:, 2 + g, 0:cols], qT_high[0:GR, par, g, i * P:(i + 1) * P],
                                  kblk_high[0:GR, par, g, 0:cols], start=True, stop=True)
                m.then_inc(s1_done, 1)

            def turn_max(b, par):
                pe.wait_ge(max_ready, BT * (b + 1))
                for i in range(BT):
                    m = pe.transpose(ps[0:GK, 0, i * P:(i + 1) * P], nm[:, i, :], ident[:])
                m.then_inc(max_turned, 1)

            def free(b, k):
                prev, at = (k - 3, b) if k >= 3 else ((18 if k == 0 else 19 if k == 1 else 17), b - 1)
                kind, i = BACK[prev][0], int(BACK[prev][1])
                read, per = {"S": (exp_ready, PAIRS), "O": (at_ready, BT), "A": (aT_ready, BT),
                             "R": (res_done, BT)}[kind]
                after(pe, read, per * at + i + 1)

            def back(b, par, k):
                kind, i = BACK[k][0], int(BACK[k][1])
                bank = RING + k % 3
                free(b, k)
                if kind == "S":
                    if i == 0:
                        pe.wait_ge(maxT_ready, b + 1)
                    g, o = divmod(i, GH // 2)
                    for k_part, q_part in ((kblk_high, qT_high), (kblk_high, qT_low), (kblk_low, qT_high)):
                        m = pe.matmul(ps[:, bank, :], k_part[:, par, g, o * P:(o + 1) * P], q_part[:, par, g, :],
                                      start=(q_part is qT_high and k_part is kblk_high),
                                      stop=(k_part is kblk_low))
                    m.then_inc(s2_done, 1)
                if kind == "O":
                    if i == 0:
                        pe.wait_ge(exp_ready, PAIRS * (b + 1))
                    for j in range(PAIRS):
                        m = pe.matmul(ps[:, bank, j * VW:(j + 1) * VW], ex[:, par, j, i * P:(i + 1) * P],
                                      vblk[:, b, j, :], start=True, stop=True)
                    m.then_inc(o_done, 1)
                if kind == "A":
                    pe.wait_ge(at_ready, BT * b + i + 1)
                    for cc in range(CC):
                        m = pe.transpose(ps[:, bank, cc * P:(cc + 1) * P], at[:, i % 2, cc * P:(cc + 1) * P],
                                         ident[:])
                    m.then_inc(at_turned, 1)
                if kind == "R":
                    pe.wait_ge(aT_ready, BT * b + i + 1)
                    for cc in range(CC):
                        m = pe.matmul(ps[:, bank, 0:C], aT[:, i % 2, cc, :], s["wo"][:, cc, :],
                                      start=(cc == 0), stop=(cc == CC - 1))
                    m.then_inc(proj_done, 1)

            def step(b, par, front, do_back):
                for k in range(len(BACK)):
                    if do_back:
                        back(b, par, k)
                    if front and k in FRONT_AT:
                        name = FRONT_AT[k]
                        if name == "turn":
                            turn(b + 1, 1 - par)
                        elif name == "query":
                            query(b + 1, 1 - par)
                        elif name == "turn_max":
                            turn_max(b + 1, 1 - par)
                        else:
                            score(b + 1, 1 - par, int(name[3]))
            pipeline(pe, step)


def route_setup(nc, d, s):
    ps, ident = s["ps"], s["ident"]
    with ExitStack() as ctx:
        def sb(name, shape, dt=F32):
            return ctx.enter_context(nc.sbuf_tensor(name, shape, dt))

        def sem(name):
            return ctx.enter_context(nc.semaphore(name))

        phi = sb("phi", [P, ST, C])
        bias = sb("phi_bias", [P, ES // P])
        rest = sb("phi_rest", [P, 2, ES // P])
        parts = sb("phi_parts", [P, 3, ES // P], BF16)
        split = nc.dram_tensor("phi_b_split", [3, ES], BF16).ap()
        phi_in = sem("phi_in")
        bias_in = sem("phi_bias_in")
        parts_ready = sem("phi_parts_ready")
        rest_ready = sem("phi_rest_ready")
        parts_out = sem("phi_parts_out")
        rows_in = sem("phi_rows_in")
        filled = sem("r_filled")
        zeroed = sem("r_zeroed")
        shaped = sem("r_shaped")
        turned = sem("phi_turned")
        high_ready = sem("phi_high_ready")
        copied = sem("phi_copied")
        block = ctx.enter_context(nc.Block())

        @block.sync
        def _(sp):
            sp.dma_start(phi[:], d["phi_w"].rearrange("(a p) c -> p a c", p=P)).then_inc(phi_in, 16)
            sp.dma_start(bias[:], d["phi_b"].rearrange("(p a) -> p a", p=P)).then_inc(bias_in, 16)
            sp.wait_ge(parts_ready, 3)
            with nc.allow_non_contiguous_dma(reason="12 KB, once"):
                sp.dma_start(split.rearrange("j (p a) -> p j a", p=P), parts[:]).then_inc(parts_out, 16)
            sp.wait_ge(parts_out, 16)
            sp.wait_ge(filled, 1)
            for j in range(3):
                sp.dma_start(s["bias_rows"][32 * j:32 * j + 1, :], split[j:j + 1, :]).then_inc(rows_in, 16)
            sp.wait_ge(rows_in, 48)

        @block.vector
        def _(dve):
            dve.memset(s["bias_rows"][:], 0.0)
            dve.memset(s["ones"][:], 1.0)
            dve.memset(s["xacc"][:], 0.0).then_inc(filled, 1)
            dve.tensor_copy(s["identb"][:], ident[:]).then_inc(filled, 1)
            dve.wait_ge(bias_in, 16)
            dve.tensor_copy(parts[:, 0], bias[:]).then_inc(parts_ready, 1)
            dve.wait_ge(parts_ready, 1)
            dve.tensor_tensor(rest[:, 0], bias[:], parts[:, 0], ALU.subtract).then_inc(rest_ready, 1)
            dve.wait_ge(rest_ready, 1)
            dve.tensor_copy(parts[:, 1], rest[:, 0]).then_inc(parts_ready, 1)
            dve.wait_ge(parts_ready, 2)
            dve.tensor_tensor(rest[:, 1], rest[:, 0], parts[:, 1], ALU.subtract).then_inc(rest_ready, 1)
            dve.wait_ge(rest_ready, 2)
            dve.tensor_copy(parts[:, 2], rest[:, 1]).then_inc(parts_ready, 1)
            for n in range(CC * EB):
                dve.wait_ge(turned, n + 1)
                high, low = (s[name][:, n // EB, (n % EB) * BLK:(n % EB + 1) * BLK]
                             for name in ("phiT_high", "phiT_low"))
                dve.tensor_copy(high, ps[:, n % 2, :]).then_inc(high_ready, 1)
                dve.wait_ge(high_ready, n + 1)
                dve.tensor_tensor(low, ps[:, n % 2, :], high.bitcast(F32), ALU.subtract).then_inc(copied, 1)

        @block.gpsimd
        def _(pool):
            pool.memset(s["sel_add"][:], 0.0)
            pool.memset(s["sel_swap"][:], 0.0).then_inc(zeroed, 1)
            pool.wait_ge(zeroed, 1)
            by_expert = dict(compare_op=ALU.not_equal, base=0, pattern=[[1, EXPERTS], [0, SLOTS]],
                             channel_multiplier=-1)
            pool.affine_select(out=s["sel_add"][:], in_=s["sel_add"][:], fill=1.0, **by_expert).then_inc(shaped, 1)
            pool.affine_select(out=s["sel_swap"][:], in_=s["sel_swap"][:], fill=-1.0, **by_expert).then_inc(shaped, 1)
            pool.wait_ge(shaped, 2)
            pool.affine_select(out=s["sel_swap"][:], in_=s["sel_swap"][:], fill=1.0, compare_op=ALU.not_equal,
                               base=EXPERTS, pattern=[[0, EXPERTS], [1, SLOTS]],
                               channel_multiplier=-1).then_inc(shaped, 1)
            pool.wait_ge(shaped, 3)

        @block.tensor
        def _(pe):
            pe.wait_ge(phi_in, 16)
            for n in range(CC * EB):
                if n >= 2:
                    pe.wait_ge(copied, n - 1)
                for i in range(BLK // P):
                    m = pe.transpose(ps[:, n % 2, i * P:(i + 1) * P],
                                     phi[:, (n % EB) * (BLK // P) + i, (n // EB) * P:(n // EB + 1) * P], ident[:])
                m.then_inc(turned, 1)


def route(nc, d, s):
    ps, x_res, ident = s["ps"], s["x_res"], s["ident"]
    xacc = s["xacc"]
    SMALL, TURN, DISP = 4, 5, 6
    NM = EXPERTS + SLOTS
    UNITS = CC * EB
    with ExitStack() as ctx:
        def sb(name, shape, dt=F32):
            return ctx.enter_context(nc.sbuf_tensor(name, shape, dt))

        def sem(name):
            return ctx.enter_context(nc.semaphore(name))

        stats = sb("r_stats", [P, 6])
        mv = sb("r_mv", [P, 2])
        lnv = sb("r_lnv", [P, 1])
        rstd = sb("r_rstd", [P, 1])
        xn = sb("r_xn", [P, 2, C])
        xh = sb("r_xh", [P, 4, C])
        xhT_high = sb("r_xhT_high", [P, 2, CC, P], F32R)
        xhT_low = sb("r_xhT_low", [P, 2, CC, P], F32R)
        nab = sb("r_nab", [P, 2, NM], BF16)
        half_b = sb("r_half_b", [P, 2, SLOTS])
        nabT = sb("r_nabT", [NM, P], BF16)
        disp = sb("r_disp", [P, 4, ES])
        comb = sb("r_comb", [P, 2, ES])
        combT = sb("r_combT", [P, 2, ST, P])
        sum_d = sb("r_sum_d", [P, EXPERTS])
        sum_c = sb("r_sum_c", [P, SLOTS])
        rec_d = sb("r_rec_d", [P, 2, EXPERTS])
        rec_c = sb("r_rec_c", [P, 2, SLOTS])
        turned_max = ps[0:NM, SMALL, 0:P // 2].bitcast(BF16)

        stats_ready = sem("r_stats_ready")
        waited = sem("r_waited")
        copy_waited = sem("r_copy_waited")
        mv_ready = sem("r_mv_ready")
        lnv_ready = sem("r_lnv_ready")
        rstd_ready = sem("r_rstd_ready")
        xn_ready = sem("r_xn_ready")
        xh_ready = sem("r_xh_ready")
        xn_turned = sem("r_xn_turned")
        xhT_high_ready = sem("r_xhT_high_ready")
        xhT_ready = sem("r_xhT_ready")
        logits_done = sem("r_logits_done")
        half_ready = sem("r_half_ready")
        max_ready = sem("r_max_ready")
        max_turned = sem("r_max_turned")
        maxT_ready = sem("r_maxT_ready")
        less_a = sem("r_less_expert_max")
        less_b = sem("r_less_slot_max")
        exp_d = sem("r_exp_d")
        exp_c = sem("r_exp_c")
        sum_d_ready = sem("r_sum_d_ready")
        sum_c_ready = sem("r_sum_c_ready")
        rec_d_ready = sem("r_rec_d_ready")
        rec_c_ready = sem("r_rec_c_ready")
        disp_ready = sem("r_disp_ready")
        comb_ready = sem("r_comb_ready")
        comb_turned = sem("r_comb_turned")
        combT_ready = sem("r_combT_ready")
        combT_out = [sem(f"r_combT_out{i}") for i in range(2)]
        unit_done = sem("r_unit_done")
        unit_added = sem("r_unit_added")
        block = ctx.enter_context(nc.Block())

        def pipeline(eng, step):
            for t in range(4):
                step(t, t)
            with eng.Fori(4, NT - 7, 4) as i:
                for r in range(4):
                    step(i + r, r)
            for t in range(NT - 4, NT + 2):
                step(t, t % 4)

        def known(t):
            return isinstance(t, int)

        def has_tile(t):
            return not known(t) or 0 <= t < NT

        def pair_units(t, r):
            return 4 * (t - r) + UNITS

        @block.sync
        def _(sp):
            def step(t, r):
                if has_tile(t - 1):
                    par = (r + 1) % 2
                    sp.wait_ge(combT_ready, EB * t)
                    sp.dma_start(s["combT_dram"][bass.ds(t - 1, 1)].rearrange("t p n -> p (t n)"),
                                 combT[:, par].rearrange("p a t -> p (a t)")).then_inc(combT_out[par], 16)
            for n in range(RING):
                load_experts(sp, s, n)
            pipeline(sp, step)
            for par in range(2):
                sp.wait_ge(combT_out[par], 16 * NT // 2)

        @block.vector
        def _(dve):
            def norm(t, r):
                dve.bn_stats(stats[:], x_res[:, bass.ds(t, 1), :].rearrange("p a c -> p (a c)")
                             if not known(t) else x_res[:, t, :]).then_inc(stats_ready, 1)
                dve.wait_ge(stats_ready, t + 1)
                dve.sem_inc(waited, 1)
                dve.bn_aggr(mv[:], stats[:]).then_inc(mv_ready, 1)

            def normed(t, r):
                dve.wait_ge(rstd_ready, t + 1)
                after(dve, xn_turned, t - 1)
                after(dve, xh_ready, t - 1)
                dve.tensor_scalar(xn[:, r % 2], x_res[:, t, :], mv[:, 0:1], rstd[:, 0:1],
                                  ALU.subtract, ALU.mult).then_inc(xn_ready, 1)

            def maxima(t, r):
                after(dve, max_turned, t - 1)
                for h in range(2):
                    for b in (2 * h, 2 * h + 1):
                        dve.wait_ge(logits_done, EB * t + b + 1)
                        dve.tensor_reduce(nab[:, r % 2, b * EXPERTS // EB:(b + 1) * EXPERTS // EB],
                                          ps[:, b, :].rearrange("p (n q) -> p n q", q=SLOTS), AX.X, ALU.max,
                                          negate=True)
                    dve.tensor_reduce(half_b[:, h], ps[:, 2 * h:2 * h + 2, :].rearrange("p b (n q) -> p q (b n)", q=SLOTS), AX.X,
                                      ALU.max, negate=True).then_inc(half_ready, 1)
                dve.wait_ge(half_ready, 2 * t + 2)
                dve.tensor_tensor(nab[:, r % 2, EXPERTS:NM], half_b[:, 0], half_b[:, 1],
                                  ALU.min).then_inc(max_ready, 1)

            def xhT_rest(t, r):
                dve.wait_ge(xhT_high_ready, t + 1)
                after(dve, logits_done, EB * (t - 1))
                dve.tensor_tensor(xhT_low[:, r % 2].rearrange("p a t -> p (a t)"), ps[:, SMALL, 0:C],
                                  xhT_high[:, r % 2].rearrange("p a t -> p (a t)").bitcast(F32),
                                  ALU.subtract).then_inc(xhT_ready, 1)

            def sums_d(t, r):
                dve.wait_ge(exp_d, 2 * t + 2)
                dve.tensor_reduce(sum_d[:], disp[:, r].rearrange("p (n q) -> p n q", q=SLOTS), AX.X,
                                  ALU.add).then_inc(sum_d_ready, 1)
                dve.wait_ge(sum_d_ready, t + 1)
                after(dve, disp_ready, t - 1)
                dve.reciprocal(rec_d[:, r % 2], sum_d[:]).then_inc(rec_d_ready, 1)

            def sums_c(t, r):
                dve.wait_ge(exp_c, 2 * t + 2)
                dve.tensor_reduce(sum_c[:], comb[:, r % 2].rearrange("p (n q) -> p q n", q=SLOTS), AX.X,
                                  ALU.add).then_inc(sum_c_ready, 1)
                dve.wait_ge(sum_c_ready, t + 1)
                after(dve, comb_ready, t - 1)
                dve.reciprocal(rec_c[:, r % 2], sum_c[:]).then_inc(rec_c_ready, 1)

            def unit(t, r, n):
                u = (r % 2) * 4 + n
                done = pair_units(t - 2, r % 2) - UNITS + u + 1
                dve.wait_ge(unit_done, done)
                part = xacc[:, u // EB, (u % EB) * BLK:(u % EB + 1) * BLK]
                dve.tensor_tensor(part, ps[:, DISP + u % 2, :], part, ALU.add).then_inc(unit_added, 1)

            def step(t, r):
                units = not known(t) or t >= 2
                if known(t) and t == 0:
                    norm(0, 0)
                    normed(0, 0)
                    xhT_rest(0, 0)
                if has_tile(t):
                    maxima(t, r)
                if units:
                    unit(t, r, 0)
                if has_tile(t + 1):
                    norm(t + 1, (r + 1) % 4)
                    normed(t + 1, (r + 1) % 4)
                if units:
                    unit(t, r, 1)
                if has_tile(t):
                    sums_d(t, r)
                if units:
                    unit(t, r, 2)
                if has_tile(t + 1):
                    xhT_rest(t + 1, (r + 1) % 4)
                if has_tile(t):
                    sums_c(t, r)
                if units:
                    unit(t, r, 3)
            pipeline(dve, step)

        @block.gpsimd
        def _(pool):
            def step(t, r):
                if known(t) and t == 0:
                    pool.wait_ge(xn_ready, 1)
                    pool.tensor_copy(xh[:, 0], xn[:, 0]).then_inc(xh_ready, 1)
                if has_tile(t):
                    pool.wait_ge(rec_d_ready, t + 1)
                    pool.tensor_tensor(disp[:, r].rearrange("p (n q) -> p n q", q=SLOTS),
                                       disp[:, r].rearrange("p (n q) -> p n q", q=SLOTS),
                                       rec_d[:, r % 2].unsqueeze(2).to_broadcast([P, EXPERTS, SLOTS]),
                                       ALU.mult).then_inc(disp_ready, 1)
                    pool.wait_ge(rec_c_ready, t + 1)
                    pool.tensor_tensor(comb[:, r % 2].rearrange("p (n q) -> p n q", q=SLOTS),
                                       comb[:, r % 2].rearrange("p (n q) -> p n q", q=SLOTS),
                                       rec_c[:, r % 2].unsqueeze(1).to_broadcast([P, EXPERTS, SLOTS]),
                                       ALU.mult).then_inc(comb_ready, 1)
                if has_tile(t + 1):
                    q = (r + 1) % 4
                    pool.wait_ge(xn_ready, t + 2)
                    after(pool, unit_done, pair_units(t - 3, (r + 1) % 2))
                    pool.sem_inc(copy_waited, 1)
                    pool.tensor_copy(xh[:, q], xn[:, q % 2]).then_inc(xh_ready, 1)
            pipeline(pool, step)

        @block.scalar
        def _(act):
            def root(t):
                act.wait_ge(mv_ready, t + 1)
                act.activation(lnv[:], mv[:, 1:2], ACT.Ln, bias=s["eps"][:, 0:1]).then_inc(lnv_ready, 1)
                act.wait_ge(lnv_ready, t + 1)
                act.activation(rstd[:], lnv[:], ACT.Exp, scale=-0.5).then_inc(rstd_ready, 1)

            def xhT_copy(t, r):
                act.wait_ge(xn_turned, t + 1)
                after(act, logits_done, EB * (t - 1))
                act.copy(xhT_high[:, r % 2].rearrange("p a t -> p (a t)"),
                         ps[:, SMALL, 0:C]).then_inc(xhT_high_ready, 1)

            def combT_copy(t, r, n):
                act.wait_ge(comb_turned, EB * t + n + 1)
                if n == 0:
                    after(act, combT_out[r % 2], 8 * (t - r % 2))
                act.copy(combT[:, r % 2, 4 * n:4 * n + 4].rearrange("p a t -> p (a t)"),
                         ps[:, TURN, :]).then_inc(combT_ready, 1)

            def exps(t, r, into, less, done):
                for h in range(2):
                    act.wait_ge(less, 2 * t + h + 1)
                    act.activation(into[:, h * 2 * BLK:(h + 1) * 2 * BLK],
                                   ps[:, 2 * h:2 * h + 2, :].rearrange("p b n -> p (b n)"),
                                   ACT.Exp).then_inc(done, 1)

            def step(t, r):
                q = (r - 1) % 4
                if known(t) and t == 0:
                    root(0)
                    xhT_copy(0, 0)
                if has_tile(t - 1):
                    combT_copy(t - 1, q, 0)
                if has_tile(t):
                    act.wait_ge(max_turned, t + 1)
                    after(act, less_b, 2 * t)
                    act.copy(nabT[:], turned_max).then_inc(maxT_ready, 1)
                if has_tile(t + 1):
                    root(t + 1)
                if has_tile(t):
                    after(act, unit_done, pair_units(t - 4, r % 2))
                    exps(t, r, disp[:, r], less_a, exp_d)
                if has_tile(t - 1):
                    combT_copy(t - 1, q, 1)
                if has_tile(t):
                    after(act, comb_turned, EB * (t - 1))
                    exps(t, r, comb[:, r % 2], less_b, exp_c)
                if has_tile(t + 1):
                    xhT_copy(t + 1, (r + 1) % 4)
                if has_tile(t - 1):
                    combT_copy(t - 1, q, 2)
                    combT_copy(t - 1, q, 3)
            act.preload_act_table_set("natural_log_exp_and_others")
            pipeline(act, step)

        @block.tensor
        def _(pe):
            def turn_xn(t, r):
                pe.wait_ge(xn_ready, t + 1)
                after(pe, maxT_ready, t)
                for cc in range(CC):
                    m = pe.transpose(ps[:, SMALL, cc * P:(cc + 1) * P], xn[:, r % 2, cc * P:(cc + 1) * P],
                                     ident[:])
                m.then_inc(xn_turned, 1)

            def logits(t, r):
                pe.wait_ge(xhT_ready, t + 1)
                for b in range(EB):
                    if b % 2 == 0:
                        after(pe, exp_c, 2 * t - 1 + b // 2)
                    cols = slice(b * BLK, (b + 1) * BLK)
                    pe.matmul(ps[:, b, :], s["ones"][:], s["bias_rows"][:, cols], start=True, stop=False)
                    for cc in range(CC):
                        for x, w in ((xhT_high, "phiT_high"), (xhT_high, "phiT_low"), (xhT_low, "phiT_high")):
                            m = pe.matmul(ps[:, b, :], x[:, r % 2, cc], s[w][:, cc, cols], start=False,
                                          stop=(cc == CC - 1 and x is xhT_low))
                    m.then_inc(logits_done, 1)

            def turn_max(t, r):
                pe.wait_ge(max_ready, t + 1)
                pe.wait_ge(xhT_ready, t + 1)
                pe.transpose(turned_max, nab[:, r % 2, :], s["identb"][:]).then_inc(max_turned, 1)

            def shift(t, r, rows, selector, done, before=None):
                for b in range(EB):
                    if before is not None and b % 2 == 0:
                        pe.wait_ge(before, 2 * t + b // 2 + 1)
                    m = pe.matmul(ps[:, b, :], nabT[0:rows], selector[0:rows, b * BLK:(b + 1) * BLK],
                                  start=False, stop=True, skip_group_check=True)
                    if b % 2:
                        m.then_inc(done, 1)

            def unit(t, r, n):
                u = (r % 2) * 4 + n
                q = (r - 2 - r % 2) % 4
                if n == 0 and r % 2 == 0:
                    pe.wait_ge(disp_ready, t)
                    pe.wait_ge(xh_ready, t)
                after(pe, unit_added, pair_units(t - 2, r % 2) - UNITS + u - 1)
                for k in range(2):
                    m = pe.matmul(ps[:, DISP + u % 2, :], xh[:, q + k, (u // EB) * P:(u // EB + 1) * P],
                                  disp[:, q + k, (u % EB) * BLK:(u % EB + 1) * BLK],
                                  start=(k == 0), stop=(k == 1))
                m.then_inc(unit_done, 1)

            def turn_comb(t, r, n):
                if n == 0:
                    pe.wait_ge(comb_ready, t + 1)
                after(pe, combT_ready, EB * t + n)
                for i in range(BLK // P):
                    m = pe.transpose(ps[:, TURN, i * P:(i + 1) * P],
                                     comb[:, r % 2, n * BLK + i * P:n * BLK + (i + 1) * P], ident[:])
                m.then_inc(comb_turned, 1)

            def step(t, r):
                def dispatch(n):
                    if not known(t) or t >= 2:
                        unit(t, r, n)

                def turn(n):
                    if has_tile(t - 1):
                        turn_comb(t - 1, (r - 1) % 4, n)
                if known(t) and t == 0:
                    turn_xn(0, 0)
                if has_tile(t):
                    logits(t, r)
                dispatch(0)
                turn(0)
                if has_tile(t):
                    turn_max(t, r)
                dispatch(1)
                if has_tile(t):
                    pe.wait_ge(maxT_ready, t + 1)
                    shift(t, r, EXPERTS, s["sel_add"], less_a)
                turn(1)
                dispatch(2)
                if has_tile(t):
                    shift(t, r, NM, s["sel_swap"], less_b, exp_d)
                if has_tile(t + 1):
                    turn_xn(t + 1, (r + 1) % 4)
                turn(2)
                dispatch(3)
                turn(3)
            pipeline(pe, step)


RING = 3


def load_experts(eng, s, n):
    eng.dma_start(s["ew"][:, n % RING].rearrange("p e a h -> p (e a) h"),
                  s["expert_w"][n].rearrange("p e a h -> p (e a) h")).then_inc(s["w_in"][n % RING], 16)


def experts(nc, d, s):
    ps, ident, xacc, xt, yt = s["ps"], s["ident"], s["xacc"], s["xt"], s["yt"]
    ew, w_in = s["ew"], s["w_in"]
    with ExitStack() as ctx:
        def sb(name, shape):
            return ctx.enter_context(nc.sbuf_tensor(name, shape, F32))

        def sem(name):
            return ctx.enter_context(nc.semaphore(name))

        stats = sb("e_stats", [P, ST, 6])
        mv = sb("e_mv", [P, ST, 2])
        lnv = sb("e_lnv", [P, ST])
        rstd = sb("e_rstd", [P, ST])
        shift = sb("e_shift", [P, ST])
        eb = sb("e_bias", [P, ST, C])
        b_in = sem("e_b_in")
        x_turned = sem("e_x_turned")
        xt_ready = sem("e_xt_ready")
        stats_ready = sem("e_stats_ready")
        mv_ready = sem("e_mv_ready")
        lnv_ready = sem("e_lnv_ready")
        rstd_ready = sem("e_rstd_ready")
        shift_ready = sem("e_shift_ready")
        tanh_ready = sem("e_tanh_ready")
        t_turned = sem("e_t_turned")
        thT_ready = sem("e_thT_ready")
        y_done = sem("e_y_done")
        y_ready = sem("e_y_ready")
        block = ctx.enter_context(nc.Block())

        @block.sync
        def _(sp):
            for n in range(ST):
                if n >= RING:
                    sp.wait_ge(y_done, n - RING + 1)
                    load_experts(sp, s, n)
                if n == 0:
                    for e in range(EPT):
                        sp.dma_start(eb[e * SLOTS:(e + 1) * SLOTS],
                                     d["expert_b"].rearrange("(s e) h -> e s h", e=EPT)[e]
                                     .partition_broadcast(SLOTS)).then_inc(b_in, 16)

        @block.tensor
        def _(pe):
            for n in range(ST):
                if n >= 2:
                    pe.wait_ge(xt_ready, n - 1)
                for cc in range(CC):
                    m = pe.transpose(ps[:, n % 2, cc * P:(cc + 1) * P], xacc[:, cc, n * P:(n + 1) * P], ident[:])
                m.then_inc(x_turned, 1)
            for n in range(ST):
                pe.wait_ge(tanh_ready, n + 1)
                if n >= 2:
                    pe.wait_ge(thT_ready, n - 1)
                for cc in range(CC):
                    m = pe.transpose(ps[:, 2 + n % 2, cc * P:(cc + 1) * P], xt[:, n, cc * P:(cc + 1) * P], ident[:])
                m.then_inc(t_turned, 1)
            for n in range(ST):
                pe.wait_ge(w_in[n % RING], 16 * (n // RING + 1))
                pe.wait_ge(thT_ready, n + 1)
                if n >= 2:
                    pe.wait_ge(y_ready, n - 1)
                for e in range(EPT):
                    rows = slice(e * SLOTS, (e + 1) * SLOTS)
                    for cc in range(CC):
                        m = pe.matmul(ps[rows, 4 + n % 2, 0:C], xacc[:, cc, n * P + e * SLOTS:n * P + (e + 1) * SLOTS],
                                      ew[:, n % RING, e, cc, :], start=(cc == 0), stop=(cc == CC - 1),
                                      tile_position=(0, e * SLOTS))
                m.then_inc(y_done, 1)

        @block.vector
        def _(dve):
            for n in range(ST):
                dve.wait_ge(x_turned, n + 1)
                dve.tensor_scalar(xt[:, n], ps[:, n % 2, 0:C], -33000.0, 65000.0, ALU.max, ALU.min).then_inc(xt_ready, 1)
            for n in range(ST):
                dve.wait_ge(xt_ready, n + 1)
                dve.bn_stats(stats[:, n], xt[:, n]).then_inc(stats_ready, 1)
            for n in range(ST):
                dve.wait_ge(stats_ready, n + 1)
                dve.bn_aggr(mv[:, n], stats[:, n]).then_inc(mv_ready, 1)
            dve.wait_ge(rstd_ready, 1)
            dve.wait_ge(mv_ready, ST)
            dve.scalar_tensor_tensor(out=shift[:], in0=mv[:, :, 0], scalar=-1.0, in1=rstd[:], op0=ALU.mult,
                                     op1=ALU.mult).then_inc(shift_ready, 1)
            for n in range(ST):
                dve.wait_ge(t_turned, n + 1)
                if n == 0:
                    dve.wait_ge(x_turned, ST)
                dve.tensor_copy(xacc[:, :, n * P:(n + 1) * P],
                                ps[:, 2 + n % 2, 0:C].rearrange("p (a t) -> p a t", a=CC)).then_inc(thT_ready, 1)
            dve.wait_ge(b_in, 16 * EPT)
            for n in range(ST):
                dve.wait_ge(y_done, n + 1)
                dve.tensor_tensor(yt[:, n], ps[:, 4 + n % 2, 0:C], eb[:, n], ALU.add).then_inc(y_ready, 1)

        @block.scalar
        def _(act):
            act.wait_ge(mv_ready, ST)
            act.activation(lnv[:], mv[:, :, 1], ACT.Ln, bias=s["eps"][:, 0:1]).then_inc(lnv_ready, 1)
            act.wait_ge(lnv_ready, 1)
            act.activation(rstd[:], lnv[:], ACT.Exp, scale=-0.5).then_inc(rstd_ready, 1)
            act.wait_ge(shift_ready, 1)
            act.wait_ge(rstd_ready, 1)
            for n in range(ST):
                act.activation(xt[:, n], xt[:, n], ACT.Tanh, bias=shift[:, n:n + 1],
                               scale=rstd[:, n:n + 1]).then_inc(tanh_ready, 1)


def combine(nc, d, s):
    ps, x_res, yt = s["ps"], s["x_res"], s["yt"]
    RING = 4
    with ExitStack() as ctx:
        def sem(name):
            return ctx.enter_context(nc.semaphore(name))

        ct = ctx.enter_context(nc.sbuf_tensor("c_combT", [P, RING, ST * P], F32))
        ct_in = [sem(f"c_in{i}") for i in range(RING)]
        y_done = sem("c_y_done")
        sum_ready = sem("c_sum_ready")
        stored = [sem(f"c_stored{i}") for i in range(RING)]
        block = ctx.enter_context(nc.Block())

        def pipeline(eng, step):
            for r in range(RING):
                step(r, r)
            with eng.Fori(RING, NT - RING + 1, RING) as i:
                for r in range(RING):
                    step(i + r, r)

        @block.sync
        def _(sp):
            def step(t, r):
                after(sp, y_done, t - RING + 1)
                sp.dma_start(ct[:, r], s["combT_dram"][bass.ds(t, 1)].rearrange("t p n -> p (t n)")
                             ).then_inc(ct_in[r], 16)
            pipeline(sp, step)

        @block.scalar
        def _(act):
            def step(t, r):
                act.wait_ge(sum_ready, t + 1)
                act.dma_start(s["out_dram"][:, bass.ds(t, 1), :], x_res[:, bass.ds(t, 1), :]).then_inc(stored[r], 16)
            pipeline(act, step)
            for r in range(RING):
                act.wait_ge(stored[r], 16 * NT // RING)

        @block.tensor
        def _(pe):
            def step(t, r):
                pe.wait_ge(ct_in[r], 4 * (t - r) + 16)
                after(pe, sum_ready, t - 1)
                for n in range(ST):
                    m = pe.matmul(ps[:, r % 2, 0:C], ct[:, r, n * P:(n + 1) * P], yt[:, n],
                                  start=(n == 0), stop=(n == ST - 1))
                m.then_inc(y_done, 1)
            pipeline(pe, step)

        @block.vector
        def _(dve):
            def step(t, r):
                dve.wait_ge(y_done, t + 1)
                dve.tensor_tensor(x_res[:, t, :], ps[:, r % 2, 0:C], x_res[:, t, :], ALU.add).then_inc(sum_ready, 1)
            pipeline(dve, step)


def route_and_experts(nc, d, s):
    with ExitStack() as ctx:
        s["combT_dram"] = nc.dram_tensor("combine_turned", [NT, P, ST * P], F32).ap()
        s["ew"] = ctx.enter_context(nc.sbuf_tensor("e_weights", [P, RING, EPT, CC, C], F32))
        s["w_in"] = [ctx.enter_context(nc.semaphore(f"e_w_in{i}")) for i in range(RING)]
        s["expert_w"] = d["expert_w"].rearrange("(s e) (a p) h -> s p e a h", e=EPT, p=P)
        s["xacc"] = ctx.enter_context(nc.sbuf_tensor("xacc", [P, CC, ES], F32))
        with ExitStack() as route_ctx:
            for name, shape, dt in (("phiT_high", [P, CC, ES], F32R), ("phiT_low", [P, CC, ES], F32R),
                                    ("sel_add", [EXPERTS, ES], BF16),
                                    ("sel_swap", [EXPERTS + SLOTS, ES], BF16), ("bias_rows", [96, ES], BF16),
                                    ("ones", [96, P], BF16), ("identb", [P, P], BF16)):
                s[name] = route_ctx.enter_context(nc.sbuf_tensor(f"r_{name}", shape, dt))
            route_setup(nc, d, s)
            route(nc, d, s)
        s["xt"] = ctx.enter_context(nc.sbuf_tensor("e_xt", [P, ST, C], F32))
        s["yt"] = ctx.enter_context(nc.sbuf_tensor("e_yt", [P, ST, C], F32))
        experts(nc, d, s)
        combine(nc, d, s)



def decoder(nc, d, out):
    with ExitStack() as ctx:
        def sb(name, shape, dt=F32):
            return ctx.enter_context(nc.sbuf_tensor(name, shape, dt))

        s = {
            "ident": sb("ident", [P, P]),
            "eps": sb("eps", [P, 1]),
            "w": sb("w", [P, CC]),
            "u": sb("u", [P, CC]),
            "cap": sb("cap", [P, CC]),
            "attn_wT": sb("attn_wT", [P, 3, CC, C]),
            "x_res": sb("x_res", [P, NT, C]),
            "ps": ctx.enter_context(nc.psum_tensor("ps", [P, 8, BLK], F32)),
            "x_dram": d["x"].rearrange("b (i p) c -> p (b i) c", p=P),
            "out_dram": out.rearrange("b (i p) c -> p (b i) c", p=P),
        }
        setup(nc, d, s)
        mixing(nc, d, s)
        with ExitStack() as attend_ctx:
            for name, shape in (("wo", [P, CC, C]), ("bq", [GR, 3]), ("bo", [P, C]), ("headmask", [GR, GH]),
                                ("vblk", [P, B, PAIRS, VW]), ("nm", [P, BT, GK])):
                s[name] = attend_ctx.enter_context(nc.sbuf_tensor(f"x_{name}", shape, F32))
            for name, shape in (("wq", [P, CC, C]), ("kT", [GR, 3, B * KV]), ("kblk", [GK, 2, 3, GN]),
                                ("qT", [GK, 2, 3, T])):
                for part in ("high", "low"):
                    s[f"{name}_{part}"] = attend_ctx.enter_context(
                        nc.sbuf_tensor(f"x_{name}_{part}", shape, F32R))
            attend_setup(nc, d, s)
            attend(nc, d, s)
        route_and_experts(nc, d, s)


_INS = {"x": "x", "ctx": "ctx_512", "attn_Wk": "L0_attn_Wk", "attn_Wr": "L0_attn_Wr", "attn_Wo": "L0_attn_Wo",
        "attn_decay": "L0_attn_time_decay", "attn_first": "L0_attn_time_first",
        "Wq": "L0_xattn_Wq", "bq": "L0_xattn_bq", "Wk": "L0_xattn_Wk", "bk": "L0_xattn_bk",
        "Wv": "L0_xattn_Wv", "bv": "L0_xattn_bv", "Wo": "L0_xattn_Wo", "bo": "L0_xattn_bo",
        "phi_w": "L0_ffn_phi_w", "phi_b": "L0_ffn_phi_b", "expert_w": "L0_ffn_expert_w",
        "expert_b": "L0_ffn_expert_b"}


def kernel(**inputs):
    import numpy as np
    import concourse.bacc as bacc
    from concourse.bass_utils import run_bass_kernel_spmd

    nc = bacc.Bacc("TRN2", target_bir_lowering=False, num_devices=1)
    arrays, dram = {}, {}
    for short, name in _INS.items():
        a = np.ascontiguousarray(inputs[name])
        arrays[f"in_{short}"] = a
        dram[short] = nc.dram_tensor(f"in_{short}", a.shape, F32, kind="ExternalInput").ap()
    out = nc.dram_tensor("out_x", (B, T, C), F32, kind="ExternalOutput").ap()
    decoder(nc, dram, out)
    return run_bass_kernel_spmd(nc, [arrays], core_ids=[0]).results[0]["out_x"]
```

```python
from contextlib import ExitStack

import concourse.bass as bass
from concourse import mybir

F32 = mybir.dt.float32
F32R = mybir.dt.float32r
BF16 = mybir.dt.bfloat16
ALU = mybir.AluOpType
ACT = mybir.ActivationFunctionType
AX = mybir.AxisListType

P = 128
B, T, C = 8, 512, 256
CC = C // P
BT = T // P
NT = B * BT
KV, CD = 64, 128
HEADS = 16
DK = C // HEADS
EPS = 1e-5
NEG_INF = -1e38
LIMIT = 40.0

GH = 6
GROUPS = [6, 6, 4]
GR = GH * DK
GK = GR + HEADS
GN = GH * KV
PAIRS = HEADS // 2
VW = 2 * (DK + 1)

EXPERTS, SLOTS = 64, 32
ES = EXPERTS * SLOTS
ST = ES // P
EPT = P // SLOTS
BLK = 512
EB = ES // BLK


def after(eng, sem, count):
    if isinstance(count, int) and count <= 0:
        return
    eng.wait_ge(sem, count)


def setup(nc, d, s):
    with ExitStack() as ctx:
        def sem(name):
            return ctx.enter_context(nc.semaphore(name))

        raw = ctx.enter_context(nc.sbuf_tensor("raw_weights", [P, 3, CC, C], F32))
        decay = ctx.enter_context(nc.sbuf_tensor("decay", [P, CC], F32))
        decay_e = ctx.enter_context(nc.sbuf_tensor("decay_e", [P, CC], F32))
        weights_in = sem("weights_in")
        vectors_in = sem("vectors_in")
        ident_done = sem("ident_done")
        turned = sem("weights_turned")
        copied = sem("weights_copied")
        decay_exp = sem("decay_exp")
        consts = sem("consts")
        block = ctx.enter_context(nc.Block())

        @block.sync
        def _(sp):
            for n, w in enumerate((d["attn_Wk"], d["attn_Wr"], d["attn_Wo"])):
                sp.dma_start(raw[:, n], w.rearrange("(a p) c -> p a c", p=P)).then_inc(weights_in, 16)
            load_x(sp, s, 0, 0)
            load_x(sp, s, 1, 1)
            sp.wait_ge(weights_in, 48)
            sp.wait_ge(vectors_in, 16 * 2)

        @block.gpsimd
        def _(pool):
            pool.memset(s["ident"][:], 0.0).then_inc(ident_done, 1)
            pool.wait_ge(ident_done, 1)
            pool.affine_select(out=s["ident"][:], in_=s["ident"][:], compare_op=ALU.not_equal, fill=1.0,
                               base=0, pattern=[[-1, P]], channel_multiplier=1).then_inc(ident_done, 1)

        @block.scalar
        def _(act):
            with nc.allow_non_contiguous_dma(reason="one value per channel, once"):
                act.dma_start(decay[:], d["attn_decay"].rearrange("(a p) -> p a", p=P)).then_inc(vectors_in, 16)
                act.dma_start(s["u"][:], d["attn_first"].rearrange("(a p) -> p a", p=P)).then_inc(vectors_in, 16)
            act.wait_ge(vectors_in, 32)
            act.activation(decay_e[:], decay[:], ACT.Exp).then_inc(decay_exp, 1)

        @block.tensor
        def _(pe):
            pe.wait_ge(ident_done, 2)
            pe.wait_ge(weights_in, 48)
            for n in range(3):
                for cc in range(CC):
                    if n * CC + cc >= 2:
                        pe.wait_ge(copied, n * CC + cc - 1)
                    for hc in range(CC):
                        m = pe.transpose(s["ps"][:, (n * CC + cc) % 2, hc * P:(hc + 1) * P],
                                         raw[:, n, hc, cc * P:(cc + 1) * P], s["ident"][:])
                    m.then_inc(turned, 1)

        @block.vector
        def _(dve):
            dve.memset(s["eps"][:], EPS).then_inc(consts, 1)
            for n in range(3 * CC):
                dve.wait_ge(turned, n + 1)
                dve.tensor_copy(s["attn_wT"][:, n // CC, n % CC, :], s["ps"][:, n % 2, 0:C]).then_inc(copied, 1)
            dve.wait_ge(decay_exp, 1)
            dve.tensor_scalar(s["w"][:], decay_e[:], -1.0, None, ALU.mult).then_inc(consts, 1)
            dve.tensor_scalar(s["cap"][:], s["u"][:], -1.0, LIMIT, ALU.mult, ALU.add).then_inc(consts, 1)
            dve.wait_ge(consts, 3)


def load_x(eng, s, b, par):
    eng.dma_start(s["x_res"][:, bass.ds(b * BT, BT), :],
                  s["x_dram"][:, bass.ds(b * BT, BT), :]).then_inc(s["x_in"][par], 16)


def mixing(nc, d, s):
    ps, x_res, ident = s["ps"], s["x_res"], s["ident"]
    x_in = s["x_in"]
    wkT, wrT, woT = (s["attn_wT"][:, n] for n in range(3))
    with ExitStack() as ctx:
        def sb(name, shape):
            return ctx.enter_context(nc.sbuf_tensor(name, shape, F32))

        def sem(name):
            return ctx.enter_context(nc.semaphore(name))

        stats = sb("m_stats", [P, 2, BT, 6])
        mv = sb("m_mv", [P, 2, BT, 2])
        lnv = sb("m_lnv", [P, 2, BT])
        rstd = sb("m_rstd", [P, 2, BT])
        xn = sb("m_xn", [P, 2, BT, C])
        xnT = sb("m_xnT", [P, CC, T])
        kr = sb("m_kr", [P, 2, 2, CC, T])
        top = sb("m_top", [P, CC, T + 1])
        num = sb("m_num", [P, CC, T + 1])
        den = sb("m_den", [P, CC, T + 1])
        gap = sb("m_gap", [P, CC, T])
        up = sb("m_up", [P, 2, CC, T])
        down = sb("m_down", [P, 2, CC, T])
        ev = sb("m_ev", [P, 2, CC, T])
        now = sb("m_now", [P, 2, CC, T])
        er = sb("m_er", [P, CC, T])
        bot = sb("m_bot", [P, CC, T])
        val = sb("m_val", [P, CC, T])
        lsig = sb("m_lsig", [P, 2, CC, T])
        oT = sb("m_oT", [P, 2, CC, T])

        stats_ready = sem("m_stats_ready")
        mv_ready = sem("m_mv_ready")
        waited = sem("m_waited")
        lnv_ready = sem("m_lnv_ready")
        rstd_ready = sem("m_rstd_ready")
        xn_ready = sem("m_xn_ready")
        xn_turned = sem("m_xn_turned")
        xnT_ready = sem("m_xnT_ready")
        kr_done = sem("m_kr_done")
        kr_ready = sem("m_kr_ready")
        first = sem("m_first_columns")
        top_ready = sem("m_top_ready")
        gap_ready = sem("m_gap_ready")
        up_ready = sem("m_up_ready")
        down_ready = sem("m_down_ready")
        now_capped = sem("m_now_capped")
        now_ready = sem("m_now_ready")
        up_exp = sem("m_up_exp")
        down_exp = sem("m_down_exp")
        er_ready = sem("m_er_ready")
        er_capped = sem("m_er_capped")
        ev_ready = sem("m_ev_ready")
        num_ready = sem("m_num_ready")
        den_ready = sem("m_den_ready")
        bot_ready = sem("m_bot_ready")
        val_ready = sem("m_val_ready")
        vsum_ready = sem("m_vsum_ready")
        lbot_ready = sem("m_lbot_ready")
        lsig_ready = sem("m_lsig_ready")
        lsum_ready = sem("m_lsum_ready")
        rec_ready = sem("m_rec_ready")
        oT_ready = sem("m_oT_ready")
        out_done = sem("m_out_done")
        res_done = sem("m_res_done")
        block = ctx.enter_context(nc.Block())

        def loaded(b, par):
            return 8 * b + 16 - 8 * par

        def pipeline(eng, step):
            for b in range(-2, 2):
                step(b, b % 2)
            with eng.Fori(2, B - 3, 2) as i:
                step(i, 0)
                step(i + 1, 1)
            for b in range(B - 2, B + 1):
                step(b, b % 2)

        def known(b, value):
            return isinstance(b, int) and b == value

        def has(b):
            return not isinstance(b, int) or 0 <= b < B

        operands = attend_operands(nc, d, s, ctx)

        @block.sync
        def _(sp):
            def load(b, par):
                after(sp, stats_ready, b - 1)
                load_x(sp, s, b, par)
            operands["load"](sp)
            with sp.Fori(2, B - 1, 2) as i:
                load(i, 0)
                load(i + 1, 1)

        @block.vector
        def _(dve):
            for buf, v in ((top, NEG_INF), (num, 0.0), (den, 0.0)):
                ins = dve.memset(buf[:, :, 0:1], v)
            ins.then_inc(first, 1)

            def norm(b, par):
                dve.wait_ge(x_in[par], loaded(b, par))
                for i in range(BT):
                    ins = dve.bn_stats(stats[:, par, i], x_res[:, b * BT + i, :])
                ins.then_inc(stats_ready, 1)
                dve.wait_ge(stats_ready, b + 1)
                after(dve, rstd_ready, b - 1)
                dve.sem_inc(waited, 1)
                for i in range(BT):
                    ins = dve.bn_aggr(mv[:, par, i], stats[:, par, i])
                ins.then_inc(mv_ready, 1)

            def normed(b, par):
                dve.wait_ge(rstd_ready, b + 1)
                after(dve, xn_turned, b - 1)
                for i in range(BT):
                    ins = dve.tensor_scalar(xn[:, par, i], x_res[:, b * BT + i, :], mv[:, par, i, 0:1],
                                            rstd[:, par, i:i + 1], ALU.subtract, ALU.mult)
                ins.then_inc(xn_ready, 1)

            def running_max(b, par):
                n = 2 * b
                dve.wait_ge(kr_ready, b + 1)
                for h in range(CC):
                    after(dve, gap_ready, n - 1 + h)
                    dve.tensor_tensor_scan(top[:, h, 1:T + 1], s["w"][:, h:h + 1].to_broadcast([P, T]),
                                           kr[:, par, 0, h], NEG_INF, ALU.add, ALU.max).then_inc(top_ready, 1)
                for h in range(CC):
                    after(dve, lsig_ready, n + h - 1)
                    dve.tensor_scalar(er[:, h], kr[:, par, 1, h], -LIMIT, None, ALU.max).then_inc(er_capped, 1)

            def exponents(b, par):
                n = 2 * b
                for h in range(CC):
                    dve.wait_ge(gap_ready, n + h + 1)
                    after(dve, num_ready, n + h - 3)
                    after(dve, val_ready, n + h - 3)
                    dve.tensor_scalar(down[:, par, h], gap[:, h], s["w"][:, h:h + 1], 0.0,
                                      ALU.subtract, ALU.min).then_inc(down_ready, 1)
                    dve.tensor_scalar(up[:, par, h], gap[:, h], s["w"][:, h:h + 1], 0.0,
                                      ALU.subtract, ALU.max).then_inc(up_ready, 1)
                    dve.tensor_scalar(now[:, par, h], gap[:, h], s["cap"][:, h:h + 1], None,
                                      ALU.min).then_inc(now_capped, 1)

            def sums(b, par):
                n = 2 * b
                for h in range(CC):
                    dve.wait_ge(up_exp, n + h + 1)
                    dve.wait_ge(first, 1)
                    after(dve, bot_ready, n + h - 1)
                    dve.tensor_tensor_scan(den[:, h, 1:T + 1], up[:, par, h], down[:, par, h], 0.0,
                                           ALU.mult, ALU.add).then_inc(den_ready, 1)
                    dve.wait_ge(ev_ready, n + h + 1)
                    after(dve, vsum_ready, n + h - 1)
                    dve.tensor_tensor_scan(num[:, h, 1:T + 1], up[:, par, h], ev[:, par, h], 0.0,
                                           ALU.mult, ALU.add).then_inc(num_ready, 1)
                    dve.wait_ge(den_ready, n + h + 1)
                    dve.wait_ge(now_ready, n + h + 1)
                    after(dve, oT_ready, n + h - 1)
                    dve.tensor_tensor(bot[:, h], now[:, par, h], den[:, h, 0:T], ALU.add).then_inc(bot_ready, 1)
                for h in range(CC):
                    dve.wait_ge(val_ready, n + h + 1)
                    dve.wait_ge(num_ready, n + h + 1)
                    dve.tensor_tensor(val[:, h], val[:, h], num[:, h, 0:T], ALU.add).then_inc(vsum_ready, 1)

            def residual(b):
                for j in range(2):
                    dve.wait_ge(out_done, 2 * b + j + 1)
                    rows = x_res[:, bass.ds(b * BT + 2 * j, 2), :]
                    dve.tensor_tensor(rows, ps[:, 6 + j, :].rearrange("p (a c) -> p a c", a=2), rows,
                                      ALU.add).then_inc(res_done, 1)

            def step(b, par):
                if has(b + 2):
                    norm(b + 2, par)
                if has(b + 2):
                    normed(b + 2, par)
                if has(b + 1):
                    running_max(b + 1, 1 - par)
                if known(b, B):
                    operands["lows"](dve)
                if has(b - 1):
                    residual(b - 1)
                if has(b):
                    sums(b, par)
                if has(b + 1):
                    exponents(b + 1, 1 - par)
                if known(b, B - 2):
                    operands["context_copies"](dve)
                if known(b, B - 1):
                    operands["keys_and_values"](dve)
            pipeline(dve, step)

        @block.gpsimd
        def _(pool):
            def gaps(b, par):
                n = 2 * b
                for h in range(CC):
                    pool.wait_ge(top_ready, n + h + 1)
                    after(pool, now_capped, n + h - 1)
                    pool.tensor_tensor(gap[:, h], kr[:, par, 0, h], top[:, h, 0:T],
                                       ALU.subtract).then_inc(gap_ready, 1)

            def values(b, par):
                n = 2 * b
                for h in range(CC):
                    pool.wait_ge(down_exp, n + h + 1)
                    after(pool, num_ready, n + h - 3)
                    pool.tensor_tensor(ev[:, par, h], down[:, par, h], kr[:, par, 1, h],
                                       ALU.mult).then_inc(ev_ready, 1)

            def value_now(b, par):
                n = 2 * b
                for h in range(CC):
                    pool.wait_ge(now_ready, n + h + 1)
                    after(pool, oT_ready, n + h - 1)
                    pool.tensor_tensor(val[:, h], now[:, par, h], kr[:, par, 1, h], ALU.mult).then_inc(val_ready, 1)

            def quotient(b, par):
                n = 2 * b
                for h in range(CC):
                    pool.wait_ge(lbot_ready, n + h + 1)
                    pool.wait_ge(lsig_ready, n + h + 1)
                    pool.tensor_tensor(bot[:, h], bot[:, h], lsig[:, par, h], ALU.add).then_inc(lsum_ready, 1)
                for h in range(CC):
                    pool.wait_ge(rec_ready, n + h + 1)
                    pool.wait_ge(vsum_ready, n + h + 1)
                    after(pool, out_done, 2 * b - 2)
                    pool.tensor_tensor(oT[:, par, h], val[:, h], bot[:, h], ALU.mult).then_inc(oT_ready, 1)

            def step(b, par):
                if has(b):
                    value_now(b, par)
                if has(b + 1):
                    gaps(b + 1, 1 - par)
                if has(b):
                    quotient(b, par)
                if has(b + 1):
                    values(b + 1, 1 - par)
            operands["zeros"](pool)
            pipeline(pool, step)
            operands["wait_shapes"](pool)

        @block.scalar
        def _(act):
            def root(b, par):
                act.wait_ge(mv_ready, b + 1)
                after(act, xn_ready, b - 1)
                act.activation(lnv[:, par], mv[:, par, :, 1], ACT.Ln, bias=s["eps"][:, 0:1]).then_inc(lnv_ready, 1)
                act.wait_ge(lnv_ready, b + 1)
                act.activation(rstd[:, par], lnv[:, par], ACT.Exp, scale=-0.5).then_inc(rstd_ready, 1)

            def evacuate_xnT(b):
                act.wait_ge(xn_turned, b + 1)
                after(act, kr_done, b)
                act.copy(xnT[:], ps[:, 0:CC, :]).then_inc(xnT_ready, 1)

            def evacuate_kr(b, par):
                act.wait_ge(kr_done, b + 1)
                after(act, val_ready, 2 * b - 2)
                act.copy(kr[:, par].rearrange("p a h t -> p (a h) t"), ps[:, 2:6, :]).then_inc(kr_ready, 1)

            def sigmoid_log(b, par):
                n = 2 * b
                for h in range(CC):
                    act.wait_ge(er_capped, n + h + 1)
                    act.activation(er[:, h], er[:, h], ACT.Exp, scale=-1.0).then_inc(er_ready, 1)
                for h in range(CC):
                    act.wait_ge(er_ready, n + h + 1)
                    after(act, lsum_ready, n + h - 3)
                    act.activation(lsig[:, par, h], er[:, h], ACT.Ln, bias=1.0).then_inc(lsig_ready, 1)

            def exponentials(b, par):
                n = 2 * b
                for h in range(CC):
                    act.wait_ge(down_ready, n + h + 1)
                    act.activation(down[:, par, h], down[:, par, h], ACT.Exp).then_inc(down_exp, 1)
                    act.wait_ge(up_ready, n + h + 1)
                    act.activation(up[:, par, h], up[:, par, h], ACT.Exp, scale=-1.0).then_inc(up_exp, 1)
                    act.wait_ge(now_capped, n + h + 1)
                    act.activation(now[:, par, h], now[:, par, h], ACT.Exp,
                                   bias=s["u"][:, h:h + 1]).then_inc(now_ready, 1)

            def bottom_log(b):
                for h in range(CC):
                    act.wait_ge(bot_ready, 2 * b + h + 1)
                    act.activation(bot[:, h], bot[:, h], ACT.Ln).then_inc(lbot_ready, 1)

            def reciprocal(b):
                for h in range(CC):
                    act.wait_ge(lsum_ready, 2 * b + h + 1)
                    act.activation(bot[:, h], bot[:, h], ACT.Exp, scale=-1.0).then_inc(rec_ready, 1)

            def step(b, par):
                if has(b + 2):
                    root(b + 2, par)
                if has(b + 1):
                    evacuate_kr(b + 1, 1 - par)
                if has(b + 2):
                    evacuate_xnT(b + 2)
                if has(b + 1):
                    sigmoid_log(b + 1, 1 - par)
                if has(b):
                    bottom_log(b)
                if has(b):
                    reciprocal(b)
                if has(b + 1):
                    exponentials(b + 1, 1 - par)
            act.preload_act_table_set("natural_log_exp_and_others")
            pipeline(act, step)
            operands["highs"](act)

        @block.tensor
        def _(pe):
            def turn(b, par):
                pe.wait_ge(xn_ready, b + 1)
                after(pe, xnT_ready, b)
                for cc in range(CC):
                    for i in range(BT):
                        m = pe.transpose(ps[:, cc, i * P:(i + 1) * P], xn[:, par, i, cc * P:(cc + 1) * P],
                                         ident[:])
                m.then_inc(xn_turned, 1)

            def project(b):
                pe.wait_ge(xnT_ready, b + 1)
                after(pe, kr_ready, b)
                for a, w in ((0, wkT), (1, wrT)):
                    for h in range(CC):
                        for cc in range(CC):
                            m = pe.matmul(ps[:, 2 + 2 * a + h, :], w[:, cc, h * P:(h + 1) * P], xnT[:, cc],
                                          start=(cc == 0), stop=(cc == CC - 1))
                m.then_inc(kr_done, 1)

            def out(b, par):
                pe.wait_ge(oT_ready, 2 * b + 2)
                for i in range(BT):
                    if i % 2 == 0:
                        after(pe, res_done, 2 * b - 1 + i // 2)
                    for h in range(CC):
                        m = pe.matmul(ps[:, 6 + i // 2, (i % 2) * C:(i % 2 + 1) * C],
                                      oT[:, par, h, i * P:(i + 1) * P], woT[:, h, :],
                                      start=(h == 0), stop=(h == CC - 1))
                    if i % 2:
                        m.then_inc(out_done, 1)

            def step(b, par):
                if has(b + 2):
                    turn(b + 2, par)
                    project(b + 2)
                if known(b, B - 2):
                    operands["turn_context"](pe)
                if has(b):
                    out(b, par)
                if known(b, B - 2):
                    pe.wait_ge(kr_ready, B)
                    operands["products"](pe)
            pipeline(pe, step)


def attend_operands(nc, d, s, ctx):
    ps, ident = s["ps"], s["ident"]

    def sem(name):
        return ctx.enter_context(nc.semaphore(name))

    space = s["xacc"][:].rearrange("p a n -> p (a n)")
    ctx_in = space[:, 0:512].rearrange("p (a c) -> p a c", c=CD)
    ctxT = space[:, 512:1536].rearrange("p (b e k) -> p b e k", e=2, k=KV)
    wk, wv, bv = (space[:, 1536 + C * n:1536 + C * (n + 1)] for n in range(3))
    kT = space[0:GR, 2304:3840].rearrange("p (g n) -> p g n", g=3)
    bk = space[0:GR, 3840:3843]
    wq = ctx.enter_context(nc.sbuf_tensor("x_wq", [P, CC, C], F32))[:]
    wo = ctx.enter_context(nc.sbuf_tensor("x_wo", [P, CC, C], F32))[:]
    loads = sem("x_loads")
    zeroed = sem("x_zeroed")
    ctx_turned = sem("x_ctx_turned")
    ctxT_ready = sem("x_ctxT_ready")
    k_done = sem("x_k_done")
    v_done = sem("x_v_done")
    kT_ready = sem("x_kT_ready")
    v_ready = sem("x_v_ready")
    high_ready = sem("x_high_ready")
    n_loads = 11
    v_banks = (4, 5, 0, 1)

    def load(sp):
        sp.dma_start(ctx_in, d["ctx"].rearrange("(a e) k c -> (e k) a c", e=2)).then_inc(loads, 16)
        sp.dma_start(wk, d["Wk"]).then_inc(loads, 16)
        sp.dma_start(wv, d["Wv"]).then_inc(loads, 16)
        sp.dma_start(wq, d["Wq"].rearrange("(a p) n -> p a n", p=P)).then_inc(loads, 16)
        sp.dma_start(wo, d["Wo"].rearrange("(a p) n -> p a n", p=P)).then_inc(loads, 16)
        for row, dst in (("bv", bv), ("bo", s["bo"][:])):
            sp.dma_start(dst, d[row].partition_broadcast(P)).then_inc(loads, 16)
        with nc.allow_non_contiguous_dma(reason="one value per channel, once"):
            for row, dst in (("bq", s["bq"]), ("bk", bk)):
                sp.dma_start(dst[:, 0:2], d[row][0:2 * GR].rearrange("(g p) -> p g", p=GR)).then_inc(loads, 16)
                sp.dma_start(dst[0:C - 2 * GR, 2:3],
                             d[row][2 * GR:C].rearrange("(g p) -> p g", g=1)).then_inc(loads, 16)

    def zeros(pool):
        pool.memset(s["headmask"][:], 1.0)
        pool.memset(s["nm"][:], 0.0)
        pool.memset(kT, 0.0)
        pool.memset(s["vblk"][:], 0.0).then_inc(zeroed, 1)
        pool.wait_ge(zeroed, 1)
        pool.memset(s["vblk"][0:KV, :, :, DK:DK + 1], 1.0)
        pool.memset(s["vblk"][KV:P, :, :, VW - 1:VW], 1.0).then_inc(zeroed, 1)
        pool.wait_ge(zeroed, 2)
        pool.affine_select(out=s["headmask"][:], in_=s["headmask"][:], compare_op=ALU.is_ge, fill=0.0,
                           base=0, pattern=[[-DK, GH]], channel_multiplier=1).then_inc(zeroed, 1)
        pool.wait_ge(zeroed, 3)
        pool.affine_select(out=s["headmask"][:], in_=s["headmask"][:], compare_op=ALU.is_ge, fill=0.0,
                           base=DK - 1, pattern=[[DK, GH]], channel_multiplier=-1).then_inc(zeroed, 1)

    def turn_context(pe):
        pe.wait_ge(loads, 16 * n_loads)
        for a in range(B * KV // P):
            m = pe.transpose(ps[:, 0, a * P:(a + 1) * P], ctx_in[:, a, :], ident[:])
        m.then_inc(ctx_turned, 1)

    def products(pe):
        pe.wait_ge(ctxT_ready, 2)
        for g in range(3):
            rows = GROUPS[g] * DK
            pe.matmul(ps[0:rows, 1 + g, :], wk[:, g * GR:g * GR + rows], ctxT[:, :, 0, :],
                      start=True, stop=True).then_inc(k_done, 1)
        for b in range(B):
            if b == 6:
                pe.wait_ge(kT_ready, 1)
            m = pe.matmul(ps[:, v_banks[b // 2], (b % 2) * C:(b % 2 + 1) * C],
                          ctxT[:, b].rearrange("p a k -> p (a k)"), wv, start=True, stop=True)
            if b % 2:
                m.then_inc(v_done, 1)

    def context_copies(dve):
        dve.wait_ge(ctx_turned, 1)
        for a in range(2):
            dve.tensor_copy(ctxT[:, :, a, :], ps[:, 0, :].rearrange("p (b k) -> p b k", b=B)).then_inc(ctxT_ready, 1)

    def keys_and_values(dve):
        dve.wait_ge(loads, 16 * n_loads)
        dve.wait_ge(zeroed, 1)
        for g in range(3):
            rows = GROUPS[g] * DK
            dve.wait_ge(k_done, g + 1)
            dve.tensor_scalar(kT[0:rows, g], ps[0:rows, 1 + g, :], bk[0:rows, g:g + 1], DK ** -0.5,
                              ALU.add, ALU.mult).then_inc(kT_ready, 1)
        dve.wait_ge(zeroed, 2)
        for b in range(B):
            if b % 2 == 0:
                dve.wait_ge(v_done, b // 2 + 1)
            for e in range(2):
                rows = slice(e * KV, (e + 1) * KV)
                made = ps[rows, v_banks[b // 2], (b % 2) * C:(b % 2 + 1) * C]
                dve.tensor_tensor(s["vblk"][rows, b, :, e * (DK + 1):e * (DK + 1) + DK],
                                  made.rearrange("p (j e d) -> p j e d", e=2, d=DK)[:, :, e, :],
                                  bv[rows].rearrange("p (j e d) -> p j e d", e=2, d=DK)[:, :, e, :],
                                  ALU.add).then_inc(v_ready, 1)

    def highs(act):
        act.wait_ge(loads, 16 * n_loads)
        act.copy(s["wq_high"][:], wq)
        act.copy(s["wo_high"][:], wo).then_inc(high_ready, 1)
        act.wait_ge(kT_ready, 3)
        act.copy(s["kT_high"][:], kT).then_inc(high_ready, 1)

    def lows(dve):
        dve.wait_ge(high_ready, 2)
        dve.wait_ge(kT_ready, 3)
        dve.tensor_tensor(s["wq_low"][:], wq, s["wq_high"][:].bitcast(F32), ALU.subtract)
        dve.tensor_tensor(s["wo_low"][:], wo, s["wo_high"][:].bitcast(F32), ALU.subtract)
        dve.tensor_tensor(s["kT_low"][:], kT, s["kT_high"][:].bitcast(F32), ALU.subtract)

    def wait_shapes(pool):
        pool.wait_ge(zeroed, 4)

    return dict(load=load, zeros=zeros, turn_context=turn_context, products=products,
                context_copies=context_copies, keys_and_values=keys_and_values, highs=highs, lows=lows,
                wait_shapes=wait_shapes)


BACK = ["S0", "S1", "S2", "S3", "S4", "S5", "S6", "S7", "O0", "O1", "A0", "O2", "A1", "R0",
        "O3", "A2", "R1", "A3", "R2", "R3"]
MAX_AT = {1: "max0", 3: "max1", 5: "max2", 7: "max3", 8: "turn_max"}
FRONT_AT = {0: "norm", 2: "normed", 7: "turn", 11: "query0", 13: "query1", 17: "query2"}


def attend(nc, d, s):
    ps, x_res, ident = s["ps"], s["x_res"], s["ident"]
    qT_high, qT_low, kblk_high, kblk_low = s["qT_high"], s["qT_low"], s["kblk_high"], s["kblk_low"]
    vblk, nm = s["vblk"], s["nm"]
    RING = 5
    with ExitStack() as ctx:
        def sb(name, shape):
            return ctx.enter_context(nc.sbuf_tensor(name, shape, F32))

        def sem(name):
            return ctx.enter_context(nc.semaphore(name))

        stats = sb("a_stats", [P, BT, 6])
        mv = sb("a_mv", [P, BT, 2])
        lnv = sb("a_lnv", [P, BT])
        rstd = sb("a_rstd", [P, BT])
        shift = sb("a_shift", [P, BT])
        xn = sb("a_xn", [P, BT, C])
        xnT_high = ctx.enter_context(nc.sbuf_tensor("a_xnT_high", [P, CC, T], F32R))
        xnT_low = ctx.enter_context(nc.sbuf_tensor("a_xnT_low", [P, CC, T], F32R))
        ex = sb("a_ex", [P, 2, PAIRS, T])
        rsum = sb("a_rsum", [P, 2, HEADS])
        at = sb("a_at", [P, 2, C])
        aT_high = ctx.enter_context(nc.sbuf_tensor("a_aT_high", [P, 2, CC, P], F32R))
        aT_low = ctx.enter_context(nc.sbuf_tensor("a_aT_low", [P, 2, CC, P], F32R))
        rows_of = sb("a_rows_of_heads", [GK, 3, GH, KV])
        bias = sb("phi_bias", [P, ES // P])
        rest = sb("phi_rest", [P, 2, ES // P])
        parts = ctx.enter_context(nc.sbuf_tensor("phi_parts", [P, 3, ES // P], BF16))
        split = nc.dram_tensor("phi_b_split", [3, ES], BF16).ap()

        stats_ready = sem("a_stats_ready")
        mv_ready = sem("a_mv_ready")
        waited = sem("a_waited")
        rstd_ready = sem("a_rstd_ready")
        shift_ready = sem("a_shift_ready")
        xn_ready = sem("a_xn_ready")
        xn_turned = sem("a_xn_turned")
        xnT_high_ready = sem("a_xnT_high_ready")
        xnT_ready = sem("a_xnT_ready")
        bias_added = sem("a_bias_added")
        q_done = sem("a_q_done")
        q_high_ready = sem("a_q_high_ready")
        q_ready = sem("a_q_ready")
        kblk_high_ready = sem("a_kblk_high_ready")
        kblk_low_ready = sem("a_kblk_low_ready")
        s1_done = sem("a_s1_done")
        max_ready = sem("a_max_ready")
        max_turned = sem("a_max_turned")
        maxT_ready = sem("a_maxT_ready")
        s2_done = sem("a_s2_done")
        exp_ready = sem("a_exp_ready")
        o_done = sem("a_o_done")
        rsum_ready = sem("a_rsum_ready")
        at_ready = sem("a_at_ready")
        at_turned = sem("a_at_turned")
        aT_high_ready = sem("a_aT_high_ready")
        aT_ready = sem("a_aT_ready")
        proj_done = sem("a_proj_done")
        res_done = sem("a_res_done")
        zeroed = sem("a_zeroed")
        shaped = sem("a_shaped")
        cleared = sem("a_cleared")
        rows_ready = sem("a_rows_ready")
        phi_in = sem("phi_in")
        bias_in = sem("phi_bias_in")
        parts_ready = sem("phi_parts_ready")
        rest_ready = sem("phi_rest_ready")
        rows_moved = sem("phi_rows_moved")
        filled = sem("r_filled")
        block = ctx.enter_context(nc.Block())

        def pipeline(eng, step):
            for b in range(-2, 2):
                step(b, b % 2)
            with eng.Fori(2, B - 3, 2) as i:
                step(i, 0)
                step(i + 1, 1)
            step(B - 2, 0)
            step(B - 1, 1)

        def known(b, value):
            return isinstance(b, int) and b == value

        def has(b):
            return not isinstance(b, int) or 0 <= b < B

        @block.sync
        def _(sp):
            sp.dma_start(s["phi"], d["phi_w"].rearrange("(a p) c -> p a c", p=P)).then_inc(phi_in, 16)
            sp.dma_start(bias[:], d["phi_b"].rearrange("(p a) -> p a", p=P)).then_inc(bias_in, 16)
            sp.wait_ge(parts_ready, 3)
            with nc.allow_non_contiguous_dma(reason="12 KB, once"):
                sp.dma_start(split.rearrange("j (p a) -> p j a", p=P), parts[:]).then_inc(rows_moved, 16)
            sp.wait_ge(rows_moved, 16)
            sp.wait_ge(filled, 1)
            for j in range(3):
                sp.dma_start(s["bias_rows"][32 * j:32 * j + 1, :], split[j:j + 1, :]).then_inc(rows_moved, 16)
            sp.wait_ge(rows_moved, 64)
            sp.wait_ge(phi_in, 16)

        @block.vector
        def _(dve):
            def bias_parts():
                dve.wait_ge(bias_in, 16)
                dve.tensor_copy(parts[:, 0], bias[:]).then_inc(parts_ready, 1)
                dve.wait_ge(parts_ready, 1)
                dve.tensor_tensor(rest[:, 0], bias[:], parts[:, 0], ALU.subtract).then_inc(rest_ready, 1)
                dve.wait_ge(rest_ready, 1)
                dve.tensor_copy(parts[:, 1], rest[:, 0]).then_inc(parts_ready, 1)
                dve.wait_ge(parts_ready, 2)
                dve.tensor_tensor(rest[:, 1], rest[:, 0], parts[:, 1], ALU.subtract).then_inc(rest_ready, 1)
                dve.wait_ge(rest_ready, 2)
                dve.tensor_copy(parts[:, 2], rest[:, 1]).then_inc(parts_ready, 1)

            def clear():
                for name in ("qT_high", "qT_low"):
                    for par in range(2):
                        ins = dve.memset(s[name][GROUPS[2] * DK:GR, par, 2].bitcast(F32), 0.0)
                ins.then_inc(cleared, 1)
                dve.memset(qT_low[GR:GK].bitcast(F32), 0.0)
                dve.memset(kblk_low[GR:GK].bitcast(F32), 0.0).then_inc(rows_ready, 1)

            def head_rows():
                dve.wait_ge(shaped, 1)
                for par in range(2):
                    dve.tensor_copy(kblk_high[GR:GK, par],
                                    rows_of[GR:GK].rearrange("p g h k -> p g (h k)")).then_inc(rows_ready, 1)

            def norm(b):
                after(dve, xn_ready, b)
                for i in range(BT):
                    ins = dve.bn_stats(stats[:, i], x_res[:, b * BT + i, :])
                ins.then_inc(stats_ready, 1)
                dve.wait_ge(stats_ready, b + 1)
                dve.sem_inc(waited, 1)
                for i in range(BT):
                    ins = dve.bn_aggr(mv[:, i], stats[:, i])
                ins.then_inc(mv_ready, 1)

            def shift_of(b):
                dve.wait_ge(rstd_ready, 2 * b + 2)
                dve.scalar_tensor_tensor(out=shift[:], in0=mv[:, :, 0], scalar=-1.0, in1=rstd[:], op0=ALU.mult,
                                         op1=ALU.mult).then_inc(shift_ready, 1)

            def xnT_rest(b):
                dve.wait_ge(xnT_high_ready, b + 1)
                after(dve, q_done, 3 * b)
                dve.tensor_tensor(xnT_low[:], ps[:, 0:CC, :], xnT_high[:].bitcast(F32),
                                  ALU.subtract).then_inc(xnT_ready, 1)

            def query_rest(b, par, g):
                dve.wait_ge(q_high_ready, 3 * b + g + 1)
                if g == 0:
                    after(dve, s2_done, PAIRS * (b - 1))
                rows = GROUPS[g] * DK
                dve.scalar_tensor_tensor(out=qT_low[0:rows, par, g], in0=ps[0:rows, 2 + g, :],
                                         scalar=s["bq"][0:rows, g:g + 1],
                                         in1=qT_high[0:rows, par, g].bitcast(F32),
                                         op0=ALU.add, op1=ALU.subtract).then_inc(q_ready, 1)

            def maxima(b, i):
                dve.wait_ge(s1_done, BT * b + i + 1)
                if i == 0:
                    after(dve, max_turned, b)
                dve.tensor_reduce(nm[:, i, GR:GR + 2 * GH],
                                  ps[:, 2:4, 0:GN].rearrange("p a (h k) -> p a h k", k=KV), AX.X, ALU.max,
                                  negate=True)
                dve.tensor_reduce(nm[:, i, GR + 2 * GH:GK],
                                  ps[:, 4, 0:GROUPS[2] * KV].rearrange("p (h k) -> p h k", k=KV), AX.X, ALU.max,
                                  negate=True).then_inc(max_ready, 1)

            def weigh(b, i, k):
                n = BT * b + i
                O = ps[:, RING + k % 3, 0:PAIRS * VW].rearrange("p (h w) -> p h w", w=DK + 1)
                dve.wait_ge(o_done, n + 1)
                dve.reciprocal(rsum[:, i % 2, :], O[:, :, DK]).then_inc(rsum_ready, 1)
                dve.wait_ge(rsum_ready, n + 1)
                after(dve, at_turned, n - 1)
                dve.tensor_tensor(at[:, i % 2].rearrange("p (h w) -> p h w", w=DK), O[:, :, 0:DK],
                                  rsum[:, i % 2, :].unsqueeze(2).to_broadcast([P, HEADS, DK]),
                                  ALU.mult).then_inc(at_ready, 1)

            def aT_rest(b, i, k):
                n = BT * b + i
                dve.wait_ge(aT_high_ready, n + 1)
                dve.tensor_tensor(aT_low[:, i % 2].rearrange("p a t -> p (a t)"), ps[:, RING + k % 3, 0:C],
                                  aT_high[:, i % 2].rearrange("p a t -> p (a t)").bitcast(F32),
                                  ALU.subtract).then_inc(aT_ready, 1)

            def add(b, i, k):
                dve.wait_ge(proj_done, BT * b + i + 1)
                if i == 0:
                    dve.wait_ge(bias_added, b + 1)
                row = x_res[:, b * BT + i, :]
                dve.tensor_tensor(row, ps[:, RING + k % 3, 0:C], row, ALU.add).then_inc(res_done, 1)

            def step(b, par):
                for k, name in enumerate(BACK):
                    front, middle = FRONT_AT.get(k, ""), MAX_AT.get(k, "")
                    if has(b) and name[0] == "O":
                        weigh(b, int(name[1]), k)
                    if has(b) and name[0] == "A":
                        aT_rest(b, int(name[1]), k)
                    if has(b) and name[0] == "R":
                        add(b, int(name[1]), k)
                    if has(b + 1) and middle.startswith("max"):
                        maxima(b + 1, int(middle[3]))
                    if has(b + 2):
                        if front == "norm":
                            norm(b + 2)
                        if front == "normed":
                            shift_of(b + 2)
                        if front == "turn":
                            xnT_rest(b + 2)
                        if front.startswith("query"):
                            query_rest(b + 2, par, int(front[5]))
                    if known(b, -2) and front == "turn":
                        clear()
                    if known(b, -1) and name == BACK[-1]:
                        head_rows()
                        bias_parts()
            pipeline(dve, step)

        @block.gpsimd
        def _(pool):
            def keys(b, par, part, ready):
                for g in range(3):
                    ins = pool.tensor_tensor(
                        s["kblk_" + part][0:GR, par, g].rearrange("p (h k) -> p h k", k=KV),
                        s["kT_" + part][:, g, bass.ds(b * KV, KV)].bitcast(F32).unsqueeze(1)
                        .to_broadcast([GR, GH, KV]),
                        s["headmask"][:].unsqueeze(2).to_broadcast([GR, GH, KV]), ALU.mult)
                ins.then_inc(ready, 1)

            def front(b, par):
                after(pool, s2_done, PAIRS * (b - 1))
                keys(b, par, "high", kblk_high_ready)
                keys(b, par, "low", kblk_low_ready)
                pool.wait_ge(xn_ready, b + 1)
                for i in range(BT):
                    row = x_res[:, b * BT + i, :]
                    ins = pool.tensor_tensor(row, row, s["bo"][:], ALU.add)
                ins.then_inc(bias_added, 1)

            front(0, 0)
            pool.memset(rows_of[:], 0.0).then_inc(zeroed, 1)
            pool.wait_ge(zeroed, 1)
            pool.affine_select(out=rows_of[:], in_=rows_of[:], compare_op=ALU.not_equal,
                               fill=1.0, base=GR, pattern=[[GH, 3], [1, GH], [0, KV]],
                               channel_multiplier=-1).then_inc(shaped, 1)
            front(1, 1)
            pool.memset(s["bias_rows"][:], 0.0)
            pool.memset(s["ones"][:], 1.0).then_inc(filled, 1)
            with pool.Fori(2, B - 1, 2) as i:
                front(i, 0)
                front(i + 1, 1)
            pool.memset(s["sel_add"][:], 0.0)
            pool.memset(s["sel_swap"][:], 0.0).then_inc(zeroed, 1)
            pool.wait_ge(zeroed, 2)
            by_expert = dict(compare_op=ALU.not_equal, base=0, pattern=[[1, EXPERTS], [0, SLOTS]],
                             channel_multiplier=-1)
            pool.affine_select(out=s["sel_add"][:], in_=s["sel_add"][:], fill=1.0, **by_expert).then_inc(shaped, 1)
            pool.affine_select(out=s["sel_swap"][:], in_=s["sel_swap"][:], fill=-1.0, **by_expert).then_inc(shaped, 1)
            pool.wait_ge(shaped, 3)
            pool.affine_select(out=s["sel_swap"][:], in_=s["sel_swap"][:], fill=1.0, compare_op=ALU.not_equal,
                               base=EXPERTS, pattern=[[0, EXPERTS], [1, SLOTS]],
                               channel_multiplier=-1).then_inc(shaped, 1)
            pool.wait_ge(shaped, 4)

        @block.scalar
        def _(act):
            def root(b):
                act.wait_ge(mv_ready, b + 1)
                act.activation(lnv[:], mv[:, :, 1], ACT.Ln, bias=s["eps"][:, 0:1]).then_inc(rstd_ready, 1)
                act.wait_ge(rstd_ready, 2 * b + 1)
                act.activation(rstd[:], lnv[:], ACT.Exp, scale=-0.5).then_inc(rstd_ready, 1)

            def normed(b):
                act.wait_ge(shift_ready, b + 1)
                after(act, xn_turned, b)
                for i in range(BT):
                    ins = act.activation(xn[:, i], x_res[:, b * BT + i, :], ACT.Identity, bias=shift[:, i:i + 1],
                                         scale=rstd[:, i:i + 1])
                ins.then_inc(xn_ready, 1)

            def turned(b):
                act.wait_ge(xn_turned, b + 1)
                after(act, q_done, 3 * b)
                act.copy(xnT_high[:], ps[:, 0:CC, :]).then_inc(xnT_high_ready, 1)

            def query(b, par, g):
                act.wait_ge(q_done, 3 * b + g + 1)
                if g == 0:
                    after(act, s2_done, PAIRS * (b - 1))
                rows = GROUPS[g] * DK
                act.activation(qT_high[0:rows, par, g], ps[0:rows, 2 + g, :], ACT.Identity,
                               bias=s["bq"][0:rows, g:g + 1]).then_inc(q_high_ready, 1)

            def max_rows(b, par):
                act.wait_ge(max_turned, b + 1)
                act.copy(qT_high[GR:GK, par], ps[GR:GK, 2:3, :].to_broadcast([HEADS, 3, T])).then_inc(maxT_ready, 1)

            def exps(b, par, j, k):
                act.wait_ge(s2_done, PAIRS * b + j + 1)
                if j == 0:
                    after(act, o_done, BT * (b - 1))
                act.activation(ex[:, par, j], ps[:, RING + k % 3, :], ACT.Exp).then_inc(exp_ready, 1)

            def turn_out(b, i, k):
                n = BT * b + i
                act.wait_ge(at_turned, n + 1)
                after(act, proj_done, n - 1)
                act.copy(aT_high[:, i % 2].rearrange("p a t -> p (a t)"),
                         ps[:, RING + k % 3, 0:C]).then_inc(aT_high_ready, 1)

            def step(b, par):
                for k, name in enumerate(BACK):
                    front = FRONT_AT.get(k, "")
                    if has(b) and name[0] == "S":
                        exps(b, par, int(name[1]), k)
                    if has(b) and name[0] == "A":
                        turn_out(b, int(name[1]), k)
                    if has(b + 1) and MAX_AT.get(k) == "turn_max":
                        max_rows(b + 1, 1 - par)
                    if has(b + 2):
                        if front == "norm":
                            root(b + 2)
                        if front == "normed":
                            normed(b + 2)
                        if front == "turn":
                            turned(b + 2)
                        if front.startswith("query"):
                            query(b + 2, par, int(front[5]))
            pipeline(act, step)

        @block.tensor
        def _(pe):
            def turn(b, par):
                pe.wait_ge(xn_ready, b + 1)
                after(pe, xnT_ready, b)
                for cc in range(CC):
                    for i in range(BT):
                        m = pe.transpose(ps[:, cc, i * P:(i + 1) * P], xn[:, i, cc * P:(cc + 1) * P], ident[:])
                m.then_inc(xn_turned, 1)

            def query(b, par, g):
                if g == 0:
                    pe.wait_ge(xnT_ready, b + 1)
                    after(pe, max_ready, BT * b)
                    after(pe, maxT_ready, b)
                rows = GROUPS[g] * DK
                for cc in range(CC):
                    for w, x in (("wq_high", xnT_high), ("wq_high", xnT_low), ("wq_low", xnT_high)):
                        m = pe.matmul(ps[0:rows, 2 + g, :], s[w][:, cc, g * GR:g * GR + rows], x[:, cc],
                                      start=(cc == 0 and x is xnT_high and w == "wq_high"),
                                      stop=(cc == CC - 1 and w == "wq_low"))
                m.then_inc(q_done, 1)

            def score(b, par, i):
                if i == 0:
                    pe.wait_ge(q_ready, 3 * (b + 1))
                    pe.wait_ge(kblk_high_ready, b + 1)
                    if known(b, 0):
                        pe.wait_ge(cleared, 1)
                else:
                    pe.wait_ge(max_ready, BT * b + i)
                for g in range(3):
                    cols = GROUPS[g] * KV
                    m = pe.matmul(ps[:, 2 + g, 0:cols], qT_high[0:GR, par, g, i * P:(i + 1) * P],
                                  kblk_high[0:GR, par, g, 0:cols], start=True, stop=True)
                m.then_inc(s1_done, 1)

            def turn_max(b, par):
                pe.wait_ge(max_ready, BT * (b + 1))
                for i in range(BT):
                    m = pe.transpose(ps[0:GK, 2, i * P:(i + 1) * P], nm[:, i, :], ident[:])
                m.then_inc(max_turned, 1)

            def free(b, k):
                prev, at = (k - 3, b) if k >= 3 else ((18 if k == 0 else 19 if k == 1 else 17), b - 1)
                kind, i = BACK[prev][0], int(BACK[prev][1])
                read, per = {"S": (exp_ready, PAIRS), "O": (at_ready, BT), "A": (aT_ready, BT),
                             "R": (res_done, BT)}[kind]
                after(pe, read, per * at + i + 1)

            def back(b, par, k):
                kind, i = BACK[k][0], int(BACK[k][1])
                bank = RING + k % 3
                free(b, k)
                if kind == "S":
                    if i == 0:
                        pe.wait_ge(maxT_ready, b + 1)
                        pe.wait_ge(kblk_low_ready, b + 1)
                        if known(b, 0):
                            pe.wait_ge(rows_ready, 3)
                    g, o = divmod(i, GH // 2)
                    for k_part, q_part in ((kblk_high, qT_high), (kblk_high, qT_low), (kblk_low, qT_high)):
                        m = pe.matmul(ps[:, bank, :], k_part[:, par, g, o * P:(o + 1) * P], q_part[:, par, g, :],
                                      start=(q_part is qT_high and k_part is kblk_high),
                                      stop=(k_part is kblk_low))
                    m.then_inc(s2_done, 1)
                if kind == "O":
                    if i == 0:
                        pe.wait_ge(exp_ready, PAIRS * (b + 1))
                    for j in range(PAIRS):
                        m = pe.matmul(ps[:, bank, j * VW:(j + 1) * VW], ex[:, par, j, i * P:(i + 1) * P],
                                      vblk[:, b, j, :], start=True, stop=True)
                    m.then_inc(o_done, 1)
                if kind == "A":
                    pe.wait_ge(at_ready, BT * b + i + 1)
                    for cc in range(CC):
                        m = pe.transpose(ps[:, bank, cc * P:(cc + 1) * P], at[:, i % 2, cc * P:(cc + 1) * P],
                                         ident[:])
                    m.then_inc(at_turned, 1)
                if kind == "R":
                    pe.wait_ge(aT_ready, BT * b + i + 1)
                    for cc in range(CC):
                        for x, w in ((aT_high, "wo_high"), (aT_high, "wo_low"), (aT_low, "wo_high")):
                            m = pe.matmul(ps[:, bank, 0:C], x[:, i % 2, cc, :], s[w][:, cc, :],
                                          start=(cc == 0 and x is aT_high and w == "wo_high"),
                                          stop=(cc == CC - 1 and x is aT_low))
                    m.then_inc(proj_done, 1)

            def step(b, par):
                for k in range(len(BACK)):
                    front, middle = FRONT_AT.get(k, ""), MAX_AT.get(k, "")
                    if has(b):
                        back(b, par, k)
                    if has(b + 1) and middle == "turn_max":
                        turn_max(b + 1, 1 - par)
                    elif has(b + 1) and middle:
                        score(b + 1, 1 - par, int(middle[3]))
                    if has(b + 2) and front == "turn":
                        turn(b + 2, par)
                    if has(b + 2) and front.startswith("query"):
                        query(b + 2, par, int(front[5]))
            pipeline(pe, step)


def route_setup(nc, d, s):
    ps, ident, phi = s["ps"], s["ident"], s["phi"]
    with ExitStack() as ctx:
        def sem(name):
            return ctx.enter_context(nc.semaphore(name))

        turned = sem("phi_turned")
        high_ready = sem("phi_high_ready")
        block = ctx.enter_context(nc.Block())

        def part(name, n):
            return s[name][:, n // EB, (n % EB) * BLK:(n % EB + 1) * BLK]

        @block.scalar
        def _(act):
            act.copy(s["identb"][:], ident[:])
            for n in range(CC * EB):
                act.wait_ge(turned, n + 1)
                act.copy(part("phiT_high", n), ps[:, n, :]).then_inc(high_ready, 1)

        @block.vector
        def _(dve):
            for n in range(CC * EB):
                dve.wait_ge(high_ready, n + 1)
                dve.tensor_tensor(part("phiT_low", n), ps[:, n, :], part("phiT_high", n).bitcast(F32),
                                  ALU.subtract)

        @block.tensor
        def _(pe):
            for n in range(CC * EB):
                for i in range(BLK // P):
                    m = pe.transpose(ps[:, n, i * P:(i + 1) * P],
                                     phi[:, (n % EB) * (BLK // P) + i, (n // EB) * P:(n // EB + 1) * P], ident[:])
                m.then_inc(turned, 1)


def route(nc, d, s):
    ps, x_res, ident = s["ps"], s["x_res"], s["ident"]
    xacc = s["xacc"]
    SMALL, TURN, DISP = 4, 5, 6
    NM = EXPERTS + SLOTS
    UNITS = CC * EB
    with ExitStack() as ctx:
        def sb(name, shape, dt=F32):
            return ctx.enter_context(nc.sbuf_tensor(name, shape, dt))

        def sem(name):
            return ctx.enter_context(nc.semaphore(name))

        stats = sb("r_stats", [P, 6])
        mv = sb("r_mv", [P, 2])
        lnv = sb("r_lnv", [P, 1])
        rstd = sb("r_rstd", [P, 1])
        xn = sb("r_xn", [P, 2, C])
        xh_high = sb("r_xh_high", [P, 4, C], F32R)
        xh_low = sb("r_xh_low", [P, 4, C], F32R)
        disp_high = sb("r_disp_high", [P, 4, ES], F32R)
        disp_low = sb("r_disp_low", [P, 4, ES], F32R)
        xhT_high = sb("r_xhT_high", [P, 2, CC, P], F32R)
        xhT_low = sb("r_xhT_low", [P, 2, CC, P], F32R)
        nab = sb("r_nab", [P, 2, NM], BF16)
        half_b = sb("r_half_b", [P, 2, SLOTS])
        nabT = sb("r_nabT", [NM, P], BF16)
        disp = sb("r_disp", [P, ES])
        comb = sb("r_comb", [P, 2, ES])
        combT = sb("r_combT", [P, EB, BLK])
        sum_d = sb("r_sum_d", [P, EXPERTS])
        sum_c = sb("r_sum_c", [P, SLOTS])
        rec_d = sb("r_rec_d", [P, 2, EXPERTS])
        rec_c = sb("r_rec_c", [P, 2, SLOTS])
        turned_max = ps[0:NM, SMALL, 0:P // 2].bitcast(BF16)

        stats_ready = sem("r_stats_ready")
        waited = sem("r_waited")
        mv_ready = sem("r_mv_ready")
        lnv_ready = sem("r_lnv_ready")
        rstd_ready = sem("r_rstd_ready")
        xn_ready = sem("r_xn_ready")
        xh_high_ready = sem("r_xh_high_ready")
        xh_ready = sem("r_xh_ready")
        xn_turned = sem("r_xn_turned")
        xhT_high_ready = sem("r_xhT_high_ready")
        xhT_ready = sem("r_xhT_ready")
        logits_done = sem("r_logits_done")
        half_ready = sem("r_half_ready")
        max_ready = sem("r_max_ready")
        max_turned = sem("r_max_turned")
        maxT_ready = sem("r_maxT_ready")
        less_a = sem("r_less_expert_max")
        less_b = sem("r_less_slot_max")
        exp_d = sem("r_exp_d")
        exp_c = sem("r_exp_c")
        sum_d_ready = sem("r_sum_d_ready")
        sum_c_ready = sem("r_sum_c_ready")
        rec_d_ready = sem("r_rec_d_ready")
        rec_c_ready = sem("r_rec_c_ready")
        disp_ready = sem("r_disp_ready")
        disp_high_ready = sem("r_disp_high_ready")
        disp_low_ready = sem("r_disp_low_ready")
        comb_ready = sem("r_comb_ready")
        comb_turned = sem("r_comb_turned")
        combT_ready = sem("r_combT_ready")
        combT_out = [sem(f"r_combT_out{i}") for i in range(EB)]
        unit_done = sem("r_unit_done")
        unit_added = sem("r_unit_added")
        block = ctx.enter_context(nc.Block())

        def pipeline(eng, step):
            for t in range(4):
                step(t, t)
            with eng.Fori(4, NT - 7, 4) as i:
                for r in range(4):
                    step(i + r, r)
            for t in range(NT - 4, NT + 2):
                step(t, t % 4)

        def known(t):
            return isinstance(t, int)

        def has_tile(t):
            return not known(t) or 0 <= t < NT

        def quarters(t):
            return [(tile, n) for tile, n in ((t - 2, 2), (t - 2, 3), (t - 1, 0), (t - 1, 1)) if has_tile(tile)]

        def pair_units(t, r):
            return 4 * (t - r) + UNITS

        @block.sync
        def _(sp):
            def step(t, r):
                for tile, n in quarters(t):
                    sp.wait_ge(combT_ready, EB * tile + n + 1)
                    sp.dma_start(s["combT_dram"][bass.ds(tile, 1), :, n * BLK:(n + 1) * BLK]
                                 .rearrange("t p n -> p (t n)"), combT[:, n]).then_inc(combT_out[n], 16)
            pipeline(sp, step)
            for n in range(EB):
                sp.wait_ge(combT_out[n], 16 * NT)

        @block.vector
        def _(dve):
            def norm(t, r):
                dve.bn_stats(stats[:], x_res[:, bass.ds(t, 1), :].rearrange("p a c -> p (a c)")
                             if not known(t) else x_res[:, t, :]).then_inc(stats_ready, 1)
                dve.wait_ge(stats_ready, t + 1)
                dve.sem_inc(waited, 1)
                dve.bn_aggr(mv[:], stats[:]).then_inc(mv_ready, 1)

            def normed(t, r):
                dve.wait_ge(rstd_ready, t + 1)
                after(dve, xn_turned, t - 1)
                after(dve, xh_ready, t - 1)
                dve.tensor_scalar(xn[:, r % 2], x_res[:, t, :], mv[:, 0:1], rstd[:, 0:1],
                                  ALU.subtract, ALU.mult).then_inc(xn_ready, 1)

            def maxima(t, r):
                after(dve, max_turned, t - 1)
                for h in range(2):
                    for b in (2 * h, 2 * h + 1):
                        dve.wait_ge(logits_done, EB * t + b + 1)
                        dve.tensor_reduce(nab[:, r % 2, b * EXPERTS // EB:(b + 1) * EXPERTS // EB],
                                          ps[:, b, :].rearrange("p (n q) -> p n q", q=SLOTS), AX.X, ALU.max,
                                          negate=True)
                    dve.tensor_reduce(half_b[:, h], ps[:, 2 * h:2 * h + 2, :].rearrange("p b (n q) -> p q (b n)", q=SLOTS), AX.X,
                                      ALU.max, negate=True).then_inc(half_ready, 1)
                dve.wait_ge(half_ready, 2 * t + 2)
                dve.tensor_tensor(nab[:, r % 2, EXPERTS:NM], half_b[:, 0], half_b[:, 1],
                                  ALU.min).then_inc(max_ready, 1)

            def xhT_rest(t, r):
                dve.wait_ge(xhT_high_ready, t + 1)
                after(dve, logits_done, EB * (t - 1))
                dve.tensor_tensor(xhT_low[:, r % 2].rearrange("p a t -> p (a t)"), ps[:, SMALL, 0:C],
                                  xhT_high[:, r % 2].rearrange("p a t -> p (a t)").bitcast(F32),
                                  ALU.subtract).then_inc(xhT_ready, 1)

            def sums_d(t, r):
                for h in range(2):
                    half = slice(h * EXPERTS // 2, (h + 1) * EXPERTS // 2)
                    dve.wait_ge(exp_d, 2 * t + h + 1)
                    dve.tensor_reduce(sum_d[:, half], disp[:].rearrange("p (n q) -> p n q", q=SLOTS)[:, half],
                                      AX.X, ALU.add).then_inc(sum_d_ready, 1)
                    dve.wait_ge(sum_d_ready, 2 * t + h + 1)
                    after(dve, disp_ready, 2 * (t - 1))
                    dve.reciprocal(rec_d[:, r % 2, half], sum_d[:, half]).then_inc(rec_d_ready, 1)

            def sums_c(t, r):
                dve.wait_ge(exp_c, 2 * t + 2)
                dve.tensor_reduce(sum_c[:], comb[:, r % 2].rearrange("p (n q) -> p q n", q=SLOTS), AX.X,
                                  ALU.add).then_inc(sum_c_ready, 1)
                dve.wait_ge(sum_c_ready, t + 1)
                after(dve, comb_ready, t - 1)
                dve.reciprocal(rec_c[:, r % 2], sum_c[:]).then_inc(rec_c_ready, 1)

            def unit(t, r, n):
                u = (r % 2) * 4 + n
                done = pair_units(t - 2, r % 2) - UNITS + u + 1
                dve.wait_ge(unit_done, done)
                part = xacc[:, u // EB, (u % EB) * BLK:(u % EB + 1) * BLK]
                if known(t) and t < 4:
                    dve.tensor_copy(part, ps[:, DISP + u % 2, :]).then_inc(unit_added, 1)
                else:
                    dve.tensor_tensor(part, ps[:, DISP + u % 2, :], part, ALU.add).then_inc(unit_added, 1)

            def step(t, r):
                units = not known(t) or t >= 2
                if known(t) and t == 0:
                    norm(0, 0)
                    normed(0, 0)
                    xhT_rest(0, 0)
                if has_tile(t + 1):
                    norm(t + 1, (r + 1) % 4)
                if has_tile(t):
                    maxima(t, r)
                if units:
                    unit(t, r, 0)
                if has_tile(t + 1):
                    normed(t + 1, (r + 1) % 4)
                if units:
                    unit(t, r, 1)
                if has_tile(t):
                    sums_d(t, r)
                if units:
                    unit(t, r, 2)
                if has_tile(t + 1):
                    xhT_rest(t + 1, (r + 1) % 4)
                if has_tile(t):
                    sums_c(t, r)
                if units:
                    unit(t, r, 3)
            pipeline(dve, step)

        @block.gpsimd
        def _(pool):
            def cols(h):
                return slice(h * ES // 2, (h + 1) * ES // 2)

            def low_x(t, r):
                pool.wait_ge(xh_high_ready, t + 1)
                pool.tensor_tensor(xh_low[:, r], xn[:, r % 2], xh_high[:, r].bitcast(F32),
                                   ALU.subtract).then_inc(xh_ready, 1)

            def dispatch_weights(t, r):
                for h in range(2):
                    n = EXPERTS // 2
                    pool.wait_ge(rec_d_ready, 2 * t + h + 1)
                    half = disp[:, cols(h)].rearrange("p (n q) -> p n q", q=SLOTS)
                    pool.tensor_tensor(half, half, rec_d[:, r % 2, h * n:(h + 1) * n].unsqueeze(2)
                                       .to_broadcast([P, n, SLOTS]), ALU.mult).then_inc(disp_ready, 1)
                for h in range(2):
                    pool.wait_ge(disp_high_ready, 2 * t + h + 1)
                    pool.tensor_tensor(disp_low[:, r, cols(h)], disp[:, cols(h)],
                                       disp_high[:, r, cols(h)].bitcast(F32),
                                       ALU.subtract).then_inc(disp_low_ready, 1)

            def combine_weights(t, r):
                pool.wait_ge(rec_c_ready, t + 1)
                pool.tensor_tensor(comb[:, r % 2].rearrange("p (n q) -> p n q", q=SLOTS),
                                   comb[:, r % 2].rearrange("p (n q) -> p n q", q=SLOTS),
                                   rec_c[:, r % 2].unsqueeze(1).to_broadcast([P, EXPERTS, SLOTS]),
                                   ALU.mult).then_inc(comb_ready, 1)

            def step(t, r):
                if known(t) and t == 0:
                    low_x(0, 0)
                if has_tile(t):
                    dispatch_weights(t, r)
                    combine_weights(t, r)
                if has_tile(t + 1):
                    low_x(t + 1, (r + 1) % 4)
            pipeline(pool, step)

        @block.scalar
        def _(act):
            def root(t):
                act.wait_ge(mv_ready, t + 1)
                act.activation(lnv[:], mv[:, 1:2], ACT.Ln, bias=s["eps"][:, 0:1]).then_inc(lnv_ready, 1)
                act.wait_ge(lnv_ready, t + 1)
                act.activation(rstd[:], lnv[:], ACT.Exp, scale=-0.5).then_inc(rstd_ready, 1)

            def xhT_copy(t, r):
                act.wait_ge(xn_turned, t + 1)
                after(act, logits_done, EB * (t - 1))
                act.copy(xhT_high[:, r % 2].rearrange("p a t -> p (a t)"),
                         ps[:, SMALL, 0:C]).then_inc(xhT_high_ready, 1)

            def combT_copy(t, n):
                act.wait_ge(comb_turned, EB * t + n + 1)
                after(act, combT_out[n], 16 * t)
                act.copy(combT[:, n], ps[:, TURN, :]).then_inc(combT_ready, 1)

            def high_x(t, r):
                act.wait_ge(xn_ready, t + 1)
                after(act, unit_done, pair_units(t - 4, r % 2))
                act.copy(xh_high[:, r], xn[:, r % 2]).then_inc(xh_high_ready, 1)

            def high_disp(t, r, h):
                act.wait_ge(disp_ready, 2 * t + h + 1)
                if h == 0:
                    after(act, unit_done, pair_units(t - 4, r % 2))
                cols = slice(h * ES // 2, (h + 1) * ES // 2)
                act.copy(disp_high[:, r, cols], disp[:, cols]).then_inc(disp_high_ready, 1)

            def exps(t, h, into, less, done):
                act.wait_ge(less, 2 * t + h + 1)
                act.activation(into[:, h * 2 * BLK:(h + 1) * 2 * BLK],
                               ps[:, 2 * h:2 * h + 2, :].rearrange("p b n -> p (b n)"),
                               ACT.Exp).then_inc(done, 1)

            def exps_d(t, h):
                after(act, disp_low_ready, 2 * t + h - 1)
                exps(t, h, disp, less_a, exp_d)

            def step(t, r):
                def quarter(n):
                    tile = t - 2 if n >= 2 else t - 1
                    if has_tile(tile):
                        combT_copy(tile, n)
                if known(t) and t == 0:
                    root(0)
                    xhT_copy(0, 0)
                    high_x(0, 0)
                if has_tile(t + 1):
                    root(t + 1)
                if has_tile(t):
                    act.wait_ge(max_turned, t + 1)
                    after(act, less_b, 2 * t)
                    act.copy(nabT[:], turned_max).then_inc(maxT_ready, 1)
                quarter(2)
                if has_tile(t):
                    exps_d(t, 0)
                quarter(3)
                if has_tile(t):
                    exps_d(t, 1)
                if has_tile(t + 1):
                    xhT_copy(t + 1, (r + 1) % 4)
                if has_tile(t):
                    after(act, comb_turned, EB * (t - 1))
                    exps(t, 0, comb[:, r % 2], less_b, exp_c)
                quarter(0)
                if has_tile(t):
                    exps(t, 1, comb[:, r % 2], less_b, exp_c)
                if has_tile(t + 1):
                    high_x(t + 1, (r + 1) % 4)
                quarter(1)
                if has_tile(t):
                    high_disp(t, r, 0)
                    high_disp(t, r, 1)
            act.preload_act_table_set("natural_log_exp_and_others")
            pipeline(act, step)

        @block.tensor
        def _(pe):
            def turn_xn(t, r):
                pe.wait_ge(xn_ready, t + 1)
                after(pe, maxT_ready, t)
                for cc in range(CC):
                    m = pe.transpose(ps[:, SMALL, cc * P:(cc + 1) * P], xn[:, r % 2, cc * P:(cc + 1) * P],
                                     ident[:])
                m.then_inc(xn_turned, 1)

            def logits(t, r):
                pe.wait_ge(xhT_ready, t + 1)
                for b in range(EB):
                    if b % 2 == 0:
                        after(pe, exp_c, 2 * t - 1 + b // 2)
                    cols = slice(b * BLK, (b + 1) * BLK)
                    pe.matmul(ps[:, b, :], s["ones"][:], s["bias_rows"][:, cols], start=True, stop=False)
                    for cc in range(CC):
                        for x, w in ((xhT_high, "phiT_high"), (xhT_high, "phiT_low"), (xhT_low, "phiT_high")):
                            m = pe.matmul(ps[:, b, :], x[:, r % 2, cc], s[w][:, cc, cols], start=False,
                                          stop=(cc == CC - 1 and x is xhT_low))
                    m.then_inc(logits_done, 1)

            def turn_max(t, r):
                pe.wait_ge(max_ready, t + 1)
                pe.wait_ge(xhT_ready, t + 1)
                pe.transpose(turned_max, nab[:, r % 2, :], s["identb"][:]).then_inc(max_turned, 1)

            def shift(t, r, rows, selector, done, blocks=range(EB), before=None):
                for b in blocks:
                    if before is not None and b % 2 == 0:
                        pe.wait_ge(before, 2 * t + b // 2 + 1)
                    m = pe.matmul(ps[:, b, :], nabT[0:rows], selector[0:rows, b * BLK:(b + 1) * BLK],
                                  start=False, stop=True, skip_group_check=True)
                    if b % 2:
                        m.then_inc(done, 1)

            def unit(t, r, n):
                u = (r % 2) * 4 + n
                q = (r - 2 - r % 2) % 4
                if n == 0 and r % 2 == 0:
                    pe.wait_ge(disp_low_ready, 2 * t)
                    pe.wait_ge(xh_ready, t)
                after(pe, unit_added, pair_units(t - 2, r % 2) - UNITS + u - 1)
                for k in range(2):
                    for x, w in ((xh_high, disp_high), (xh_high, disp_low), (xh_low, disp_high)):
                        m = pe.matmul(ps[:, DISP + u % 2, :], x[:, q + k, (u // EB) * P:(u // EB + 1) * P],
                                      w[:, q + k, (u % EB) * BLK:(u % EB + 1) * BLK],
                                      start=(k == 0 and x is xh_high and w is disp_high),
                                      stop=(k == 1 and x is xh_low))
                m.then_inc(unit_done, 1)

            def turn_comb(t, r, n):
                if n == 0:
                    pe.wait_ge(comb_ready, t + 1)
                after(pe, combT_ready, EB * t + n)
                for i in range(BLK // P):
                    m = pe.transpose(ps[:, TURN, i * P:(i + 1) * P],
                                     comb[:, r % 2, n * BLK + i * P:n * BLK + (i + 1) * P], ident[:])
                m.then_inc(comb_turned, 1)

            def step(t, r):
                def dispatch(n):
                    if not known(t) or t >= 2:
                        unit(t, r, n)

                def turn(n):
                    back = 2 if n >= 2 else 1
                    if has_tile(t - back):
                        turn_comb(t - back, (r - back) % 4, n)
                if known(t) and t == 0:
                    turn_xn(0, 0)
                if has_tile(t):
                    logits(t, r)
                dispatch(0)
                dispatch(1)
                if has_tile(t):
                    turn_max(t, r)
                turn(2)
                if has_tile(t):
                    pe.wait_ge(maxT_ready, t + 1)
                    shift(t, r, EXPERTS, s["sel_add"], less_a)
                turn(3)
                if has_tile(t + 1):
                    turn_xn(t + 1, (r + 1) % 4)
                dispatch(2)
                if has_tile(t):
                    shift(t, r, NM, s["sel_swap"], less_b, range(0, 2), exp_d)
                turn(0)
                if has_tile(t):
                    shift(t, r, NM, s["sel_swap"], less_b, range(2, 4), exp_d)
                dispatch(3)
                turn(1)
            pipeline(pe, step)


RING = 4


def load_experts(eng, s, n):
    eng.dma_start(s["ew"][:, n % RING].rearrange("p e a h -> p (e a) h"),
                  s["expert_w"][n].rearrange("p e a h -> p (e a) h")).then_inc(s["w_in"][n % RING], 16)


def load_combine(eng, s, t, r):
    eng.dma_start(s["ct"][:, r], s["combT_dram"][bass.ds(t, 1)].rearrange("t p n -> p (t n)")
                  ).then_inc(s["ct_in"][r], 16)


def experts(nc, d, s):
    ps, ident, xacc = s["ps"], s["ident"], s["xacc"]
    with ExitStack() as ctx:
        def sb(name, shape):
            return ctx.enter_context(nc.sbuf_tensor(name, shape, F32))

        def sem(name):
            return ctx.enter_context(nc.semaphore(name))

        s["ew"] = ew = sb("e_weights", [P, RING, EPT, CC, C])
        s["w_in"] = w_in = [sem(f"e_w_in{i}") for i in range(RING)]
        xt = sb("e_xt", [P, ST, C])
        stats = sb("e_stats", [P, ST, 6])
        mv = sb("e_mv", [P, ST, 2])
        lnv = sb("e_lnv", [P, ST])
        rstd = sb("e_rstd", [P, ST])
        shift = sb("e_shift", [P, ST])
        eb = sb("e_bias", [P, ST, C])
        y = sb("e_y", [P, 3, C])
        b_in = sem("e_b_in")
        turned = sem("e_turned")
        xt_ready = sem("e_xt_ready")
        mv_ready = sem("e_mv_ready")
        rstd_ready = sem("e_rstd_ready")
        shift_ready = sem("e_shift_ready")
        tanh_ready = sem("e_tanh_ready")
        thT_ready = sem("e_thT_ready")
        y_done = sem("e_y_done")
        y_ready = sem("e_y_ready")
        y_high_ready = sem("e_y_high_ready")
        y_low_ready = sem("e_y_low_ready")
        block = ctx.enter_context(nc.Block())

        @block.sync
        def _(sp):
            for n in range(ST):
                if n >= RING:
                    sp.wait_ge(y_done, n - RING + 1)
                load_experts(sp, s, n)
                if n == 0:
                    for e in range(EPT):
                        sp.dma_start(eb[e * SLOTS:(e + 1) * SLOTS],
                                     d["expert_b"].rearrange("(s e) h -> e s h", e=EPT)[e]
                                     .partition_broadcast(SLOTS)).then_inc(b_in, 16)
            for t in range(RING):
                load_combine(sp, s, t, t)

        @block.tensor
        def _(pe):
            for n in range(ST):
                if n >= 2:
                    pe.wait_ge(xt_ready, n - 1)
                for cc in range(CC):
                    m = pe.transpose(ps[:, n % 2, cc * P:(cc + 1) * P], xacc[:, cc, n * P:(n + 1) * P], ident[:])
                m.then_inc(turned, 1)
            def turn_tanh(n):
                pe.wait_ge(tanh_ready, n + 1)
                if n >= 2:
                    pe.wait_ge(thT_ready, n - 1)
                for cc in range(CC):
                    m = pe.transpose(ps[:, 2 + n % 2, cc * P:(cc + 1) * P], xt[:, n, cc * P:(cc + 1) * P], ident[:])
                m.then_inc(turned, 1)

            turn_tanh(0)
            for n in range(ST):
                if n + 1 < ST:
                    turn_tanh(n + 1)
                pe.wait_ge(w_in[n % RING], 16 * (n // RING + 1))
                pe.wait_ge(thT_ready, n + 1)
                if n >= 2:
                    pe.wait_ge(y_ready, n - 1)
                for e in range(EPT):
                    rows = slice(e * SLOTS, (e + 1) * SLOTS)
                    for cc in range(CC):
                        m = pe.matmul(ps[rows, 4 + n % 2, 0:C], xacc[:, cc, n * P + e * SLOTS:n * P + (e + 1) * SLOTS],
                                      ew[:, n % RING, e, cc, :], start=(cc == 0), stop=(cc == CC - 1),
                                      tile_position=(0, e * SLOTS))
                m.then_inc(y_done, 1)

        @block.vector
        def _(dve):
            def y_low(n):
                dve.wait_ge(y_high_ready, n + 1)
                dve.tensor_tensor(s["y_low"][:, n], y[:, n % 3], s["y_high"][:, n].bitcast(F32),
                                  ALU.subtract).then_inc(y_low_ready, 1)

            def statistics(n):
                dve.wait_ge(xt_ready, n + 1)
                dve.bn_stats(stats[:, n], xt[:, n]).then_inc(mv_ready, 1)

            def thT(n):
                dve.wait_ge(turned, ST + n + 1)
                dve.tensor_copy(xacc[:, :, n * P:(n + 1) * P],
                                ps[:, 2 + n % 2, 0:C].rearrange("p (a t) -> p a t", a=CC)).then_inc(thT_ready, 1)

            for n in range(ST):
                dve.wait_ge(turned, n + 1)
                dve.tensor_scalar(xt[:, n], ps[:, n % 2, 0:C], -33000.0, 65000.0, ALU.max, ALU.min).then_inc(xt_ready, 1)
                if n >= 1:
                    statistics(n - 1)
            statistics(ST - 1)
            for n in range(ST):
                dve.wait_ge(mv_ready, n + 1)
                dve.bn_aggr(mv[:, n], stats[:, n]).then_inc(mv_ready, 1)
            dve.wait_ge(rstd_ready, 2)
            dve.wait_ge(mv_ready, 2 * ST)
            dve.scalar_tensor_tensor(out=shift[:], in0=mv[:, :, 0], scalar=-1.0, in1=rstd[:], op0=ALU.mult,
                                     op1=ALU.mult).then_inc(shift_ready, 1)
            thT(0)
            for n in range(ST):
                if n + 1 < ST:
                    thT(n + 1)
                if n == 0:
                    dve.wait_ge(b_in, 16 * EPT)
                dve.wait_ge(y_done, n + 1)
                if n >= 3:
                    dve.wait_ge(y_low_ready, n - 2)
                dve.tensor_tensor(y[:, n % 3], ps[:, 4 + n % 2, 0:C], eb[:, n], ALU.add).then_inc(y_ready, 1)
                if n >= 1:
                    y_low(n - 1)
            y_low(ST - 1)

        @block.scalar
        def _(act):
            act.wait_ge(mv_ready, 2 * ST)
            act.activation(lnv[:], mv[:, :, 1], ACT.Ln, bias=s["eps"][:, 0:1]).then_inc(rstd_ready, 1)
            act.wait_ge(rstd_ready, 1)
            act.activation(rstd[:], lnv[:], ACT.Exp, scale=-0.5).then_inc(rstd_ready, 1)
            act.wait_ge(shift_ready, 1)
            AHEAD = 3
            for n in range(ST + AHEAD):
                if n < ST:
                    act.activation(xt[:, n], xt[:, n], ACT.Tanh, bias=shift[:, n:n + 1],
                                   scale=rstd[:, n:n + 1]).then_inc(tanh_ready, 1)
                if n >= AHEAD:
                    act.wait_ge(y_ready, n - AHEAD + 1)
                    act.copy(s["y_high"][:, n - AHEAD], y[:, (n - AHEAD) % 3]).then_inc(y_high_ready, 1)


def combine(nc, d, s):
    ps, x_res, ct, ct_in = s["ps"], s["x_res"], s["ct"], s["ct_in"]
    HALF = ST * P // 2
    with ExitStack() as ctx:
        def sem(name):
            return ctx.enter_context(nc.semaphore(name))

        ct_high = ctx.enter_context(nc.sbuf_tensor("c_combT_high", [P, 2, ST * P], F32R))
        ct_low = ctx.enter_context(nc.sbuf_tensor("c_combT_low", [P, 2, ST * P], F32R))
        high_ready = sem("c_high_ready")
        low_ready = sem("c_low_ready")
        y_done = sem("c_y_done")
        sum_ready = sem("c_sum_ready")
        stored = [sem(f"c_stored{i}") for i in range(RING)]
        block = ctx.enter_context(nc.Block())

        def pipeline(eng, step):
            for r in range(RING):
                step(r, r)
            with eng.Fori(RING, NT - RING + 1, RING) as i:
                for r in range(RING):
                    step(i + r, r)

        @block.sync
        def _(sp):
            def step(t, r):
                if not isinstance(t, int) or t >= RING:
                    sp.wait_ge(low_ready, 2 * (t - RING + 1))
                    load_combine(sp, s, t, r)
            pipeline(sp, step)

        @block.gpsimd
        def _(pool):
            def step(t, r):
                pool.wait_ge(sum_ready, t + 1)
                pool.dma_start(s["out_dram"][:, bass.ds(t, 1), :], x_res[:, bass.ds(t, 1), :]).then_inc(stored[r], 16)
            pipeline(pool, step)
            for r in range(RING):
                pool.wait_ge(stored[r], 16 * NT // RING)

        @block.scalar
        def _(act):
            def step(t, r):
                act.wait_ge(ct_in[r], 4 * (t - r) + 16)
                after(act, y_done, t - 1)
                for h in range(2):
                    half = slice(h * HALF, (h + 1) * HALF)
                    act.copy(ct_high[:, r % 2, half], ct[:, r, half]).then_inc(high_ready, 1)
            pipeline(act, step)

        @block.tensor
        def _(pe):
            def step(t, r):
                after(pe, sum_ready, t - 1)
                for n in range(ST):
                    if n % (ST // 2) == 0:
                        pe.wait_ge(low_ready, 2 * t + n // (ST // 2) + 1)
                    cols = slice(n * P, (n + 1) * P)
                    for c, y in ((ct_high, "y_high"), (ct_high, "y_low"), (ct_low, "y_high")):
                        m = pe.matmul(ps[:, r % 2, 0:C], c[:, r % 2, cols], s[y][:, n],
                                      start=(n == 0 and y == "y_high" and c is ct_high),
                                      stop=(n == ST - 1 and c is ct_low))
                m.then_inc(y_done, 1)
            pipeline(pe, step)

        @block.vector
        def _(dve):
            def total(t, r):
                dve.wait_ge(y_done, t + 1)
                dve.tensor_tensor(x_res[:, t, :], ps[:, r % 2, 0:C], x_res[:, t, :], ALU.add).then_inc(sum_ready, 1)

            def step(t, r):
                for h in range(2):
                    half = slice(h * HALF, (h + 1) * HALF)
                    dve.wait_ge(high_ready, 2 * t + h + 1)
                    dve.tensor_tensor(ct_low[:, r % 2, half], ct[:, r, half], ct_high[:, r % 2, half].bitcast(F32),
                                      ALU.subtract).then_inc(low_ready, 1)
                if not isinstance(t, int) or t >= 1:
                    total(t - 1, (r - 1) % RING)
            pipeline(dve, step)
            total(NT - 1, RING - 1)


def route_and_experts(nc, d, s):
    with ExitStack() as ctx:
        s["combT_dram"] = nc.dram_tensor("combine_turned", [NT, P, ST * P], F32).ap()
        s["expert_w"] = d["expert_w"].rearrange("(s e) (a p) h -> s p e a h", e=EPT, p=P)
        with ExitStack() as route_ctx:
            for name, shape, dt in (("phiT_high", [P, CC, ES], F32R), ("phiT_low", [P, CC, ES], F32R),
                                    ("identb", [P, P], BF16)):
                s[name] = route_ctx.enter_context(nc.sbuf_tensor(f"r_{name}", shape, dt))
            route_setup(nc, d, s)
            route(nc, d, s)
        s["ct"] = ctx.enter_context(nc.sbuf_tensor("c_combT", [P, RING, ST * P], F32))
        s["ct_in"] = [ctx.enter_context(nc.semaphore(f"c_in{i}")) for i in range(RING)]
        for name in ("y_high", "y_low"):
            s[name] = ctx.enter_context(nc.sbuf_tensor(f"e_{name}", [P, ST, C], F32R))
        experts(nc, d, s)
        combine(nc, d, s)



def decoder(nc, d, out):
    with ExitStack() as ctx:
        def sb(name, shape, dt=F32):
            return ctx.enter_context(nc.sbuf_tensor(name, shape, dt))

        s = {
            "ident": sb("ident", [P, P]),
            "eps": sb("eps", [P, 1]),
            "w": sb("w", [P, CC]),
            "u": sb("u", [P, CC]),
            "cap": sb("cap", [P, CC]),
            "x_res": sb("x_res", [P, NT, C]),
            "ps": ctx.enter_context(nc.psum_tensor("ps", [P, 8, BLK], F32)),
            "x_dram": d["x"].rearrange("b (i p) c -> p (b i) c", p=P),
            "x_in": [ctx.enter_context(nc.semaphore(f"m_x_in{i}")) for i in range(2)],
            "out_dram": out.rearrange("b (i p) c -> p (b i) c", p=P),
        }
        s["xacc"] = sb("xacc", [P, CC, ES])
        s["phi"] = s["xacc"][:].rearrange("p a n -> p (a n)").rearrange("p (a c) -> p a c", c=C)
        for name, rows, cols in (("sel_add", EXPERTS, ES), ("sel_swap", EXPERTS + SLOTS, ES),
                                 ("bias_rows", 96, ES), ("ones", 96, P)):
            s[name] = sb(f"r_{name}", [rows, cols], BF16)
        with ExitStack() as attend_ctx:
            def attend_sb(name, shape, dt=F32):
                s[name] = attend_ctx.enter_context(nc.sbuf_tensor(f"x_{name}", shape, dt))

            for name, shape in (("bq", [GR, 3]), ("bo", [P, C]), ("headmask", [GR, GH]),
                                ("vblk", [P, B, PAIRS, VW]), ("nm", [P, BT, GK])):
                attend_sb(name, shape)
            for name, shape in (("wq", [P, CC, C]), ("wo", [P, CC, C]), ("kT", [GR, 3, B * KV])):
                attend_sb(name + "_high", shape, F32R)
                attend_sb(name + "_low", shape, F32R)
            attend_sb("attn_wT", [P, 3, CC, C])
            setup(nc, d, s)
            mixing(nc, d, s)
            for name, shape in (("kblk", [GK, 2, 3, GN]), ("qT", [GK, 2, 3, T])):
                attend_sb(name + "_high", shape, F32R)
                attend_sb(name + "_low", shape, F32R)
            attend(nc, d, s)
        route_and_experts(nc, d, s)


_INS = {"x": "x", "ctx": "ctx_512", "attn_Wk": "L0_attn_Wk", "attn_Wr": "L0_attn_Wr", "attn_Wo": "L0_attn_Wo",
        "attn_decay": "L0_attn_time_decay", "attn_first": "L0_attn_time_first",
        "Wq": "L0_xattn_Wq", "bq": "L0_xattn_bq", "Wk": "L0_xattn_Wk", "bk": "L0_xattn_bk",
        "Wv": "L0_xattn_Wv", "bv": "L0_xattn_bv", "Wo": "L0_xattn_Wo", "bo": "L0_xattn_bo",
        "phi_w": "L0_ffn_phi_w", "phi_b": "L0_ffn_phi_b", "expert_w": "L0_ffn_expert_w",
        "expert_b": "L0_ffn_expert_b"}


def kernel(**inputs):
    import numpy as np
    import concourse.bacc as bacc
    from concourse.bass_utils import run_bass_kernel_spmd

    nc = bacc.Bacc("TRN2", target_bir_lowering=False, num_devices=1)
    arrays, dram = {}, {}
    for short, name in _INS.items():
        a = np.ascontiguousarray(inputs[name])
        arrays[f"in_{short}"] = a
        dram[short] = nc.dram_tensor(f"in_{short}", a.shape, F32, kind="ExternalInput").ap()
    out = nc.dram_tensor("out_x", (B, T, C), F32, kind="ExternalOutput").ap()
    decoder(nc, dram, out)
    return run_bass_kernel_spmd(nc, [arrays], core_ids=[0]).results[0]["out_x"]
```
